# Optimizing a Trainium2 kernel written in Bass

```python
import numpy as np
import jax
import jax.numpy as jnp

def _softmax(x, axis=-1):
    return jax.nn.softmax(x, axis=axis)

def _gelu(x):
    return jax.nn.gelu(x, approximate=True)

def _silu(x):
    return jax.nn.silu(x)

def _sigmoid(x):
    return jax.nn.sigmoid(x)

def _layernorm(x, axis=-1, eps=1e-05):
    m = jnp.mean(x, axis=axis, keepdims=True)
    v = jnp.var(x, axis=axis, keepdims=True)
    return (x - m) / jnp.sqrt(v + eps)

def _scatter_add(tgt, idx, src, axis=0):
    return tgt.at[idx].add(src)

def _segment_sum(src, seg, n):
    return jax.ops.segment_sum(src, seg, n)
kernel_name = 'mk_perceiver_d2_seqx_r2_6fcf3c'

def setup_inputs(seed: int=0):
    np.random.seed(seed)
    _w = jnp.asarray

    def _rec_inputs():
        import jax
        import jax.numpy as jnp
        _rk = jax.random.key(seed)
        x = -0.0002928 + 1 * jax.random.normal(jax.random.fold_in(_rk, 1), (16, 64, 512), jnp.float32)
        _lenS = 64 - jax.random.randint(jax.random.fold_in(_rk, 7), (16,), 0, max(1, 64 // 4) + 1, jnp.int32)
        _lenS2 = 1601 - jax.random.randint(jax.random.fold_in(_rk, 8), (16,), 0, max(1, 1601 // 4) + 1, jnp.int32)
        _ctx_1024P = jax.random.normal(jax.random.fold_in(_rk, 11), (16, 16, 512), jnp.float32)
        _ctx_1024c = jax.random.dirichlet(jax.random.fold_in(_rk, 511), 0.3 * jnp.ones((16,), jnp.float32), (16, 1601))
        _ctx_1024t = jnp.einsum('bsk,bkd->bsd', _ctx_1024c, _ctx_1024P)
        _ctx_1024t = _ctx_1024t * jax.lax.rsqrt(jnp.mean(jnp.square(_ctx_1024t)) + 1e-12) * 0.953939
        ctx_1024 = -1.39393e-06 + 0.999914 * (_ctx_1024t + 0.3 * jax.random.normal(jax.random.fold_in(_rk, 611), (16, 1601, 512), jnp.float32))
        itok_BxS_0_7 = jax.random.randint(jax.random.fold_in(_rk, 13), (16, 64), 0, 8, jnp.int32)
        itok_BxS_0_4092 = jax.random.randint(jax.random.fold_in(_rk, 14), (16, 64), 0, 4093, jnp.int32)
        _validS = jnp.arange(64)[None, :] < _lenS[:, None]
        _validS2 = jnp.arange(1601)[None, :] < _lenS2[:, None]
        _causal = jnp.tril(jnp.ones((64, 64), dtype=bool))
        mask_BxS2_ik0 = jnp.where(jnp.broadcast_to(_validS2[:, :], (16, 1601)), 0, 1).astype(jnp.int32)
        return (x, ctx_1024, itok_BxS_0_7, itok_BxS_0_4092, mask_BxS2_ik0)
    x, ctx_1024, itok_BxS_0_7, itok_BxS_0_4092, mask_BxS2_ik0 = _rec_inputs()

    def _L0_xattn_setup():
        import jax, jax.numpy as jnp
        import numpy as np
        EPS = 1e-05

        def layer_norm(x, gamma):
            mu = jnp.mean(x, axis=-1, keepdims=True)
            var = jnp.mean(jnp.square(x - mu), axis=-1, keepdims=True)
            return (x - mu) / jnp.sqrt(var + EPS) * gamma
        key = jax.random.key(seed)
        ks = jax.random.split(key, 10)
        b, n, j = (2, 1024, 1024)
        dim, ctx_dim, heads, dim_head, ff_mult = (512, 512, 16, 64, 4)
        inner = heads * dim_head
        ff_inner = ff_mult * dim
        s = 0.02
        return {'x': jax.random.normal(ks[0], (b, n, dim), jnp.float32), 'context': jax.random.normal(ks[1], (b, j, ctx_dim), jnp.float32), 'mask': jax.random.randint(ks[2], (b, j), 0, 2, jnp.int32), 'gamma': jnp.ones((dim,), jnp.float32), 'ctx_gamma': jnp.ones((ctx_dim,), jnp.float32), 'Wq': jax.random.normal(ks[3], (dim, inner), jnp.float32) * s, 'Wkv': jax.random.normal(ks[4], (ctx_dim, 2 * dim_head), jnp.float32) * s, 'Wout': jax.random.normal(ks[5], (inner, dim), jnp.float32) * s, 'Wff1': jax.random.normal(ks[6], (dim, 2 * ff_inner), jnp.float32) * s, 'Wff2': jax.random.normal(ks[7], (ff_inner, dim), jnp.float32) * s}
    _L0_xattn_all = _L0_xattn_setup()
    _L0_xattn_in = {k: v for k, v in _L0_xattn_all.items() if k in ('gamma', 'ctx_gamma', 'Wq', 'Wkv', 'Wout', 'Wff1', 'Wff2')}
    del _L0_xattn_all

    def _L0_attn_setup():
        import jax, jax.numpy as jnp
        import numpy as np
        B, T, D, H = (4, 1024, 512, 16)
        HD = D // H
        NEG = -np.finfo(np.float32).max
        key = jax.random.key(seed)
        ks = jax.random.split(key, 9)
        s = 1.0 / np.sqrt(D)
        return {'x': jax.random.normal(ks[0], (B, T, D), jnp.float32), 'wq': jax.random.normal(ks[1], (D, D), jnp.float32) * s, 'bq': jax.random.normal(ks[2], (D,), jnp.float32) * 0.02, 'wk': jax.random.normal(ks[3], (D, D), jnp.float32) * s, 'bk': jax.random.normal(ks[4], (D,), jnp.float32) * 0.02, 'wv': jax.random.normal(ks[5], (D, D), jnp.float32) * s, 'bv': jax.random.normal(ks[6], (D,), jnp.float32) * 0.02, 'wo': jax.random.normal(ks[7], (D, D), jnp.float32) * s, 'bo': jax.random.normal(ks[8], (D,), jnp.float32) * 0.02}
    _L0_attn_all = _L0_attn_setup()
    _L0_attn_in = {k: v for k, v in _L0_attn_all.items() if k in ('wq', 'bq', 'wk', 'bk', 'wv', 'bv', 'wo', 'bo')}
    del _L0_attn_all

    def _L0_ffn_setup():
        import jax, jax.numpy as jnp
        import numpy as np
        DIM = 512

        def _reference_tuple_inner(x, W_r, W_k, W_v, mu_r, mu_k):
            B, T, C = x.shape
            x_prev = jnp.concatenate([jnp.zeros((B, 1, C), x.dtype), x[:, :-1, :]], axis=1)
            xr = mu_r * x + (1.0 - mu_r) * x_prev
            xk = mu_k * x + (1.0 - mu_k) * x_prev
            r = jax.nn.sigmoid(jnp.einsum('btc,dc->btd', xr, W_r))
            k = jnp.einsum('btc,dc->btd', xk, W_k)
            k_act = jnp.square(jax.nn.relu(k))
            out = r * jnp.einsum('btc,dc->btd', k_act, W_v)
            new_state = x[:, -1, :]
            return (out, new_state)
        key = jax.random.key(seed)
        ks = jax.random.split(key, 6)
        B, T, C = (8, 1024, DIM)
        x = jax.random.normal(ks[0], (B, T, C), dtype=jnp.float32)
        s = 1.0 / np.sqrt(C)
        W_r = jax.random.uniform(ks[1], (C, C), jnp.float32, -s, s)
        W_k = jax.random.uniform(ks[2], (C, C), jnp.float32, -s, s)
        W_v = jax.random.uniform(ks[3], (C, C), jnp.float32, -s, s)
        mu_r = jax.random.uniform(ks[4], (C,), jnp.float32)
        mu_k = jax.random.uniform(ks[5], (C,), jnp.float32)
        return {'x': x, 'W_r': W_r, 'W_k': W_k, 'W_v': W_v, 'mu_r': mu_r, 'mu_k': mu_k}
    _L0_ffn_all = _L0_ffn_setup()
    _L0_ffn_in = {k: v for k, v in _L0_ffn_all.items() if k in ('W_r', 'W_k', 'W_v', 'mu_r', 'mu_k')}
    del _L0_ffn_all

    def _L1_xattn_setup():
        import math
        import jax, jax.numpy as jnp
        import numpy as np
        B, T, L, H = (4, 2048, 2048, 512)

        def _forward(hidden_states, advisor_states, advisor_ids, pointer_ids, Wqj, Wkj, Wvj, Wqi, Wki, Wvi, Wout, gain, council_weights):
            b, t, h = hidden_states.shape
            l = advisor_states.shape[1]
            inv_sqrt_h = 1.0 / math.sqrt(float(h))
            p = pointer_ids[:, :, None]
            indices = jnp.clip(jnp.concatenate([p, p + 1, p + 2], axis=-1), 0, l - 1)
            win_states = jax.vmap(lambda a, idx: a[idx])(advisor_states, indices)
            win_ids = jax.vmap(lambda a, idx: a[idx])(advisor_ids, indices)
            qj = hidden_states @ Wqj.T
            kj = win_states @ Wkj.T
            vj = win_states @ Wvj.T
            sj = jnp.einsum('bth,btwh->btw', qj, kj) * inv_sqrt_h
            l_rel, l_v1, l_v2 = (sj[:, :, 0], sj[:, :, 1], sj[:, :, 2])
            rel_ids = win_ids[:, :, 0]
            is_and = (rel_ids == 0).astype(sj.dtype)
            is_or = (rel_ids == 1).astype(sj.dtype)
            is_not = (rel_ids == 2).astype(sj.dtype)
            is_implies = (rel_ids == 3).astype(sj.dtype)
            is_xor = (rel_ids == 4).astype(sj.dtype)
            l_new = is_and * (l_v1 + l_v2) + is_or * jnp.maximum(l_v1, l_v2) + is_not * -l_v1 + is_implies * jnp.maximum(-l_v1, l_v2) + is_xor * jnp.abs(l_v1 - l_v2)
            mask_any = jnp.clip(is_and + is_or + is_not + is_implies + is_xor, 0.0, 1.0)
            l_final = mask_any * l_new + (1.0 - mask_any) * l_rel
            sj = jnp.stack([l_final, l_v1, l_v2], axis=-1)
            aj = jax.nn.softmax(sj, axis=-1)
            cj = jnp.einsum('btw,btwh->bth', aj, vj)
            qi = hidden_states @ Wqi.T
            ki = win_states @ Wki.T
            vi = win_states @ Wvi.T
            si = jnp.einsum('bth,btwh->btw', qi, ki) * inv_sqrt_h
            ai = jax.nn.softmax(si, axis=-1)
            ci = jnp.einsum('btw,btwh->bth', ai, vi)
            w = jax.nn.softmax(council_weights, axis=0)
            context = w[0] * cj + w[1] * ci
            return context @ Wout.T * gain
        key = jax.random.key(seed)
        ks = jax.random.split(key, 12)
        inp = {'hidden_states': jax.random.normal(ks[0], (B, T, H), jnp.float32), 'advisor_states': jax.random.normal(ks[1], (B, L, H), jnp.float32), 'advisor_ids': jax.random.randint(ks[2], (B, L), 0, 8, jnp.int32), 'pointer_ids': jax.random.randint(ks[3], (B, T), 0, L - 2, jnp.int32)}
        s = 1.0 / math.sqrt(H)
        names = ['Wqj', 'Wkj', 'Wvj', 'Wqi', 'Wki', 'Wvi', 'Wout']
        for i, n in enumerate(names):
            inp[n] = jax.random.normal(ks[4 + i], (H, H), jnp.float32) * s
        inp['gain'] = jnp.asarray(0.1, jnp.float32)
        inp['council_weights'] = jnp.ones((2,), jnp.float32)
        return inp
    _L1_xattn_all = _L1_xattn_setup()
    _L1_xattn_in = {k: v for k, v in _L1_xattn_all.items() if k in ('Wqj', 'Wkj', 'Wvj', 'Wqi', 'Wki', 'Wvi', 'Wout', 'gain', 'council_weights')}
    del _L1_xattn_all

    def _L1_attn_setup():
        import jax, jax.numpy as jnp
        import numpy as np
        B, T, E, H, L = (8, 2048, 512, 16, 64)
        HD = E // H
        key = jax.random.key(seed)
        ks = jax.random.split(key, 5)
        s = 1.0 / np.sqrt(E).astype(np.float32)
        x = jax.random.normal(ks[0], (B, T, E), dtype=jnp.float32)
        W_qkv = jax.random.normal(ks[1], (3 * E, E), dtype=jnp.float32) * s
        b_qkv = jnp.zeros((3 * E,), dtype=jnp.float32)
        W_out = jax.random.normal(ks[2], (E, E), dtype=jnp.float32) * s
        b_out = jnp.zeros((E,), dtype=jnp.float32)
        return {'x': x, 'W_qkv': W_qkv, 'b_qkv': b_qkv, 'W_out': W_out, 'b_out': b_out}
    _L1_attn_all = _L1_attn_setup()
    _L1_attn_in = {k: v for k, v in _L1_attn_all.items() if k in ('W_qkv', 'b_qkv', 'W_out', 'b_out')}
    del _L1_attn_all

    def _L1_ffn_setup():
        import jax, jax.numpy as jnp
        import numpy as np
        EPS = 1e-06
        LN_EPS = 1e-05

        def _absmean_core(W):
            gamma = jnp.mean(jnp.abs(W)) + EPS
            Ws = W / gamma
            Wq = jnp.sign(Ws) * jnp.minimum(jnp.round(jnp.abs(Ws)), 1.0)
            return (Wq, gamma)

        @jax.custom_vjp
        def absmean(W):
            return _absmean_core(W)[0]

        def _absmean_fwd(W):
            Wq, gamma = _absmean_core(W)
            return (Wq, gamma)

        def _absmean_bwd(gamma, g):
            return (g / gamma,)
        absmean.defvjp(_absmean_fwd, _absmean_bwd)

        def layernorm(x, w, b, eps=LN_EPS):
            mu = jnp.mean(x, axis=-1, keepdims=True)
            var = jnp.mean((x - mu) ** 2, axis=-1, keepdims=True)
            return (x - mu) * jax.lax.rsqrt(var + eps) * w + b
        key = jax.random.key(seed)
        k1, k2, k3 = jax.random.split(key, 3)
        d, h = (512, 2048)
        B, T = (8, 1024)
        return {'x': jax.random.normal(k1, (B, T, d), jnp.float32), 'W_fc': jax.random.normal(k2, (h, d), jnp.float32), 'ln_w': jnp.ones((h,), jnp.float32), 'ln_b': jnp.zeros((h,), jnp.float32), 'W_proj': jax.random.normal(k3, (d, h), jnp.float32)}
    _L1_ffn_all = _L1_ffn_setup()
    _L1_ffn_in = {k: v for k, v in _L1_ffn_all.items() if k in ('W_fc', 'ln_w', 'ln_b', 'W_proj')}
    del _L1_ffn_all
    return {'x': x, 'ctx_1024': ctx_1024, 'itok_BxS_0_7': itok_BxS_0_7, 'itok_BxS_0_4092': itok_BxS_0_4092, 'mask_BxS2_ik0': mask_BxS2_ik0, 'L0_xattn_gamma': _L0_xattn_in['gamma'], 'L0_xattn_ctx_gamma': _L0_xattn_in['ctx_gamma'], 'L0_xattn_Wq': _L0_xattn_in['Wq'], 'L0_xattn_Wkv': _L0_xattn_in['Wkv'], 'L0_xattn_Wout': _L0_xattn_in['Wout'], 'L0_xattn_Wff1': _L0_xattn_in['Wff1'], 'L0_xattn_Wff2': _L0_xattn_in['Wff2'], 'L0_attn_wq': _L0_attn_in['wq'], 'L0_attn_bq': _L0_attn_in['bq'], 'L0_attn_wk': _L0_attn_in['wk'], 'L0_attn_bk': _L0_attn_in['bk'], 'L0_attn_wv': _L0_attn_in['wv'], 'L0_attn_bv': _L0_attn_in['bv'], 'L0_attn_wo': _L0_attn_in['wo'], 'L0_attn_bo': _L0_attn_in['bo'], 'L0_ffn_W_r': _L0_ffn_in['W_r'], 'L0_ffn_W_k': _L0_ffn_in['W_k'], 'L0_ffn_W_v': _L0_ffn_in['W_v'], 'L0_ffn_mu_r': _L0_ffn_in['mu_r'], 'L0_ffn_mu_k': _L0_ffn_in['mu_k'], 'L1_xattn_Wqj': _L1_xattn_in['Wqj'], 'L1_xattn_Wkj': _L1_xattn_in['Wkj'], 'L1_xattn_Wvj': _L1_xattn_in['Wvj'], 'L1_xattn_Wqi': _L1_xattn_in['Wqi'], 'L1_xattn_Wki': _L1_xattn_in['Wki'], 'L1_xattn_Wvi': _L1_xattn_in['Wvi'], 'L1_xattn_Wout': _L1_xattn_in['Wout'], 'L1_xattn_gain': _L1_xattn_in['gain'], 'L1_xattn_council_weights': _L1_xattn_in['council_weights'], 'L1_attn_W_qkv': _L1_attn_in['W_qkv'], 'L1_attn_b_qkv': _L1_attn_in['b_qkv'], 'L1_attn_W_out': _L1_attn_in['W_out'], 'L1_attn_b_out': _L1_attn_in['b_out'], 'L1_ffn_W_fc': _L1_ffn_in['W_fc'], 'L1_ffn_ln_w': _L1_ffn_in['ln_w'], 'L1_ffn_ln_b': _L1_ffn_in['ln_b'], 'L1_ffn_W_proj': _L1_ffn_in['W_proj']}

def reference(x, ctx_1024, itok_BxS_0_7, itok_BxS_0_4092, mask_BxS2_ik0, L0_xattn_gamma, L0_xattn_ctx_gamma, L0_xattn_Wq, L0_xattn_Wkv, L0_xattn_Wout, L0_xattn_Wff1, L0_xattn_Wff2, L0_attn_wq, L0_attn_bq, L0_attn_wk, L0_attn_bk, L0_attn_wv, L0_attn_bv, L0_attn_wo, L0_attn_bo, L0_ffn_W_r, L0_ffn_W_k, L0_ffn_W_v, L0_ffn_mu_r, L0_ffn_mu_k, L1_xattn_Wqj, L1_xattn_Wkj, L1_xattn_Wvj, L1_xattn_Wqi, L1_xattn_Wki, L1_xattn_Wvi, L1_xattn_Wout, L1_xattn_gain, L1_xattn_council_weights, L1_attn_W_qkv, L1_attn_b_qkv, L1_attn_W_out, L1_attn_b_out, L1_ffn_W_fc, L1_ffn_ln_w, L1_ffn_ln_b, L1_ffn_W_proj):
    import jax
    import jax.numpy as jnp

    def _L0_xattn_ref(x, context, mask, gamma, ctx_gamma, Wq, Wkv, Wout, Wff1, Wff2):
        import jax, jax.numpy as jnp
        import numpy as np
        EPS = 1e-05

        def layer_norm(x, gamma):
            mu = jnp.mean(x, axis=-1, keepdims=True)
            var = jnp.mean(jnp.square(x - mu), axis=-1, keepdims=True)
            return (x - mu) / jnp.sqrt(var + EPS) * gamma
        heads, dim_head = (16, 64)
        b, n, dim = x.shape
        scale = dim_head ** (-0.5)
        xn = layer_norm(x, gamma)
        ctx = layer_norm(context, ctx_gamma)
        q = (xn @ Wq).reshape(b, n, heads, dim_head).transpose(0, 2, 1, 3) * scale
        kv = ctx @ Wkv
        k, v = (kv[..., :dim_head], kv[..., dim_head:])
        sim = jnp.einsum('bhid,bjd->bhij', q, k)
        sim = jnp.where((mask == 0)[:, None, None, :], -jnp.inf, sim)
        attn = jax.nn.softmax(sim, axis=-1)
        out = jnp.einsum('bhij,bjd->bhid', attn, v)
        out = out.transpose(0, 2, 1, 3).reshape(b, n, heads * dim_head)
        out = out @ Wout
        h = xn @ Wff1
        ff_inner = Wff2.shape[0]
        a, gate = (h[..., :ff_inner], h[..., ff_inner:])
        out = out + jax.nn.silu(gate) * a @ Wff2
        return out

    def _L0_attn_ref(x, wq, bq, wk, bk, wv, bv, wo, bo):
        import jax, jax.numpy as jnp
        import numpy as np
        B, T, D, H = (4, 1024, 512, 16)
        HD = D // H
        NEG = -np.finfo(np.float32).max
        b, t, d = x.shape

        def proj(w, bias):
            y = x @ w + bias
            return y.reshape(b, t, H, HD).transpose(0, 2, 1, 3)
        q = proj(wq, bq)
        k = proj(wk, bk)
        v = proj(wv, bv)
        scale = 1.0 / np.sqrt(HD).astype(np.float32)
        scores = jnp.einsum('bhqd,bhkd->bhqk', q, k) * scale
        mask = jnp.triu(jnp.full((t, t), NEG, jnp.float32), k=1)
        attn = jax.nn.softmax(scores + mask, axis=-1)
        out = jnp.einsum('bhqk,bhkd->bhqd', attn, v)
        out = out.transpose(0, 2, 1, 3).reshape(b, t, d)
        return out @ wo + bo

    def _L0_ffn_ref(x, W_r, W_k, W_v, mu_r, mu_k):
        import jax, jax.numpy as jnp
        import numpy as np
        DIM = 512

        def _reference_tuple_inner(x, W_r, W_k, W_v, mu_r, mu_k):
            B, T, C = x.shape
            x_prev = jnp.concatenate([jnp.zeros((B, 1, C), x.dtype), x[:, :-1, :]], axis=1)
            xr = mu_r * x + (1.0 - mu_r) * x_prev
            xk = mu_k * x + (1.0 - mu_k) * x_prev
            r = jax.nn.sigmoid(jnp.einsum('btc,dc->btd', xr, W_r))
            k = jnp.einsum('btc,dc->btd', xk, W_k)
            k_act = jnp.square(jax.nn.relu(k))
            out = r * jnp.einsum('btc,dc->btd', k_act, W_v)
            new_state = x[:, -1, :]
            return (out, new_state)
        return _reference_tuple_inner(x, W_r, W_k, W_v, mu_r, mu_k)[0]

    def _L1_xattn_ref(hidden_states, advisor_states, advisor_ids, pointer_ids, Wqj, Wkj, Wvj, Wqi, Wki, Wvi, Wout, gain, council_weights):
        import math
        import jax, jax.numpy as jnp
        import numpy as np
        B, T, L, H = (4, 2048, 2048, 512)

        def _forward(hidden_states, advisor_states, advisor_ids, pointer_ids, Wqj, Wkj, Wvj, Wqi, Wki, Wvi, Wout, gain, council_weights):
            b, t, h = hidden_states.shape
            l = advisor_states.shape[1]
            inv_sqrt_h = 1.0 / math.sqrt(float(h))
            p = pointer_ids[:, :, None]
            indices = jnp.clip(jnp.concatenate([p, p + 1, p + 2], axis=-1), 0, l - 1)
            win_states = jax.vmap(lambda a, idx: a[idx])(advisor_states, indices)
            win_ids = jax.vmap(lambda a, idx: a[idx])(advisor_ids, indices)
            qj = hidden_states @ Wqj.T
            kj = win_states @ Wkj.T
            vj = win_states @ Wvj.T
            sj = jnp.einsum('bth,btwh->btw', qj, kj) * inv_sqrt_h
            l_rel, l_v1, l_v2 = (sj[:, :, 0], sj[:, :, 1], sj[:, :, 2])
            rel_ids = win_ids[:, :, 0]
            is_and = (rel_ids == 0).astype(sj.dtype)
            is_or = (rel_ids == 1).astype(sj.dtype)
            is_not = (rel_ids == 2).astype(sj.dtype)
            is_implies = (rel_ids == 3).astype(sj.dtype)
            is_xor = (rel_ids == 4).astype(sj.dtype)
            l_new = is_and * (l_v1 + l_v2) + is_or * jnp.maximum(l_v1, l_v2) + is_not * -l_v1 + is_implies * jnp.maximum(-l_v1, l_v2) + is_xor * jnp.abs(l_v1 - l_v2)
            mask_any = jnp.clip(is_and + is_or + is_not + is_implies + is_xor, 0.0, 1.0)
            l_final = mask_any * l_new + (1.0 - mask_any) * l_rel
            sj = jnp.stack([l_final, l_v1, l_v2], axis=-1)
            aj = jax.nn.softmax(sj, axis=-1)
            cj = jnp.einsum('btw,btwh->bth', aj, vj)
            qi = hidden_states @ Wqi.T
            ki = win_states @ Wki.T
            vi = win_states @ Wvi.T
            si = jnp.einsum('bth,btwh->btw', qi, ki) * inv_sqrt_h
            ai = jax.nn.softmax(si, axis=-1)
            ci = jnp.einsum('btw,btwh->bth', ai, vi)
            w = jax.nn.softmax(council_weights, axis=0)
            context = w[0] * cj + w[1] * ci
            return context @ Wout.T * gain
        return _forward(hidden_states, advisor_states, advisor_ids, pointer_ids, Wqj, Wkj, Wvj, Wqi, Wki, Wvi, Wout, gain, council_weights)

    def _L1_attn_ref(x, W_qkv, b_qkv, W_out, b_out):
        import jax, jax.numpy as jnp
        import numpy as np
        B, T, E, H, L = (8, 2048, 512, 16, 64)
        HD = E // H
        b, t, e = x.shape
        scaling = HD ** (-0.5)
        qkv = x @ W_qkv.T + b_qkv
        q, k, v = jnp.split(qkv, 3, axis=-1)
        q = q * scaling

        def to_blocks(a):
            return a.reshape(b, t, H, HD).transpose(0, 2, 1, 3).reshape(b, H, t // L, L, HD)
        qb, kb, vb = (to_blocks(q), to_blocks(k), to_blocks(v))
        attn = jax.nn.softmax(jnp.einsum('bhnld,bhnmd->bhnlm', qb, kb), axis=-1)
        out = jnp.einsum('bhnlm,bhnmd->bhnld', attn, vb)
        out = out.reshape(b, H, t, HD).transpose(0, 2, 1, 3).reshape(b, t, e)
        return out @ W_out.T + b_out

    def _L1_ffn_ref(x, W_fc, ln_w, ln_b, W_proj):
        import jax, jax.numpy as jnp
        import numpy as np
        EPS = 1e-06
        LN_EPS = 1e-05

        def _absmean_core(W):
            gamma = jnp.mean(jnp.abs(W)) + EPS
            Ws = W / gamma
            Wq = jnp.sign(Ws) * jnp.minimum(jnp.round(jnp.abs(Ws)), 1.0)
            return (Wq, gamma)

        @jax.custom_vjp
        def absmean(W):
            return _absmean_core(W)[0]

        def _absmean_fwd(W):
            Wq, gamma = _absmean_core(W)
            return (Wq, gamma)

        def _absmean_bwd(gamma, g):
            return (g / gamma,)
        absmean.defvjp(_absmean_fwd, _absmean_bwd)

        def layernorm(x, w, b, eps=LN_EPS):
            mu = jnp.mean(x, axis=-1, keepdims=True)
            var = jnp.mean((x - mu) ** 2, axis=-1, keepdims=True)
            return (x - mu) * jax.lax.rsqrt(var + eps) * w + b
        h = jnp.einsum('btd,hd->bth', x, absmean(W_fc))
        h = jax.nn.gelu(h, approximate=False)
        h = layernorm(h, ln_w, ln_b)
        return jnp.einsum('bth,dh->btd', h, absmean(W_proj))
    x = x + _L0_xattn_ref(_layernorm(x, axis=-1), ctx_1024, mask_BxS2_ik0, L0_xattn_gamma, L0_xattn_ctx_gamma, L0_xattn_Wq, L0_xattn_Wkv, L0_xattn_Wout, L0_xattn_Wff1, L0_xattn_Wff2)
    x = x + _L0_attn_ref(_layernorm(x, axis=-1), L0_attn_wq, L0_attn_bq, L0_attn_wk, L0_attn_bk, L0_attn_wv, L0_attn_bv, L0_attn_wo, L0_attn_bo)
    x = x + _L0_ffn_ref(_layernorm(x, axis=-1), L0_ffn_W_r, L0_ffn_W_k, L0_ffn_W_v, L0_ffn_mu_r, L0_ffn_mu_k)
    x = x + _L1_xattn_ref(_layernorm(x, axis=-1), ctx_1024, itok_BxS_0_7, itok_BxS_0_4092, L1_xattn_Wqj, L1_xattn_Wkj, L1_xattn_Wvj, L1_xattn_Wqi, L1_xattn_Wki, L1_xattn_Wvi, L1_xattn_Wout, L1_xattn_gain, L1_xattn_council_weights)
    x = x + _L1_attn_ref(_layernorm(x, axis=-1), L1_attn_W_qkv, L1_attn_b_qkv, L1_attn_W_out, L1_attn_b_out)
    x = x + _L1_ffn_ref(_layernorm(x, axis=-1), L1_ffn_W_fc, L1_ffn_ln_w, L1_ffn_ln_b, L1_ffn_W_proj)
    return x

_drawn_inputs = setup_inputs


def setup_inputs(seed=0):
    import zlib

    import numpy as np

    out = dict(_drawn_inputs(seed))
    spreads = {'L0_xattn_gamma': (1.0, 0.2),
     'L0_xattn_ctx_gamma': (1.0, 0.2),
     'L1_xattn_council_weights': (1.0, 0.6),
     'L1_attn_b_qkv': (0.0, 0.1),
     'L1_attn_b_out': (0.0, 0.1),
     'L1_ffn_ln_w': (1.0, 0.2),
     'L1_ffn_ln_b': (0.0, 0.1)}
    factors = {'L0_xattn_Wq': 4.297,
     'L0_attn_bq': 8.0,
     'L0_attn_bk': 8.0,
     'L0_ffn_W_r': 3.011,
     'L0_ffn_mu_r': 6.643,
     'L1_xattn_Wqj': 5.616,
     'L1_xattn_Wkj': 5.815,
     'L1_xattn_Wqi': 6.193,
     'L1_xattn_Wki': 6.404}
    for name, (base, spread) in spreads.items():
        noise = np.random.default_rng([zlib.crc32(name.encode()), seed]).standard_normal(out[name].shape)
        drawn = base * np.exp(spread * noise) if base else spread * noise
        out[name] = jnp.asarray(drawn.astype(out[name].dtype))
    for name, factor in factors.items():
        out[name] = (out[name] * factor).astype(out[name].dtype)
    return out
```

```python
from contextlib import ExitStack

import concourse.bass as bass
from concourse import mybir

F32 = mybir.dt.float32
BF16 = mybir.dt.bfloat16
I32 = mybir.dt.int32
ALU = mybir.AluOpType
ACT = mybir.ActivationFunctionType
AX = mybir.AxisListType

LAYERS = 6
P = 128
B, S, D = 16, 64, 512
T = B * S // P
HT = T // 2
KC = D // P
SCTX = 1601
XH, XD = 16, 64
FF = 2048
AH, AD = 16, 32
RING = 6
STAGED = 2
LN_EPS = 1e-5
ABSMEAN_EPS = 1e-6
MASKED = -3.0e38
NEG = -3.4028234663852886e38
ALL_MASKED = 1.0e38
ACT_CREDIT = 2
CONSTS = 11
SC_E = 20
LINKS = {"ln0": 36, "attend13": 81, "attend4": 30, "attention": 30, "mix": 21, "window": 95, "mlp": 85}
RSQRT_SEED = float(0x5F3759DF)
KB = 256

FULL_TILES = (SCTX + P - 1) // P
TAIL_TILES = 4
TAIL = TAIL_TILES * P
HEAD_ROWS = SCTX - (FULL_TILES - 1) * P
KEYS = FULL_TILES * P


class Stage:

    def __init__(self, letters, passes=1, banks=8, rolling=False):
        self.letters, self.passes, self.banks, self.rolling = letters, passes, banks, rolling
        assert not rolling or len(letters) == banks
        self.n = len(letters)
        self.n_dve = self.n - letters.count("A")
        self.n_act = letters.count("A")
        self.n_hi = letters.count("h")
        self.base = None

    def freed(self, g):
        head = self.letters[:g + 1]
        return (True, head.count("A")) if self.letters[g] == "A" else (False, len(head) - head.count("A"))


class Chain:

    def __init__(self, eng, semaphore, base=0, i=0, per_pass=0):
        self.eng, self.sem, self.start, self.n, self.per_pass = eng, semaphore, base + i * per_pass, 0, per_pass

    def link(self, ins):
        self.n += 1
        ins.then_inc(self.sem, 1)
        self.eng.wait_ge(self.sem, self.start + self.n)

    def close(self):
        assert not self.per_pass or self.n == self.per_pass, f"links in a pass: {self.n}"


def build(nc, a, out):
    ctx = ExitStack()
    with ctx:
        def sb(name, shape, dt=F32):
            return ctx.enter_context(nc.sbuf_tensor(name, shape, dt))

        def sem(name):
            return ctx.enter_context(nc.semaphore(name))

        X = sb("X", [P, T, D])
        y_mem = sb("y_mem", [P, 16 * KB])
        o_mem = sb("o_mem", [P, 32 * KB])
        big = sb("big", [P, 64 * KB])
        side = sb("side", [P, 8 * KB])
        ring_hi = sb("ring_hi", [P, RING, KC, D], BF16)
        ring_lo = sb("ring_lo", [P, RING, KC, D], BF16)
        stage = sb("stage", [P, STAGED, KC, D])
        ybuf = sb("ybuf", [P, 2, D])
        ident = sb("ident", [P, P])
        identb = sb("identb", [P, P], BF16)
        ones = sb("ones", [P, P])
        causal = sb("causal", [P, S])
        stats = sb("stats", [P, 4, 6])
        mv = sb("mv", [P, 4, 2])
        nw = sb("nw", [P, 3, 4])
        cols = sb("cols", [P, 48])
        small = sb("small", [P, 168])
        key_no = sb("key_no", [P, S], I32)
        flag = sb("flag", [P, 1], I32)
        psum = ctx.enter_context(nc.psum_tensor("psum", [P, 8, 512], F32))

        def settle(eng):
            eng.sem_inc(idle, 1)

        def carve(mem, at_kb, kb, dt, pattern=None, **dims):
            v = mem[:, int(at_kb * KB):int((at_kb + kb) * KB)]
            if dt != F32:
                v = v.bitcast(dt)
            return v.rearrange(pattern, **dims) if pattern else v

        def halves(mem, at_kb, kb, pattern, **dims):
            return [carve(mem, at_kb + i * kb, kb, BF16, pattern, **dims) for i in range(2)]

        yT = halves(y_mem, 0, 8, "p (k n) -> p k n", k=KC)
        yh = halves(y_mem, 0, 4, "p (k n) -> p k n", k=KC)
        y2 = halves(y_mem, 8, 4, "p (k n) -> p k n", k=KC)
        oT = halves(o_mem, 0, 16, "p (k n) -> p k n", k=8)
        Q = carve(big, 0, 32, BF16, "p (b h s) -> p b h s", b=B, h=XH)
        x0 = carve(big, 32, 8, F32, "p (t n) -> p t n", t=HT)
        gamma_row = carve(big, 40, 2, F32)
        wkv_f = carve(o_mem, 0, 2, F32, "p (k n) -> p k n", k=KC)
        mask_i = carve(o_mem, 8, 7, I32)
        mask_f = carve(o_mem, 16, 7, F32)
        maskadd = carve(side, 0, 3.25, BF16)
        wk = halves(side, 3.25, 1, "p (k n) -> p k n", k=KC)
        wv = halves(side, 5.25, 0.5, "p (k n) -> p k n", k=KC)
        ffT = halves(big, 0, 32, "p (k n) -> p k n", k=FF // P)
        prod = carve(side, 0, 4, F32, "p (i n) -> p i n", i=2)
        qh = halves(big, 0, 4, "p (k n) -> p k n", k=KC)
        kh = halves(big, 8, 4, "p (k n) -> p k n", k=KC)
        vb = halves(big, 16, 8, "p (b g m e) -> p b g m e", b=8, g=8, m=2)
        vb_words = carve(big, 16, 16, I32)
        prob = carve(big, 32, 8, F32, "p (i r m s) -> p i r m s", i=2, r=4, m=4)
        pT = [carve(big, 40 + 4 * i, 4, BF16, "p (i g q) -> p i g q", i=2, g=8) for i in range(2)]
        vf = carve(big, 48, 4, F32, "p (i n) -> p i n", i=2)
        ah = halves(big, 52, 4, "p (k n) -> p k n", k=KC)
        bv = carve(side, 4, 1, F32, "p (j e) -> p j e", j=2)
        bo = carve(side, 5, 2, F32)
        woT = halves(y_mem, 8, 4, "p (k n) -> p k n", k=KC)
        zp = carve(big, 0, 8.125, F32, "p (k b s) -> p k b s", k=KC, b=8)
        mixT = [halves(big, 9 + 8 * i, 4, "p (k n) -> p k n", k=KC) for i in range(2)]
        mix_t = carve(big, 25, 4, F32, "p (i n) -> p i n", i=2)
        mix_f = carve(big, 29, 4, F32, "p (i n) -> p i n", i=2)
        kact = halves(big, 33, 4, "p (k n) -> p k n", k=KC)
        recept = carve(big, 41, 8, F32, "p (t n) -> p t n", t=HT)
        relu = carve(big, 49, 4, F32, "p (i n) -> p i n", i=2)
        relu2 = carve(big, 53, 4, F32, "p (i n) -> p i n", i=2)
        fold = [halves(big, 8 * i, 4, "p (k n) -> p k n", k=KC) for i in range(4)]
        win = carve(big, 32, 24, F32, "p (t w n) -> p t w n", t=HT, w=3)
        comb = carve(big, 56, 4, F32, "p (i n) -> p i n", i=2)
        junk = carve(big, 60, 4, F32, "p (i n) -> p i n", i=2)
        ids_rows = carve(o_mem, 0, 2, I32, "p (t s) -> p t s", t=T)
        id_hit = carve(o_mem, 3, 0.25, F32)
        ptr = carve(o_mem, 4, 1, I32)
        ptf = carve(o_mem, 5, 1, F32)
        row_of = carve(o_mem, 6, 1, I32)[:, 0:4 * T]
        sc = carve(o_mem, 8, 2, F32, "p (n t) -> p n t", t=HT)
        rel_id = carve(o_mem, 7, 0.25, F32)
        fcT = carve(big, 0, 16, BF16, "p (i k n) -> p i k n", i=4, k=KC)
        projT = carve(big, 16, 16, BF16, "p (k n) -> p k n", k=FF // P)
        lnw = carve(big, 32, 8, F32)
        lnb = carve(big, 40, 8, F32)
        hid = carve(o_mem, 0, 16, F32, "p (i n) -> p i n", i=2)
        hT = [halves(o_mem, 16 + 8 * i, 4, "p (k n) -> p k n", k=FF // P) for i in range(2)]

        C_CGAMMA, C_BQ0, C_BK0, C_BQ1, C_BK1, C_MUR, C_MUK, C_OMR, C_OMK, C_GAIN, C_CW = 0, 4, 8, 12, 16, 20, 24, 28, 32, 36, 38
        gsum = small[:, 0:32].rearrange("p (w b) -> p w b", w=2)
        gtot = small[:, 32:34]
        thr = small[:, 34:36]
        nthr = small[:, 36:38]
        s_max = small[:, 40:72].rearrange("p (i h) -> p i h", i=2)
        s_sum = small[:, 72:104].rearrange("p (i h) -> p i h", i=2)
        xq_max = small[:, 104:112]
        xq_neg = small[:, 112:120]
        xq_sum = small[:, 120:128]
        xq_ok = small[:, 128:136]
        xq_r = small[:, 136:144]
        council = small[:, 160:168]
        tile_base = small[:, 144:152].bitcast(I32)

        x_loaded, cols_loaded, gamma_loaded, wkv_loaded, mask_loaded = map(
            sem, ("x_loaded", "cols_loaded", "gamma_loaded", "wkv_loaded", "mask_loaded"))
        stage_loaded = [sem(f"stage_loaded{i}") for i in range(STAGED)]
        bias_loaded, ids_loaded, win_loaded, out_stored = map(sem, ("bias_loaded", "ids_loaded", "win_loaded", "out_stored"))
        idle = sem("idle")
        const_ready = sem("const_ready")
        pool_split = sem("pool_split")
        pool_part = sem("pool_part")
        group_ready = sem("group_ready")
        act_hi = sem("act_hi")
        dve_freed = sem("dve_freed")
        act_freed = sem("act_freed")
        step = sem("step")
        y_ready = sem("y_ready")
        wkv_ready = sem("wkv_ready")
        sg_ready, prod_ready, prod_hi, prod_lo = map(sem, ("sg_ready", "prod_ready", "prod_hi", "prod_lo"))
        v_sum, v_hi, v_done, p_max, p_exp, o_free = map(sem, ("v_sum", "v_hi", "v_done", "p_max", "p_exp", "o_free"))
        layer_done = sem("layer_done")
        zeroed = sem("zeroed")
        om_ready, mix_a, mix_b, mix_hi, mix_lo = map(sem, ("om_ready", "mix_a", "mix_b", "mix_hi", "mix_lo"))
        relu_ready, relu_sq, relu_hi, relu_lo = map(sem, ("relu_ready", "relu_sq", "relu_hi", "relu_lo"))
        rows_ready, win_used, logit, e_ready, comb_ready = map(sem, ("rows_ready", "win_used", "logit", "e_ready", "comb_ready"))
        thr_ready, gelu_done, hid_norm, hid_ready = map(sem, ("thr_ready", "gelu_done", "hid_norm", "hid_ready"))
        flag_part, flag_ready, x_attended, gamma_part, hid_scaled = map(
            sem, ("flag_part", "flag_ready", "x_attended", "gamma_part", "hid_scaled"))

        def rows(w, c0=0):
            return w[:, c0:c0 + D].rearrange("(k p) n -> p k n", p=P)

        entries, W = [], {}

        def entry(key, kind, src=None):
            W[key] = len(entries)
            entries.append((kind, src))

        for i in range(2):
            entry(("q", i), "n", rows(a["L0_xattn_Wq"], i * D))
        for i in range(4):
            entry(("ffa", i), "n", rows(a["L0_xattn_Wff1"], i * D))
            entry(("ffg", i), "n", rows(a["L0_xattn_Wff1"], FF + i * D))
        for i in range(2):
            entry(("xo", i), "n", rows(a["L0_xattn_Wout"][i * D:(i + 1) * D, :]))
        for i in range(4):
            entry(("ff2", i), "n", rows(a["L0_xattn_Wff2"][i * D:(i + 1) * D, :]))
        before_x = 8
        ends = [len(entries)]
        for n in "qkvo":
            entry(("w0", n), "n", rows(a["L0_attn_w" + n]))
        ends.append(len(entries))
        for n in "rkv":
            entry(("mixn", n), "n", rows(a["L0_ffn_W_" + n]))
            entry(("mix", n), "T")
        ends.append(len(entries))
        for n in ("Wqj", "Wkj", "Wqi", "Wki", "Wout"):
            entry(("win", n), "n", rows(a["L1_xattn_" + n]))
        entry(("win", "WoutT"), "T")
        for n in ("Wvj", "Wvi"):
            entry(("win", n), "n", rows(a["L1_xattn_" + n]))
        ends.append(len(entries))
        for i, n in enumerate("qkv"):
            entry(("w1n", n), "n", rows(a["L1_attn_W_qkv"][i * D:(i + 1) * D, :]))
            entry(("w1", n), "T")
        entry(("w1n", "o"), "n", rows(a["L1_attn_W_out"]))
        ends.append(len(entries))
        for i in range(4):
            entry(("fc", i), "t", rows(a["L1_ffn_W_fc"][i * D:(i + 1) * D, :]))
        for i in range(4):
            entry(("proj", i), "t", rows(a["L1_ffn_W_proj"], i * D))
        ends.append(len(entries))
        entries = entries[:ends[LAYERS - 1]]
        staged_order = [e for e, (kind, _) in enumerate(entries) if kind != "T"]
        released = {}

        def w_of(key):
            s = W[key] % RING
            return ring_hi[:, s], ring_lo[:, s]

        def wait_slot(eng, e):
            if e >= RING:
                eng.wait_ge(*released[e - RING])

        def wait_split(eng, key):
            eng.wait_ge(pool_split, staged_order.index(W[key]) + 1)

        plan = {"ln0": Stage("hhhh", 2), "q": Stage("hhhh", 4, 4, True), "ff": Stage("DADA", 16, 4, True),
                "xout": Stage("DDDD", 2)}
        if LAYERS > 5:
            plan["gamma"] = Stage("D")
        attn = ("hhhh" "hhhh" "hhhh" "DDDD"
                "DDDD" + "DDDDhhDh" * 3 + "hhDh"
                + "DDDD")
        if LAYERS > 1:
            plan["attn0"] = Stage(attn, 2)
        if LAYERS > 2:
            plan["turn_mix"] = Stage("AD" * 6)
            plan["mix"] = Stage("AAAA" "AAAA" "DDDD" "DDDD", 2)
        if LAYERS > 3:
            plan["fold"] = Stage("hhhh" "hhhh" "ADAD" "hhhh" "hhhh")
            plan["window"] = Stage("hhhh" "DDDDDDDD" "hhhhhhhh" "DDDD", 2)
        if LAYERS > 4:
            plan["turn_w1"] = Stage("AD" * 8)
            plan["attn1"] = Stage(attn, 2)
        if LAYERS > 5:
            plan["turn_mlp"] = Stage("AD" * 8)
            plan["mlp"] = Stage("hhhh" + "AAAA" + "AAAAhhhhD" * 3 + "hhhhD", 2)
        total = [0, 0, ACT_CREDIT, 0]
        for st in plan.values():
            st.base = tuple(total)
            for i, n in enumerate((st.n, st.n_dve, st.n_act, st.n_hi)):
                total[i] += n * st.passes

        def after(name, groups=None):
            st = plan[name]
            return group_ready, st.base[0] + (st.n * st.passes if groups is None else groups)

        class Pass:

            def __init__(self, eng, name, i=0):
                self.eng, self.st = eng, plan[name]
                st = self.st
                self.ready, self.dve, self.act, self.hi = (
                    b + n * i for b, n in zip(st.base, (st.n, st.n_dve, st.n_act, st.n_hi)))
                self.first = st.base[0] == 0
                self.at = 0

            def bank(self, g):
                return psum[:, g % self.st.banks, :]

            def open(self):
                g, st = self.at, self.st
                self.at += 1
                if st.rolling:
                    is_act, n = st.freed(g)
                    if is_act:
                        self.eng.wait_ge(act_freed, self.act - st.n_act + n)
                    else:
                        self.eng.wait_ge(dve_freed, self.dve - st.n_dve + n)
                elif g >= st.banks:
                    is_act, n = st.freed(g - st.banks)
                    self.eng.wait_ge(act_freed if is_act else dve_freed, (self.act if is_act else self.dve) + n)
                elif g == 0:
                    self.all_free()
                return self.bank(g)

            def all_free(self):
                self.eng.wait_ge(dve_freed, self.dve)
                self.eng.wait_ge(act_freed, self.act)

            def take(self, g):
                self.eng.wait_ge(group_ready, self.ready + g + 1)
                return self.bank(g)

            def wait_hi(self, g):
                self.eng.wait_ge(act_hi, self.hi + self.st.letters[:g + 1].count("h"))
                return self.bank(g)

            def wait_done(self, g):
                is_act, n = self.st.freed(g)
                self.eng.wait_ge(act_freed if is_act else dve_freed, (self.act if is_act else self.dve) + n)

        for i in range(2):
            released[W["q", i]] = after("q", 8 * (i + 1))
        for i in range(4):
            released[W["ffa", i]] = released[W["ffg", i]] = after("ff", 16 * (i + 1))
            released[W["ff2", i]] = after("xout")
        for i in range(2):
            released[W["xo", i]] = after("xout")
        if LAYERS > 1:
            for n in "qkvo":
                released[W["w0", n]] = after("attn0")
        if LAYERS > 2:
            for i, n in enumerate("rkv"):
                released[W["mixn", n]] = after("turn_mix", 4 * (i + 1))
                released[W["mix", n]] = after("mix")
        if LAYERS > 3:
            for n, g in (("Wqj", 4), ("Wkj", 4), ("Wqi", 8), ("Wki", 8), ("Wout", 12), ("WoutT", 20), ("Wvj", 16), ("Wvi", 20)):
                released[W["win", n]] = after("fold", g)
        if LAYERS > 4:
            for i, n in enumerate("qkvo"):
                released[W["w1n", n]] = after("turn_w1", 4 * (i + 1))
                if n != "o":
                    released[W["w1", n]] = after("attn1")
        if LAYERS > 5:
            for i in range(4):
                released[W["fc", i]] = after("turn_mlp", 2 * (i + 1))
                released[W["proj", i]] = after("turn_mlp", 8 + 2 * (i + 1))
        y_base, n_y = {}, 0
        for name, passes, n in (("ln0", 2, 4), ("attn0", 2, 4), ("mix", 2, 4), ("window", 2, 4), ("attn1", 2, 4), ("mlp", 2, 4)):
            y_base[name] = (n_y, n)
            n_y += passes * n

        def xviews(nkt):
            n = nkt * P
            full = nkt > TAIL_TILES
            v = {"full": full, "nkt": nkt, "n": n, "chunks": (nkt + 3) // 4, "m0": 0 if full else (FULL_TILES - 1 - TAIL_TILES) * P}
            at = 32

            def put(key, kb, dt, pattern=None, **dims):
                nonlocal at
                v[key] = carve(big, at, kb, dt, pattern, **dims)
                at += kb
            kb = n / 512
            put("KA", kb, BF16)
            put("KB", kb, BF16)
            put("V", kb, F32, "p (t e) -> p t e", e=XD)
            put("mb", kb, BF16)
            shared = at
            put("ctx", 8, F32, "p (t n) -> p t n", t=4)
            put("cT_hi", 4, BF16, "p (k n) -> p k n", k=KC)
            put("cT_lo", 4, BF16, "p (k n) -> p k n", k=KC)
            if full:
                v["P"] = carve(big, shared, n / 256, F32, "p (i n) -> p i n", i=1)
                v["PT"] = carve(big, shared + n / 256, 4, F32, "p (i t q) -> p i t q", i=2, t=4)
            else:
                put("P", n / 256 * 2, F32, "p (i n) -> p i n", i=2)
                put("PT", 4, F32, "p (i t q) -> p i t q", i=2, t=4)
            put("O", 2, F32, "p (j d) -> p j d", j=8)
            assert at <= 64, at
            return v

        XN = {n: sem("x_" + n) for n in (
            "ctx_loaded",
            "ctx_zero",
            "ctx_norm",
            "ctx_turned",
            "ctx_hi", "ctx_lo",
            "shared_ready",
            "shared_free",
            "k_hi", "v_mm", "v_copied", "s_mm", "s_max", "exp", "p_turned", "p_act", "p_dve", "pv", "o_norm",
            "ot_hi", "g_loaded", "g_summed")}
        xstep = sem("xstep")

        def xmap(nkt):
            v = xviews(nkt)
            v["tiles_of"] = [range(4 * c, min(4 * c + 4, nkt)) for c in range(v["chunks"])]
            v["S"] = (lambda j: psum[:, 0:4].rearrange("p a n -> p (a n)")[:, 0:v["n"]]) if v["full"] \
                else (lambda j: psum[:, j % 2])
            v["PTbank"] = (lambda w: psum[:, 6 + w % 2]) if v["full"] else (lambda w: psum[:, 2 + w % 2])
            v["groups"] = 8 * v["chunks"]
            v["shared_n"] = 2 * v["chunks"] + 2
            return v
        O_BANK, SHARED = psum[:, 4], psum[:, 5]

        block = ctx.enter_context(nc.Block())

        @block.sync
        def _(sp):
            def stage_block(e):
                i = staged_order.index(e)
                if i >= STAGED:
                    sp.wait_ge(pool_split, i - STAGED + 1)
                sp.dma_start(stage[:, i % STAGED], entries[e][1]).then_inc(stage_loaded[i % STAGED], 16)

            def across(v, n=P):
                return v.rearrange("(a n) -> a n", a=1).to_broadcast([n, v.shape[0]])

            for t in range(T):
                sp.dma_start(X[:, t], a["x"][2 * t:2 * t + 2].rearrange("b s d -> (b s) d")).then_inc(x_loaded, 16)
            sp.dma_start(gamma_row, across(a["L0_xattn_gamma"])).then_inc(gamma_loaded, 16)
            with nc.allow_non_contiguous_dma(reason="short vectors as columns"):
                for c, src in ((C_CGAMMA, a["L0_xattn_ctx_gamma"]), (C_BQ0, a["L0_attn_bq"]), (C_BK0, a["L0_attn_bk"]),
                               (C_BQ1, a["L1_attn_b_qkv"][0:D]), (C_BK1, a["L1_attn_b_qkv"][D:2 * D]),
                               (C_MUR, a["L0_ffn_mu_r"]), (C_MUK, a["L0_ffn_mu_k"])):
                    sp.dma_start(cols[:, c:c + KC], src.rearrange("(k p) -> p k", p=P)).then_inc(cols_loaded, 16)
                sp.dma_start(cols[:, C_GAIN:C_GAIN + 1], across(a["L1_xattn_gain"])).then_inc(cols_loaded, 16)
                sp.dma_start(cols[:, C_CW:C_CW + 2], across(a["L1_xattn_council_weights"])).then_inc(cols_loaded, 16)
            stage_block(staged_order[0])
            stage_block(staged_order[1])
            sp.dma_start(wkv_f, a["L0_xattn_Wkv"].rearrange("(k p) n -> p k n", p=P)).then_inc(wkv_loaded, 16)
            sp.dma_start(mask_i[0:B, 0:SCTX], a["mask_BxS2_ik0"]).then_inc(mask_loaded, 16)
            for e in staged_order[2:before_x]:
                stage_block(e)

            fc_rows = a["L1_ffn_W_fc"].rearrange("(b p) n -> b p n", p=P)
            proj_rows = a["L1_ffn_W_proj"].rearrange("d (c n) -> (d c) n", n=D).rearrange("(b p) n -> b p n", p=P)

            def context(nkt):
                v = xmap(nkt)
                with sp.Fori(0, B) as b:
                    if LAYERS > 5:
                        sp.wait_ge(XN["g_summed"], b)
                        settle(sp)
                        for w, r in enumerate((fc_rows, proj_rows)):
                            sp.dma_start(ybuf[:, w], r[bass.ds(b, 1)].rearrange("b p n -> (b p) n"))\
                                .then_inc(XN["g_loaded"], 16)
                    for c, tiles in enumerate(v["tiles_of"]):
                        sp.wait_ge(XN["ctx_turned"], b * nkt + tiles[0])
                        settle(sp)
                        if v["full"] and c == 0:
                            sp.wait_ge(XN["pv"], b * v["groups"])
                            settle(sp)
                        for kt in tiles:
                            src = a["ctx_1024"][bass.ds(b, 1)].rearrange("b s d -> (b s) d")
                            if kt == FULL_TILES - 1:
                                sp.wait_ge(XN["ctx_zero"], b + 1)
                                settle(sp)
                                sp.dma_start(v["ctx"][0:HEAD_ROWS, kt % 4], src[0:HEAD_ROWS]).then_inc(XN["ctx_loaded"], 16)
                            else:
                                r0 = HEAD_ROWS + kt * P if v["full"] else SCTX - TAIL + kt * P
                                sp.dma_start(v["ctx"][:, kt % 4], src[r0:r0 + P]).then_inc(XN["ctx_loaded"], 16)

            sp.wait_ge(flag_ready, 1)
            sp.wait_ge(*after("q"))
            head_rows_used = sp.value_load(flag[0:1, 0:1], min_val=0, max_val=1)
            with sp.If(head_rows_used > 0):
                context(FULL_TILES)
            with sp.If(head_rows_used < 1):
                context(TAIL_TILES)

            def load_bias(n, v_src, o_src):
                if n:
                    sp.wait_ge(layer_done, 2)
                sp.wait_ge(*after("ff", 4))
                for m in range(2):
                    sp.dma_start(bv[64 * m:64 * m + 64], v_src.rearrange("(a j m e) -> a m j e", a=1, j=2, m=2)[:, m]
                                 .to_broadcast([64, 2, P])).then_inc(bias_loaded, 16)
                sp.dma_start(bo, across(o_src)).then_inc(bias_loaded, 16)

            for e in staged_order[before_x:]:
                if LAYERS > 1 and e == W["w0", "o"]:
                    load_bias(0, a["L0_attn_bv"], a["L0_attn_bo"])
                if LAYERS > 3 and e == W["win", "Wqj"]:
                    sp.wait_ge(layer_done, 1)
                    for b2 in range(2):
                        src = a["itok_BxS_0_7"].rearrange("(a t c) s -> c a t s", a=1, c=2)[b2]
                        sp.dma_start(ids_rows[64 * b2:64 * b2 + 64], src.to_broadcast([64, T, S])).then_inc(ids_loaded, 16)
                    with nc.allow_non_contiguous_dma(reason="a pointer per token"):
                        sp.dma_start(ptr[:, 0:T], a["itok_BxS_0_4092"].rearrange("(t c) s -> (c s) t", c=2))\
                            .then_inc(ids_loaded, 16)
                if LAYERS > 4 and e == W["w1n", "o"]:
                    load_bias(1, a["L1_attn_b_qkv"][2 * D:3 * D], a["L1_attn_b_out"])
                stage_block(e)
            if LAYERS > 5:
                sp.wait_ge(layer_done, 5)
                sp.dma_start(lnw, across(a["L1_ffn_ln_w"])).then_inc(bias_loaded, 16)
                sp.dma_start(lnb, across(a["L1_ffn_ln_b"])).then_inc(bias_loaded, 16)
            sp.wait_ge(layer_done, LAYERS)
            for t in range(T):
                sp.dma_start(out[2 * t:2 * t + 2].rearrange("b s d -> (b s) d"), X[:, t]).then_inc(out_stored, 16)
            sp.wait_ge(out_stored, 16 * T)

        @block.gpsimd
        def _(pool):
            consts = [0]

            def const(ins, wait=False):
                consts[0] += 1
                ins.then_inc(const_ready, 1)
                if wait:
                    pool.wait_ge(const_ready, consts[0])

            const(pool.memset(ident[:], 0.0), wait=True)
            const(pool.affine_select(out=ident[:], in_=ident[:], compare_op=ALU.not_equal, fill=1.0, base=0,
                                     pattern=[[-1, P]], channel_multiplier=1), wait=True)
            const(pool.tensor_copy(identb[:], ident[:]))
            const(pool.memset(ones[:], 1.0))
            const(pool.memset(small[:, 153:154], 0.0))
            const(pool.memset(causal[:], 0.0), wait=True)
            for b2 in range(2):
                part = causal[64 * b2:64 * b2 + 64]
                const(pool.affine_select(out=part, in_=part, compare_op=ALU.is_ge, fill=NEG, base=0,
                                         pattern=[[-1, S]], channel_multiplier=1), wait=True)
                const(pool.iota(tile_base[64 * b2:64 * b2 + 64], pattern=[[2 * SCTX, T]], base=b2 * SCTX,
                                channel_multiplier=0), wait=True)
            const(pool.iota(key_no[:], pattern=[[1, S]], base=0, channel_multiplier=0))
            assert consts[0] == CONSTS

            def split(e):
                i = staged_order.index(e)
                src = stage[:, i % STAGED]
                pool.wait_ge(stage_loaded[i % STAGED], 16 * (i // STAGED + 1))
                wait_slot(pool, e)
                hi, lo = ring_hi[:, e % RING], ring_lo[:, e % RING]
                if entries[e][0] == "n":
                    pool.tensor_tensor(hi, src, small[:, 153:154].unsqueeze(2).to_broadcast([P, KC, D]), ALU.add)\
                        .then_inc(pool_part, 1)
                    parts[0] += 1
                    pool.wait_ge(pool_part, parts[0])
                    pool.tensor_tensor(lo, src, hi, ALU.subtract).then_inc(pool_split, 1)
                else:
                    w = 0 if e < W["proj", 0] else 1
                    if e == W["fc", 0]:
                        pool.wait_ge(thr_ready, 1)
                    pool.tensor_scalar(hi, src, thr[:, w:w + 1], None, ALU.is_gt).then_inc(pool_part, 1)
                    pool.tensor_scalar(lo, src, nthr[:, w:w + 1], None, ALU.is_lt).then_inc(pool_part, 1)
                    parts[0] += 2
                    pool.wait_ge(pool_part, parts[0])
                    pool.tensor_tensor(hi, hi, lo, ALU.subtract).then_inc(pool_split, 1)

            parts = [0]
            ctx_rows = a["ctx_1024"].rearrange("b s d -> (b s) d")

            def gather(h):
                for u in range(HT):
                    for w in range(3):
                        idx = row_of.rearrange("p (t w) -> p t w", w=4)[:, 4 * h + u, w:w + 1]
                        pool.indirect_dma_start(win[:, u, w, :], None, ctx_rows,
                                                bass.IndirectOffsetOnAxis(ap=idx.bitcast(mybir.dt.uint32), axis=0))\
                            .then_inc(win_loaded, 16)

            def window_gathers():
                pool.wait_ge(rows_ready, 1)
                gather(0)
                pool.wait_ge(comb_ready, 2 * HT)
                gather(1)

            for e in staged_order:
                if LAYERS > 3 and e == W["win", "Wvi"] + 1:
                    window_gathers()
                split(e)
            if LAYERS == 4:
                window_gathers()
            if LAYERS > 5:
                pool.wait_ge(bias_loaded, 16 * 8)
                with pool.Fori(0, 2) as h:
                    for u in range(HT):
                        x = hid[:, u % 2]
                        pool.wait_ge(hid_norm, h * HT + u + 1)
                        pool.tensor_tensor(x, x, lnw, ALU.mult).then_inc(hid_scaled, 1)
                        pool.wait_ge(hid_scaled, h * HT + u + 1)
                        pool.tensor_tensor(x, x, lnb, ALU.add).then_inc(hid_ready, 1)

        @block.tensor
        def _(pe):
            pe.wait_ge(const_ready, CONSTS)

            def product(bank, terms):
                passes = []
                for (lh, ll), (rh, rl) in terms:
                    passes.append((lh, rh))
                    if rl is not None:
                        passes.append((lh, rl))
                    if ll is not None:
                        passes.append((ll, rh))
                for n, (l, r) in enumerate(passes):
                    ins = pe.matmul(bank, l, r, start=n == 0, stop=n == len(passes) - 1)
                return ins

            def cut(pair, f):
                return tuple(None if x is None else f(x) for x in pair)

            def turn_tile(bank, tile):
                for k in range(KC):
                    ins = pe.transpose(bank[:, k * P:(k + 1) * P], tile[:, k * P:(k + 1) * P], ident[:])
                return ins

            def turn_y(g, name, i):
                base, n = y_base[name]
                for u in range(HT):
                    bank = g.open()
                    pe.wait_ge(y_ready, base + i * n + u + 1)
                    turn_tile(bank, ybuf[:, u % 2]).then_inc(group_ready, 1)

            def turn_block(g, pair):
                for x in pair:
                    for z in range(2):
                        bank = g.open().bitcast(BF16).rearrange("p (c n) -> p c n", c=2)
                        for c2 in range(2):
                            for c in range(KC):
                                ins = pe.transpose(bank[:, c2, c * P:(c + 1) * P],
                                                   x[:, c, (2 * z + c2) * P:(2 * z + c2 + 1) * P], identb[:])
                        ins.then_inc(group_ready, 1)

            with pe.Fori(0, 2) as h:
                g = Pass(pe, "ln0", h)
                turn_y(g, "ln0", h)
            Pass(pe, "q").all_free()
            for i in range(2):
                wait_split(pe, ("q", i))
                w = w_of(("q", i))
                with pe.Fori(0, 2) as mp:
                    g = Pass(pe, "q", 2 * i + mp)
                    for mm in range(2):
                        for hf in range(2):
                            bank = g.open()
                            product(bank, [(cut(w, lambda x: x[:, k, bass.ds(mp * 256 + mm * P, P)]),
                                            cut(yT, lambda x: x[:, k, hf * 512:(hf + 1) * 512])) for k in range(KC)])\
                                .then_inc(group_ready, 1)

            pe.wait_ge(flag_part, 1)
            Pass(pe, "ff").all_free()
            pe.matmul(SHARED[:, 0:1], ones[0:B, :], small[0:B, 152:153], start=True, stop=True).then_inc(XN["shared_ready"], 1)

            def attend(nkt):
                v = xmap(nkt)
                W_, ch, ns = v["groups"], v["chunks"], v["shared_n"]
                with pe.Fori(0, B) as b:
                    shared = [0]

                    def open_shared():
                        pe.wait_ge(XN["shared_free"], b * ns + shared[0] + 1)
                        shared[0] += 1
                        return SHARED

                    if v["full"]:
                        pe.wait_ge(XN["p_act"], b * (W_ // 2))
                        pe.wait_ge(XN["p_dve"], b * (W_ // 2))
                    for c, tiles in enumerate(v["tiles_of"]):
                        n = len(tiles)
                        for kt in tiles:
                            pe.wait_ge(XN["ctx_lo"], b * nkt + max(kt - 1, 0))
                            pe.wait_ge(XN["ctx_norm"], b * nkt + kt + 1)
                            turn_tile(psum[:, 6 + kt % 2], v["ctx"][:, kt % 4]).then_inc(XN["ctx_turned"], 1)
                        bank = open_shared()
                        settle(pe)
                        pe.matmul(bank[:, 0:n * P], identb[0:B, bass.ds(b, 1)].to_broadcast([B, P]),
                                  maskadd[0:B, v["m0"] + tiles[0] * P:v["m0"] + tiles[0] * P + n * P],
                                  start=True, stop=True).then_inc(XN["shared_ready"], 1)
                        pe.wait_ge(XN["ctx_lo"], b * nkt + tiles[0] + n)
                        bank = open_shared()
                        cT = (v["cT_hi"], v["cT_lo"])
                        product(bank[:, 0:n * P], [(cut(wk, lambda x: x[:, k, :]), cut(cT, lambda x: x[:, k, 0:n * P]))
                                                   for k in range(KC)]).then_inc(XN["shared_ready"], 1)
                        if c == 0:
                            pe.wait_ge(XN["o_norm"], b)
                        else:
                            pe.wait_ge(XN["v_copied"], b * ch + c)
                        for u in range(n):
                            ins = product(O_BANK[:, u * XD:(u + 1) * XD],
                                          [(cut(cT, lambda x: x[:, k, u * P:(u + 1) * P]), cut(wv, lambda x: x[:, k, :]))
                                           for k in range(KC)])
                        ins.then_inc(XN["v_mm"], 1)

                    pe.wait_ge(XN["shared_free"], b * ns + 2 * ch + 1)

                    def scores(j):
                        pe.wait_ge(XN["s_max"], b * 8 + (j if v["full"] else max(j - 1, 0)))
                        S = v["S"](j)
                        q = Q[:, bass.ds(b, 1), 2 * j:2 * j + 2, :].rearrange("p b h s -> p (b h s)")
                        for c, tiles in enumerate(v["tiles_of"]):
                            c0, c1 = tiles[0] * P, (tiles[-1] + 1) * P
                            pe.matmul(S[:, c0:c1], q, v["KA"][:, c0:c1], start=True, stop=False)
                            ins = pe.matmul(S[:, c0:c1], q, v["KB"][:, c0:c1], start=False, stop=True)
                        ins.then_inc(XN["s_mm"], 1)

                    def turn_p(j, i):
                        w = j * ch + i
                        if i == 0:
                            pe.wait_ge(XN["exp"], b * 8 + j + 1)
                        pe.wait_ge(XN["p_dve" if w % 2 else "p_act"], b * (W_ // 2) + w // 2)
                        bank = v["PTbank"](w)
                        for n, kt in enumerate(v["tiles_of"][i]):
                            ins = pe.transpose(bank[:, n * P:(n + 1) * P],
                                               v["P"][:, j % v["P"].shape[1], kt * P:(kt + 1) * P], ident[:])
                        ins.then_inc(XN["p_turned"], 1)

                    def values(j, i):
                        w = j * ch + i
                        if w == 0:
                            pe.wait_ge(XN["v_copied"], (b + 1) * ch)
                        pe.wait_ge(XN["p_dve" if w % 2 else "p_act"], b * (W_ // 2) + w // 2 + 1)
                        for n, kt in enumerate(v["tiles_of"][i]):
                            ins = pe.matmul(O_BANK[:, j * XD:(j + 1) * XD], v["PT"][:, w % 2, n, :], v["V"][:, kt, :],
                                            start=kt == 0, stop=kt == nkt - 1)
                        ins.then_inc(XN["pv"], 1)

                    scores(0)
                    before = None
                    for j in range(8):
                        if j + 1 < 8 and not v["full"]:
                            scores(j + 1)
                        for i in range(ch):
                            turn_p(j, i)
                            if before:
                                values(*before)
                            before = (j, i)
                        if j + 1 < 8 and v["full"]:
                            scores(j + 1)
                    values(*before)
                    pe.wait_ge(XN["o_norm"], b + 1)
                    for half in range(2):
                        bank = open_shared()
                        settle(pe)
                        for jj in range(4):
                            ins = pe.transpose(bank[0:XD, jj * P:(jj + 1) * P], v["O"][:, 4 * half + jj, :], ident[:])
                        ins.then_inc(XN["shared_ready"], 1)

            pe.wait_ge(flag_ready, 1)
            head_rows_used = pe.value_load(flag[0:1, 0:1], min_val=0, max_val=1)
            with pe.If(head_rows_used > 0):
                attend(FULL_TILES)
            with pe.If(head_rows_used < 1):
                attend(TAIL_TILES)

            pe.wait_ge(x_attended, 1)
            for i in range(4):
                wait_split(pe, ("ffg", i))
                wa, wg = w_of(("ffa", i)), w_of(("ffg", i))
                with pe.Fori(0, 4) as m:
                    g = Pass(pe, "ff", 4 * i + m)
                    for hf in range(2):
                        for w in (wa, wg):
                            bank = g.open()
                            product(bank, [(cut(w, lambda x: x[:, k, bass.ds(m * P, P)]),
                                            cut(yT, lambda x: x[:, k, hf * 512:(hf + 1) * 512])) for k in range(KC)])\
                                .then_inc(group_ready, 1)
            pe.wait_ge(prod_lo, 32)
            wait_split(pe, ("ff2", 3))
            with pe.Fori(0, 2) as h:
                g = Pass(pe, "xout", h)
                for u in range(HT):
                    bank = g.open()
                    terms = []
                    for c in range(24):
                        src, w = (oT, w_of(("xo", c // 4))) if c < 8 else (ffT, w_of(("ff2", (c - 8) // 4)))
                        cc = c if c < 8 else c - 8
                        terms.append((cut(src, lambda x: x[:, cc, bass.ds(h * 512 + u * P, P)]),
                                      cut(w, lambda x: x[:, c % 4, :])))
                    product(bank, terms).then_inc(group_ready, 1)
            if LAYERS > 5:
                g = Pass(pe, "gamma")
                bank = g.open()
                pe.wait_ge(gamma_part, 1)
                pe.matmul(bank[:, 0:2], ones[:], gtot, start=True, stop=True).then_inc(group_ready, 1)

            def attention(n, name):
                wq, wk_, wv_ = (w_of((f"w{n}", x)) for x in "qkv")
                wo = woT if n else w_of(("w0", "o"))
                if not n:
                    wait_split(pe, ("w0", "o"))
                with pe.Fori(0, 2) as h:
                    g = Pass(pe, name, h)
                    turn_y(g, name, h)
                    g.wait_done(3)
                    for w in (wq, wk_):
                        for m in range(KC):
                            bank = g.open()
                            product(bank, [(cut(w, lambda x: x[:, k, m * P:(m + 1) * P]), cut(yh, lambda x: x[:, k, :]))
                                           for k in range(KC)]).then_inc(group_ready, 1)
                    wv4 = cut(wv_, lambda x: x.rearrange("p k (j m e) -> p k j m e", j=2, m=2))
                    for u in range(HT):
                        bank = g.open()
                        for m in range(2):
                            for b2 in range(2):
                                t0 = u * P + b2 * S
                                ins = product(bank[64 * m:64 * m + 64, b2 * 256:(b2 + 1) * 256],
                                              [(cut(yh, lambda x: x[:, k, t0:t0 + S]), cut(wv4, lambda x: x[:, k, :, m, :]))
                                               for k in range(KC)])
                        ins.then_inc(group_ready, 1)

                    def scores(u):
                        for r in range(4):
                            bank = g.open()
                            if u == 0 and r == 0:
                                g.wait_done(11)
                            for m in range(4):
                                for b2 in range(2):
                                    t0 = u * P + b2 * S
                                    f = lambda x: x[32 * r:32 * r + 32, m, t0:t0 + S]
                                    ins = product(bank[64 * b2:64 * b2 + 64, m * S:(m + 1) * S], [(cut(qh, f), cut(kh, f))])
                            ins.then_inc(group_ready, 1)

                    scores(0)
                    for u in range(HT):
                        if u + 1 < HT:
                            scores(u + 1)
                        pe.wait_ge(p_exp, (n * 2 + h) * HT + u + 1)
                        for j in range(2):
                            bank = g.open()
                            for r in range(4):
                                ins = pe.transpose(bank[:, r * P:(r + 1) * P],
                                                   prob[:, u % 2, r, 2 * j:2 * j + 2, :].rearrange("p m s -> p (m s)"), ident[:])
                            ins.then_inc(group_ready, 1)
                        pt = g.at - 1
                        bank = g.open()
                        if u == 0:
                            pe.wait_ge(v_done, (n * 2 + h) * HT + HT)
                        g.wait_done(pt)
                        for j in range(2):
                            for r in range(4):
                                for b2 in range(2):
                                    o = bank.rearrange("p (j m r d) -> p j m r d", j=2, m=2, r=4)[64 * b2:64 * b2 + 64, j, :, r, :]
                                    ins = product(o, [(cut(pT, lambda x: x[:, u % 2, 4 * j + r, b2 * S:(b2 + 1) * S]),
                                                       cut(vb, lambda x: x[:, 2 * u + b2, 4 * j + r]))])
                        ins.then_inc(group_ready, 1)
                        o_group = g.at - 1
                        bank = g.open()
                        g.wait_done(o_group)
                        turn_tile(bank, ybuf[:, u % 2]).then_inc(group_ready, 1)
                    last = g.at - 1
                    for u in range(HT):
                        bank = g.open()
                        if u == 0:
                            g.wait_done(last)
                        product(bank, [(cut(ah, lambda x: x[:, k, u * P:(u + 1) * P]), cut(wo, lambda x: x[:, k, :]))
                                       for k in range(KC)]).then_inc(group_ready, 1)

            if LAYERS > 1:
                attention(0, "attn0")

            if LAYERS > 2:
                g = Pass(pe, "turn_mix")
                for n in "rkv":
                    wait_split(pe, ("mixn", n))
                    turn_block(g, w_of(("mixn", n)))
                wr, wk2, wv2 = (w_of(("mix", n)) for n in "rkv")
                with pe.Fori(0, 2) as h:
                    g = Pass(pe, "mix", h)
                    turn_y(g, "mix", h)
                    for u in range(HT):
                        bank = g.open()
                        if u == 0:
                            pe.wait_ge(mix_lo, 8 * h + 4)
                        product(bank, [(cut(mixT[0], lambda x: x[:, k, u * P:(u + 1) * P]), cut(wr, lambda x: x[:, k, :]))
                                       for k in range(KC)]).then_inc(group_ready, 1)
                    pe.wait_ge(mix_lo, 8 * h + 8)
                    for m in range(KC):
                        bank = g.open()
                        product(bank, [(cut(wk2, lambda x: x[:, k, m * P:(m + 1) * P]), cut(mixT[1], lambda x: x[:, k, :]))
                                       for k in range(KC)]).then_inc(group_ready, 1)
                    for u in range(HT):
                        bank = g.open()
                        if u == 0:
                            pe.wait_ge(relu_lo, 4 * h + 4)
                        product(bank, [(cut(kact, lambda x: x[:, k, u * P:(u + 1) * P]), cut(wv2, lambda x: x[:, k, :]))
                                       for k in range(KC)]).then_inc(group_ready, 1)

            if LAYERS > 3:
                g = Pass(pe, "fold")

                def weights_product(left, right):
                    for m in range(KC):
                        bank = g.open()
                        product(bank, [(cut(left, lambda x: x[:, k, m * P:(m + 1) * P]), cut(right, lambda x: x[:, k, :]))
                                       for k in range(KC)]).then_inc(group_ready, 1)

                for s in "ji":
                    wait_split(pe, ("win", "Wk" + s))
                    weights_product(w_of(("win", "Wq" + s)), w_of(("win", "Wk" + s)))
                wait_split(pe, ("win", "Wout"))
                turn_block(g, w_of(("win", "Wout")))
                g.wait_done(10)
                g.wait_done(11)
                for s in "ji":
                    wait_split(pe, ("win", "Wv" + s))
                    weights_product(w_of(("win", "Wv" + s)), w_of(("win", "WoutT")))
                with pe.Fori(0, 2) as h:
                    g = Pass(pe, "window", h)
                    turn_y(g, "window", h)
                    for u in range(HT):
                        for s in range(2):
                            bank = g.open()
                            g.wait_done(u)
                            product(bank, [(cut(yh, lambda x: x[:, k, u * P:(u + 1) * P]), cut(fold[s], lambda x: x[:, k, :]))
                                           for k in range(KC)]).then_inc(group_ready, 1)
                    for n in range(2 * HT):
                        bank = g.open()
                        pe.wait_ge(comb_ready, h * 2 * HT + n + 1)
                        turn_tile(bank, comb[:, n % 2]).then_inc(group_ready, 1)
                    last = g.at - 1
                    for u in range(HT):
                        bank = g.open()
                        if u == 0:
                            g.wait_done(last)
                        product(bank, [(cut(src, lambda x: x[:, k, u * P:(u + 1) * P]), cut(fold[2 + s], lambda x: x[:, k, :]))
                                       for s, src in enumerate((yh, y2)) for k in range(KC)]).then_inc(group_ready, 1)

            if LAYERS > 4:
                g = Pass(pe, "turn_w1")
                for n in "qkvo":
                    wait_split(pe, ("w1n", n))
                    turn_block(g, w_of(("w1n", n)))
                attention(1, "attn1")

            if LAYERS > 5:
                g = Pass(pe, "turn_mlp")
                for kind in ("fc", "proj"):
                    for i in range(4):
                        wait_split(pe, (kind, i))
                        turn_block(g, w_of((kind, i))[:1])
                with pe.Fori(0, 2) as h:
                    g = Pass(pe, "mlp", h)
                    turn_y(g, "mlp", h)

                    def hidden(u):
                        for n in range(4):
                            bank = g.open()
                            if u == 0 and n == 0:
                                g.wait_done(3)
                            product(bank, [(cut(yh, lambda x: x[:, k, u * P:(u + 1) * P]), (fcT[:, n, k, :], None))
                                           for k in range(KC)]).then_inc(group_ready, 1)

                    hidden(0)
                    for u in range(HT):
                        if u + 1 < HT:
                            hidden(u + 1)
                        pe.wait_ge(hid_ready, h * HT + u + 1)
                        for n in range(4):
                            turn_tile(g.open(), hid[:, u % 2, n * 512:(n + 1) * 512]).then_inc(group_ready, 1)
                        last = g.at - 1
                        bank = g.open()
                        g.wait_done(last)
                        product(bank, [(cut(hT[u % 2], lambda x: x[:, c, :]), (projT[:, c, :], None)) for c in range(FF // P)])\
                            .then_inc(group_ready, 1)

        @block.scalar
        def _(act):
            for _ in range(ACT_CREDIT):
                act.drain().then_inc(act_freed, 1)
            act.wait_ge(const_ready, CONSTS)

            def copy_hi(dst, bank, g_=None, **kw):
                return act.activation(dst, bank, ACT.Copy, **kw)

            def quad(bank):
                return bank.rearrange("p (k n) -> p k n", k=KC)

            def hi_of_tile(g, i, dst):
                copy_hi(dst, quad(g.take(i))).then_inc(act_hi, 1)

            def turned_half(g):
                for u in range(HT):
                    hi_of_tile(g, u, yh[0][:, :, u * P:(u + 1) * P])

            def copy_turned(g, i, dst):
                act.activation(dst, g.take(i).bitcast(BF16).rearrange("p (c n) -> p c n", c=2), ACT.Copy).then_inc(act_freed, 1)

            with act.Fori(0, 2) as h:
                g = Pass(act, "ln0", h)
                for u in range(HT):
                    hi_of_tile(g, u, yT[0][:, :, bass.ds(h * 512 + u * P, P)])
            for i in range(2):
                with act.Fori(0, 2) as mp:
                    g = Pass(act, "q", 2 * i + mp)
                    for mm in range(2):
                        for hf in range(2):
                            bank = g.take(2 * mm + hf)
                            for h2 in range(2):
                                dst = Q[0:64, hf * 8:hf * 8 + 8, bass.ds(i * 8 + mp * 4 + mm * 2 + h2, 1), :]
                                ins = act.activation(dst.rearrange("p b h s -> p b (h s)"),
                                                     bank[64 * h2:64 * h2 + 64].rearrange("p (b s) -> p b s", b=8),
                                                     ACT.Copy, scale=XD ** -0.5)
                            ins.then_inc(act_hi, 1)

            def attend(nkt):
                v = xmap(nkt)
                W_, ch, ns = v["groups"], v["chunks"], v["shared_n"]
                with act.Fori(0, B) as b:
                    if LAYERS > 5:
                        act.wait_ge(XN["g_loaded"], 32 * (b + 1))
                        for w in range(2):
                            ins = act.activation(ybuf[:, w], ybuf[:, w], ACT.Abs, accum_out=gsum[:, w, bass.ds(b, 1)])
                        ins.then_inc(XN["g_summed"], 1)
                    for c, tiles in enumerate(v["tiles_of"]):
                        n = len(tiles)
                        for kt in tiles:
                            act.wait_ge(XN["ctx_turned"], b * nkt + kt + 1)
                            u = kt % 4
                            copy_hi(v["cT_hi"][:, :, u * P:(u + 1) * P], quad(psum[:, 6 + kt % 2])).then_inc(XN["ctx_hi"], 1)
                        cols_ = slice(tiles[0] * P, (tiles[-1] + 1) * P)
                        act.wait_ge(XN["shared_ready"], b * ns + 2 * c + 2)
                        copy_hi(v["mb"][:, cols_], SHARED[:, 0:n * P]).then_inc(XN["shared_free"], 1)
                        act.wait_ge(XN["shared_ready"], b * ns + 2 * c + 3)
                        copy_hi(v["KA"][:, cols_], SHARED[:, 0:n * P]).then_inc(XN["k_hi"], 1)
                        act.wait_ge(XN["v_mm"], b * ch + c + 1)
                        copy_hi(v["V"][:, tiles[0]:tiles[-1] + 1, :],
                                O_BANK[:, 0:n * XD].rearrange("p (t e) -> p t e", e=XD)).then_inc(XN["v_copied"], 1)

                    def exp(j):
                        p = v["P"][:, j % v["P"].shape[1], :]
                        act.wait_ge(XN["s_max"], b * 8 + j + 1)
                        act.activation(p, p, ACT.Exp, bias=xq_neg[:, j:j + 1], accum_out=xq_sum[:, j:j + 1])\
                            .then_inc(XN["exp"], 1)

                    def copies(j):
                        for i in range(ch):
                            w = j * ch + i
                            if w % 2 == 0:
                                n = len(v["tiles_of"][i])
                                act.wait_ge(XN["p_turned"], b * W_ + w + 1)
                                act.wait_ge(XN["pv"], b * W_ + max(w - 1, 0))
                                copy_hi(v["PT"][:, 0, 0:n, :], v["PTbank"](w)[:, 0:n * P].rearrange("p (t q) -> p t q", q=P))\
                                    .then_inc(XN["p_act"], 1)

                    exp(0)
                    for j in range(8):
                        if j + 1 < 8 and not v["full"]:
                            exp(j + 1)
                        copies(j)
                        if j + 1 < 8 and v["full"]:
                            exp(j + 1)
                    for half in range(2):
                        act.wait_ge(XN["shared_ready"], b * ns + 2 * ch + half + 2)
                        bank = SHARED[0:XD].rearrange("p (j m s) -> p j m s", j=4, m=2)
                        for h2 in range(2):
                            ins = copy_hi(oT[0][64 * h2:64 * h2 + 64, 4 * half:4 * half + 4, bass.ds(b * S, S)], bank[:, :, h2, :])
                        ins.then_inc(XN["ot_hi"], 1)

            act.wait_ge(flag_ready, 1)
            head_rows_used = act.value_load(flag[0:1, 0:1], min_val=0, max_val=1)
            with act.If(head_rows_used > 0):
                attend(FULL_TILES)
            with act.If(head_rows_used < 1):
                attend(TAIL_TILES)

            for i in range(4):
                with act.Fori(0, 4) as m:
                    g = Pass(act, "ff", 4 * i + m)
                    for hf in range(2):
                        act.activation(ybuf[:, hf], g.take(2 * hf + 1), ACT.Silu).then_inc(act_freed, 1)
                    for hf in range(2):
                        g.wait_done(2 * hf)
                        act.activation(ffT[0][:, bass.ds(4 * i + m, 1), hf * 512:(hf + 1) * 512].rearrange("p a n -> p (a n)"),
                                       prod[:, hf], ACT.Copy).then_inc(prod_hi, 1)

            def attention(n, name):
                bq, bk = (C_BQ1, C_BK1) if n else (C_BQ0, C_BK0)
                with act.Fori(0, 2) as h:
                    g = Pass(act, name, h)
                    turned_half(g)
                    for x, (dst, bias) in enumerate(((qh, bq), (kh, bk))):
                        for m in range(KC):
                            act.activation(dst[0][:, m, :], g.take(4 + 4 * x + m), ACT.Identity,
                                           bias=cols[:, bias + m:bias + m + 1]).then_inc(act_hi, 1)
                    for u in range(HT):
                        g.wait_done(12 + u)
                        for m in range(2):
                            rows_ = slice(64 * m, 64 * m + 64)
                            ins = act.activation(vb[0][rows_, 2 * u:2 * u + 2, :, m, :],
                                                 vf[rows_, u % 2].rearrange("p (b g e) -> p b g e", b=2, g=8), ACT.Copy)
                        ins.then_inc(v_hi, 1)

                    def exp(u):
                        act.wait_ge(p_max, (n * 2 + h) * HT + u + 1)
                        p = prob[:, u % 2].rearrange("p r m s -> p (r m s)")
                        act.activation(p, p, ACT.Exp).then_inc(p_exp, 1)

                    at = 16 + 4
                    exp(0)
                    for u in range(HT):
                        if u + 1 < HT:
                            exp(u + 1)
                            at += 4
                        for j in range(2):
                            hi_of_tile(g, at + j, pT[0][:, u % 2, 4 * j:4 * j + 4, :])
                        hi_of_tile(g, at + 3, ah[0][:, :, u * P:(u + 1) * P])
                        at += 4

            if LAYERS > 1:
                attention(0, "attn0")

            if LAYERS > 2:
                g = Pass(act, "turn_mix")
                for i, n in enumerate("rkv"):
                    wait_slot(act, W["mix", n])
                    for x in range(2):
                        copy_turned(g, 4 * i + 2 * x, w_of(("mix", n))[x][:, 0:2, :])
                act.wait_ge(om_ready, 1)
                with act.Fori(0, 2) as h:
                    g = Pass(act, "mix", h)
                    for u in range(HT):
                        act.activation(zp[:, :, 2 * u:2 * u + 2, 1:], g.take(u).rearrange("p (k b s) -> p k b s", k=KC, b=2),
                                       ACT.Copy).then_inc(act_freed, 1)
                    g.wait_done(HT - 1)

                    def previous_part(n):
                        act.activation(mix_t[:, n % 2].rearrange("p (b s) -> p b s", b=8), zp[:, n % 4, :, 0:S], ACT.Copy,
                                       scale=cols[:, (C_OMR, C_OMK)[n // 4] + n % 4:(C_OMR, C_OMK)[n // 4] + n % 4 + 1])\
                            .then_inc(mix_a, 1)

                    previous_part(0)
                    for n in range(8):
                        if n < 7:
                            previous_part(n + 1)
                        act.wait_ge(mix_b, 8 * h + n + 1)
                        act.activation(mixT[n // 4][0][:, n % 4, :], mix_f[:, n % 2], ACT.Copy).then_inc(mix_hi, 1)
                    for u in range(HT):
                        act.activation(recept[:, u], g.take(4 + u), ACT.Sigmoid).then_inc(act_freed, 1)
                    for m in range(KC):
                        g.wait_done(8 + m)
                        if m >= 2:
                            act.wait_ge(relu_lo, 4 * h + m - 1)
                        act.activation(relu2[:, m % 2], relu[:, m % 2], ACT.Square).then_inc(relu_sq, 1)
                        act.activation(kact[0][:, m, :], relu[:, m % 2], ACT.Square).then_inc(relu_hi, 1)

            if LAYERS > 3:
                g = Pass(act, "fold")

                def folded(first, pair):
                    for m in range(KC):
                        copy_hi(pair[0][:, m, :], g.take(first + m)).then_inc(act_hi, 1)

                folded(0, fold[0])
                folded(4, fold[1])
                wait_slot(act, W["win", "WoutT"])
                for x in range(2):
                    copy_turned(g, 8 + 2 * x, w_of(("win", "WoutT"))[x][:, 0:2, :])
                folded(12, fold[2])
                folded(16, fold[3])
                act.wait_ge(logit, 1)
                act.activation(council[:, 4:6], council[:, 2:4], ACT.Exp).then_inc(e_ready, 1)
                with act.Fori(0, 2) as h:
                    g = Pass(act, "window", h)
                    turned_half(g)
                    act.wait_ge(logit, h + 2)
                    act.activation(sc[:, SC_E:SC_E + 6, :], sc[:, SC_E:SC_E + 6, :], ACT.Exp).then_inc(e_ready, 1)
                    for n in range(2 * HT):
                        u = n // 2
                        hi_of_tile(g, 12 + n, (yh, y2)[n % 2][0][:, :, u * P:(u + 1) * P])

            if LAYERS > 4:
                g = Pass(act, "turn_w1")
                for i, n in enumerate("qkvo"):
                    dst = woT
                    if n != "o":
                        wait_slot(act, W["w1", n])
                        dst = w_of(("w1", n))
                    for x in range(2):
                        copy_turned(g, 4 * i + 2 * x, dst[x][:, 0:2, :])
                attention(1, "attn1")

            if LAYERS > 5:
                g = Pass(act, "turn_mlp")
                for i in range(4):
                    copy_turned(g, 2 * i, fcT[:, i, 0:2, :])
                for i in range(4):
                    copy_turned(g, 8 + 2 * i, projT[:, 4 * i:4 * i + 2, :])
                with act.Fori(0, 2) as h:
                    g = Pass(act, "mlp", h)
                    turned_half(g)
                    at = 4

                    def gelus(u, at):
                        for n in range(4):
                            act.activation(hid[:, u % 2, n * 512:(n + 1) * 512], g.take(at + n), ACT.Gelu).then_inc(act_freed, 1)

                    gelus(0, at)
                    at += 4
                    for u in range(HT):
                        if u + 1 < HT:
                            gelus(u + 1, at)
                            at += 4
                        for n in range(4):
                            hi_of_tile(g, at + n, hT[u % 2][0][:, 4 * n:4 * n + 4, :])
                        at += 5

        @block.vector
        def _(dve):
            main = Chain(dve, step)
            done = {"step": 0}

            def piece(i=0, passes=1, key=None):
                n = LINKS.get(key, 0)
                c = Chain(dve, step, done["step"], i, n if passes > 1 else 0)
                c.passes, c.key = passes, key
                return c

            def close(c):
                if c.passes > 1:
                    assert c.n == LINKS.get(c.key), f"LINKS[{c.key!r}] = {c.n}"
                done["step"] += c.n * c.passes

            def finished(semaphore):
                settle(dve)
                dve.drain().then_inc(semaphore, 1)

            def xt(i, u):
                return X[:, bass.ds(i * HT + u, 1), :].rearrange("p a n -> p (a n)")

            def quad(x):
                return x.rearrange("p (k n) -> p k n", k=KC)

            def rstd(c, n):
                v, y, t = (nw[:, i, 0:n] for i in range(3))
                c.link(dve.tensor_scalar(v, mv[:, 0:n, 1], LN_EPS, None, ALU.add))
                c.link(dve.tensor_scalar(y.bitcast(I32), v.bitcast(I32), 1, None, ALU.arith_shift_right))
                c.link(dve.tensor_scalar(y.bitcast(I32), y.bitcast(I32), -1.0, RSQRT_SEED, ALU.mult, ALU.add))
                for _ in range(3):
                    c.link(dve.tensor_tensor(t, v, y, ALU.mult))
                    c.link(dve.tensor_tensor(t, t, y, ALU.mult))
                    c.link(dve.tensor_scalar(t, t, -0.5, 1.5, ALU.mult, ALU.add))
                    c.link(dve.tensor_tensor(y, y, t, ALU.mult))

            def moments(c, tiles):
                for u, x in enumerate(tiles):
                    ins = dve.bn_stats(stats[:, u, :], x)
                c.link(ins)
                settle(dve)
                for u in range(len(tiles)):
                    ins = dve.bn_aggr(mv[:, u, :], stats[:, u, :])
                c.link(ins)
                rstd(c, len(tiles))

            def normed(dst, src, u):
                return dve.tensor_scalar(dst, src, mv[:, u, 0:1], nw[:, 1, u:u + 1], ALU.subtract, ALU.mult)

            def lo_of_tile(g, i, dst, hi):
                bank = g.wait_hi(i)
                dve.tensor_tensor(dst, quad(bank), hi, ALU.subtract).then_inc(dve_freed, 1)

            def norm_half(c, g, i, last=None):
                def low(u):
                    sl = slice(u * P, (u + 1) * P)
                    lo_of_tile(g, u, yh[1][:, :, sl], yh[0][:, :, sl])
                moments(c, [xt(i, u) for u in range(HT)])
                for u in range(HT):
                    if u >= 2:
                        g.take(u - 2)
                    normed(ybuf[:, u % 2], xt(i, u), u).then_inc(y_ready, 1)
                    if u >= 1:
                        low(u - 1)
                low(HT - 1)

            def copy_turned(g, i, dst):
                dve.tensor_copy(dst, g.take(i).bitcast(BF16).rearrange("p (c n) -> p c n", c=2)).then_inc(dve_freed, 1)

            dve.wait_ge(const_ready, CONSTS)
            dve.wait_ge(x_loaded, 16 * T)
            dve.wait_ge(gamma_loaded, 16)
            with dve.Fori(0, 2) as h:
                c = piece(h, 2, "ln0")
                g = Pass(dve, "ln0", h)
                moments(c, [xt(h, u) for u in range(HT)])
                for u in range(HT):
                    ins = normed(x0[:, u], xt(h, u), u)
                c.link(ins)
                moments(c, [x0[:, u] for u in range(HT)])
                for u in range(HT):
                    ins = normed(x0[:, u], x0[:, u], u)
                c.link(ins)

                def low(u):
                    sl = bass.ds(h * 512 + u * P, P)
                    lo_of_tile(g, u, yT[1][:, :, sl], yT[0][:, :, sl])

                for u in range(HT):
                    if u >= 2:
                        g.take(u - 2)
                    dve.tensor_tensor(ybuf[:, u % 2], x0[:, u], gamma_row, ALU.mult).then_inc(y_ready, 1)
                    if u >= 1:
                        low(u - 1)
                low(HT - 1)
            close(c)

            c = piece()
            dve.wait_ge(mask_loaded, 16)
            head = SCTX - HEAD_ROWS
            c.link(dve.memset(maskadd[0:B, SCTX:KEYS], MASKED))
            c.link(dve.tensor_scalar(maskadd[0:B, 0:head], mask_i[0:B, HEAD_ROWS:SCTX], 0.0, MASKED, ALU.is_equal, ALU.mult))
            c.link(dve.tensor_scalar(maskadd[0:B, head:SCTX], mask_i[0:B, 0:HEAD_ROWS], 0.0, MASKED, ALU.is_equal, ALU.mult))
            c.link(dve.tensor_scalar(mask_f[0:B, 0:SCTX - TAIL], mask_i[0:B, 0:SCTX - TAIL], 0.0, None, ALU.not_equal))
            dve.tensor_reduce(small[0:B, 152:153], mask_f[0:B, 0:SCTX - TAIL], AX.X, ALU.max).then_inc(flag_part, 1)
            dve.wait_ge(wkv_loaded, 16)
            dve.wait_ge(cols_loaded, 16 * 9)
            for k in range(KC):
                ins = dve.tensor_scalar(wkv_f[:, k], wkv_f[:, k], cols[:, C_CGAMMA + k:C_CGAMMA + k + 1], None, ALU.mult)
            c.link(ins)
            for i in range(2):
                ins = dve.tensor_copy(wk[0][:, :, i * XD:(i + 1) * XD], wkv_f[:, :, 0:XD])
            dve.tensor_copy(wv[0], wkv_f[:, :, XD:2 * XD])
            c.link(dve.tensor_scalar(cols[:, C_OMR:C_OMR + 8], cols[:, C_MUR:C_MUR + 8], -1.0, 1.0, ALU.mult, ALU.add))
            for i in range(2):
                sl = slice(i * XD, (i + 1) * XD)
                dve.tensor_tensor(wk[1][:, :, sl], wkv_f[:, :, 0:XD], wk[0][:, :, sl], ALU.subtract)
            c.link(dve.tensor_tensor(wv[1], wkv_f[:, :, XD:2 * XD], wv[0], ALU.subtract))
            close(c)

            for i in range(2):
                with dve.Fori(0, 2) as mp:
                    g = Pass(dve, "q", 2 * i + mp)
                    for mm in range(2):
                        for hf in range(2):
                            bank = g.wait_hi(2 * mm + hf)
                            for h2 in range(2):
                                def q_of(rows_):
                                    return Q[rows_, hf * 8:hf * 8 + 8, bass.ds(i * 8 + mp * 4 + mm * 2 + h2, 1), :]\
                                        .rearrange("p b h s -> p b (h s)")
                                ins = dve.scalar_tensor_tensor(
                                    out=q_of(slice(64, 128)), in0=bank[64 * h2:64 * h2 + 64].rearrange("p (b s) -> p b s", b=8),
                                    scalar=XD ** -0.5, in1=q_of(slice(0, 64)), op0=ALU.mult, op1=ALU.subtract)
                            ins.then_inc(dve_freed, 1)

            dve.wait_ge(XN["shared_ready"], 1)
            dve.tensor_scalar(flag[:], SHARED[:, 0:1], 0.5, None, ALU.is_gt).then_inc(XN["shared_free"], 1)
            dve.wait_ge(XN["shared_free"], 1)
            finished(flag_ready)

            def attend(nkt):
                v = xmap(nkt)
                W_, ch, ns = v["groups"], v["chunks"], v["shared_n"]
                key = f"attend{nkt}"
                with dve.Fori(0, B) as b:
                    c_ = Chain(dve, xstep, 0, b, LINKS.get(key, 0))
                    for c, tiles in enumerate(v["tiles_of"]):
                        n = len(tiles)
                        if tiles[-1] == FULL_TILES - 1:
                            dve.wait_ge(XN["ctx_turned"], b * nkt + tiles[0])
                            dve.memset(v["ctx"][:, tiles[0] % 4], 0.0).then_inc(XN["ctx_zero"], 1)
                        dve.wait_ge(XN["ctx_loaded"], 16 * (b * nkt + tiles[0] + n))
                        moments(c_, [v["ctx"][:, kt % 4] for kt in tiles])
                        for u, kt in enumerate(tiles):
                            normed(v["ctx"][:, kt % 4], v["ctx"][:, kt % 4], u).then_inc(XN["ctx_norm"], 1)
                        for kt in tiles:
                            sl = slice(kt % 4 * P, (kt % 4 + 1) * P)
                            dve.wait_ge(XN["ctx_hi"], b * nkt + kt + 1)
                            dve.tensor_tensor(v["cT_lo"][:, :, sl], quad(psum[:, 6 + kt % 2]), v["cT_hi"][:, :, sl],
                                              ALU.subtract).then_inc(XN["ctx_lo"], 1)
                        sl = slice(tiles[0] * P, (tiles[-1] + 1) * P)
                        dve.wait_ge(XN["k_hi"], b * ch + c + 1)
                        dve.tensor_tensor(v["KB"][:, sl], SHARED[:, 0:n * P], v["KA"][:, sl], ALU.subtract)\
                            .then_inc(XN["shared_free"], 1)

                    def maximum(j):
                        dve.wait_ge(XN["s_mm"], b * 8 + j + 1)
                        np_ = v["P"].shape[1]
                        if j >= np_:
                            dve.wait_ge(XN["p_turned"], b * W_ + (j - np_ + 1) * ch)
                        settle(dve)
                        c_.link(dve.tensor_tensor_reduce(v["P"][:, j % np_, :], v["S"](j), v["mb"], 1.0, NEG, ALU.add, ALU.max,
                                                         xq_max[:, j:j + 1]))
                        dve.tensor_scalar(xq_neg[:, j:j + 1], xq_max[:, j:j + 1], -1.0, None, ALU.mult).then_inc(XN["s_max"], 1)

                    def copies(j):
                        for i in range(ch):
                            w = j * ch + i
                            if w % 2:
                                n = len(v["tiles_of"][i])
                                dve.wait_ge(XN["p_turned"], b * W_ + w + 1)
                                dve.wait_ge(XN["pv"], b * W_ + w - 1)
                                dve.tensor_copy(v["PT"][:, 1, 0:n, :], v["PTbank"](w)[:, 0:n * P].rearrange("p (t q) -> p t q", q=P))\
                                    .then_inc(XN["p_dve"], 1)

                    maximum(0)
                    for j in range(8):
                        if j + 1 < 8 and not v["full"]:
                            maximum(j + 1)
                        copies(j)
                        if j + 1 < 8 and v["full"]:
                            maximum(j + 1)
                    dve.wait_ge(XN["exp"], (b + 1) * 8)
                    c_.link(dve.tensor_scalar(xq_ok, xq_neg, ALL_MASKED, None, ALU.is_lt))
                    c_.link(dve.reciprocal(xq_r, xq_ok))
                    c_.link(dve.tensor_tensor(xq_r, xq_r, xq_ok, ALU.mult))
                    c_.link(dve.reciprocal(xq_ok, xq_sum))
                    c_.link(dve.tensor_tensor(xq_r, xq_r, xq_ok, ALU.mult))
                    dve.wait_ge(XN["pv"], (b + 1) * W_)
                    dve.tensor_tensor(v["O"], O_BANK.rearrange("p (j d) -> p j d", j=8), xq_r.unsqueeze(2).to_broadcast([P, 8, XD]),
                                      ALU.mult).then_inc(XN["o_norm"], 1)
                    for half in range(2):
                        dve.wait_ge(XN["ot_hi"], 2 * b + half + 1)
                        bank = SHARED[0:XD].rearrange("p (j m s) -> p j m s", j=4, m=2)
                        for h2 in range(2):
                            o = [x[64 * h2:64 * h2 + 64, 4 * half:4 * half + 4, bass.ds(b * S, S)] for x in oT]
                            ins = dve.tensor_tensor(o[1], bank[:, :, h2, :], o[0], ALU.subtract)
                        ins.then_inc(XN["shared_free"], 1)
                    assert c_.n == LINKS.get(key), f"LINKS[{key!r}] = {c_.n}"

            head_rows_used = dve.value_load(flag[0:1, 0:1], min_val=0, max_val=1)
            with dve.If(head_rows_used > 0):
                attend(FULL_TILES)
            with dve.If(head_rows_used < 1):
                attend(TAIL_TILES)
            finished(x_attended)
            dve.wait_ge(x_attended, 1)

            for i in range(4):
                with dve.Fori(0, 4) as m:
                    g = Pass(dve, "ff", 4 * i + m)
                    dve.wait_ge(prod_lo, 8 * i + 2 * m)
                    for hf in range(2):
                        g.wait_done(2 * hf + 1)
                        dve.tensor_tensor(prod[:, hf], g.take(2 * hf), ybuf[:, hf], ALU.mult).then_inc(dve_freed, 1)
                    for hf in range(2):
                        dve.wait_ge(prod_hi, 8 * i + 2 * m + hf + 1)
                        x = [t[:, bass.ds(4 * i + m, 1), hf * 512:(hf + 1) * 512].rearrange("p a n -> p (a n)") for t in ffT]
                        dve.tensor_tensor(x[1], prod[:, hf], x[0], ALU.subtract).then_inc(prod_lo, 1)
            with dve.Fori(0, 2) as h:
                g = Pass(dve, "xout", h)
                for u in range(HT):
                    dve.tensor_tensor(xt(h, u), g.take(u), xt(h, u), ALU.add).then_inc(dve_freed, 1)
            if LAYERS > 5:
                c = piece()
                c.link(dve.reduce_sum(gtot, gsum, AX.X))
                finished(gamma_part)
                g = Pass(dve, "gamma")
                dve.tensor_scalar(thr, g.take(0)[:, 0:2], 0.5 / (FF * D), 0.5 * ABSMEAN_EPS, ALU.mult, ALU.add).then_inc(dve_freed, 1)
                g.wait_done(0)
                dve.tensor_scalar(nthr, thr, -1.0, None, ALU.mult).then_inc(thr_ready, 1)
                close(c)
            finished(layer_done)
            dve.wait_ge(layer_done, 1)

            def attention(n, name):
                bq, bk = (C_BQ1, C_BK1) if n else (C_BQ0, C_BK0)
                c = piece()
                dve.wait_ge(bias_loaded, 48 * (n + 1))
                c.link(dve.memset(vb_words, 0))
                close(c)
                with dve.Fori(0, 2) as h:
                    c = piece(h, 2, "attention")
                    g = Pass(dve, name, h)
                    norm_half(c, g, h)
                    for x, (dst, bias) in enumerate(((qh, bq), (kh, bk))):
                        for m in range(KC):
                            bank = g.wait_hi(4 + 4 * x + m)
                            dve.scalar_tensor_tensor(out=dst[1][:, m, :], in0=bank, scalar=cols[:, bias + m:bias + m + 1],
                                                     in1=dst[0][:, m, :], op0=ALU.add, op1=ALU.subtract).then_inc(dve_freed, 1)

                    def v_low(u):
                        dve.wait_ge(v_hi, (n * 2 + h) * HT + u + 1)
                        for m in range(2):
                            r_ = slice(64 * m, 64 * m + 64)
                            ins = dve.tensor_tensor(vb[1][r_, 2 * u:2 * u + 2, :, m, :],
                                                    vf[r_, u % 2].rearrange("p (b g e) -> p b g e", b=2, g=8),
                                                    vb[0][r_, 2 * u:2 * u + 2, :, m, :], ALU.subtract)
                        ins.then_inc(v_done, 1)

                    for u in range(HT):
                        if u >= 2:
                            dve.wait_ge(v_done, (n * 2 + h) * HT + u - 1)
                        dve.tensor_tensor(vf[:, u % 2].rearrange("p (b e) -> p b e", b=2),
                                          g.take(12 + u).rearrange("p (b e) -> p b e", b=2),
                                          bv.rearrange("p j e -> p (j e)").unsqueeze(1).to_broadcast([P, 2, 256]),
                                          ALU.add).then_inc(dve_freed, 1)
                        if u >= 1:
                            v_low(u - 1)
                    v_low(HT - 1)

                    def weigh(u, at):
                        pu = prob[:, u % 2]
                        for r in range(4):
                            s = g.take(at + r)[:, 0:4 * S].rearrange("p (m s) -> p m s", m=4)
                            if n:
                                ins = dve.tensor_scalar(pu[:, r], s, AD ** -0.5, None, ALU.mult)
                            else:
                                ins = dve.scalar_tensor_tensor(out=pu[:, r], in0=s, scalar=AD ** -0.5,
                                                               in1=causal[:].unsqueeze(1).to_broadcast([P, 4, S]),
                                                               op0=ALU.mult, op1=ALU.add)
                            ins.then_inc(dve_freed, 1)
                        g.wait_done(at + 3)
                        flat = pu.rearrange("p r m s -> p (r m) s")
                        c.link(dve.tensor_reduce(s_max[:, u % 2], flat, AX.X, ALU.max))
                        dve.tensor_tensor(flat, flat, s_max[:, u % 2].unsqueeze(2).to_broadcast([P, AH, S]), ALU.subtract)\
                            .then_inc(p_max, 1)

                    at = 16
                    weigh(0, at)
                    at += 4
                    for u in range(HT):
                        if u + 1 < HT:
                            weigh(u + 1, at)
                            at += 4
                        dve.wait_ge(p_exp, (n * 2 + h) * HT + u + 1)
                        c.link(dve.reduce_sum(s_sum[:, u % 2], prob[:, u % 2].rearrange("p r m s -> p (r m) s"), AX.X))
                        c.link(dve.reciprocal(s_sum[:, u % 2], s_sum[:, u % 2]))
                        for j in range(2):
                            lo_of_tile(g, at + j, pT[1][:, u % 2, 4 * j:4 * j + 4, :], pT[0][:, u % 2, 4 * j:4 * j + 4, :])
                        dve.tensor_tensor(ybuf[:, u % 2].rearrange("p (m r d) -> p m r d", m=4, r=4),
                                          g.take(at + 2).rearrange("p (m r d) -> p m r d", m=4, r=4),
                                          s_sum[:, u % 2].rearrange("p (r m) -> p m r", r=4).unsqueeze(3).to_broadcast([P, 4, 4, AD]),
                                          ALU.mult).then_inc(dve_freed, 1)
                        sl = slice(u * P, (u + 1) * P)
                        lo_of_tile(g, at + 3, ah[1][:, :, sl], ah[0][:, :, sl])
                        at += 4
                    for u in range(HT):
                        dve.tensor_tensor(xt(h, u), g.take(at + u), xt(h, u), ALU.add).then_inc(dve_freed, 1)
                    g.wait_done(at + 3)
                    for u in range(HT):
                        ins = dve.tensor_tensor(xt(h, u), xt(h, u), bo, ALU.add)
                    c.link(ins)
                close(c)
                finished(layer_done)

            if LAYERS > 1:
                attention(0, "attn0")

            if LAYERS > 2:
                c = piece()
                g = Pass(dve, "turn_mix")
                for i, n in enumerate("rkv"):
                    wait_slot(dve, W["mix", n])
                    for x in range(2):
                        copy_turned(g, 4 * i + 2 * x + 1, w_of(("mix", n))[x][:, 2:4, :])
                c.link(dve.memset(zp[:, :, :, 0:1], 0.0))
                finished(om_ready)
                close(c)
                with dve.Fori(0, 2) as h:
                    c = piece(h, 2, "mix")
                    g = Pass(dve, "mix", h)
                    moments(c, [xt(h, u) for u in range(HT)])
                    for u in range(HT):
                        if u >= 2:
                            g.take(u - 2)
                        normed(ybuf[:, u % 2], xt(h, u), u).then_inc(y_ready, 1)

                    def mixed(n):
                        mu = (C_MUR, C_MUK)[n // 4] + n % 4
                        if n >= 2:
                            dve.wait_ge(mix_lo, 8 * h + n - 1)
                        dve.wait_ge(mix_a, 8 * h + n + 1)
                        dve.scalar_tensor_tensor(out=mix_f[:, n % 2].rearrange("p (b s) -> p b s", b=8),
                                                 in0=zp[:, n % 4, :, 1:], scalar=cols[:, mu:mu + 1],
                                                 in1=mix_t[:, n % 2].rearrange("p (b s) -> p b s", b=8),
                                                 op0=ALU.mult, op1=ALU.add).then_inc(mix_b, 1)

                    def mixed_low(n):
                        dve.wait_ge(mix_hi, 8 * h + n + 1)
                        dst = mixT[n // 4]
                        dve.tensor_tensor(dst[1][:, n % 4, :], mix_f[:, n % 2], dst[0][:, n % 4, :], ALU.subtract)\
                            .then_inc(mix_lo, 1)

                    mixed(0)
                    for n in range(8):
                        if n < 7:
                            mixed(n + 1)
                        mixed_low(n)

                    def relu_low(m):
                        dve.wait_ge(relu_hi, 4 * h + m + 1)
                        dve.tensor_tensor(kact[1][:, m, :], relu2[:, m % 2], kact[0][:, m, :], ALU.subtract).then_inc(relu_lo, 1)

                    for m in range(KC):
                        dve.tensor_scalar(relu[:, m % 2], g.take(8 + m), 0.0, None, ALU.max).then_inc(dve_freed, 1)
                        if m:
                            relu_low(m - 1)
                    relu_low(KC - 1)
                    g.wait_done(7)
                    for u in range(HT):
                        dve.tensor_tensor(relu[:, u % 2], g.take(12 + u), recept[:, u], ALU.mult).then_inc(dve_freed, 1)
                        g.wait_done(12 + u)
                        c.link(dve.tensor_tensor(xt(h, u), xt(h, u), relu[:, u % 2], ALU.add))
                close(c)
                finished(layer_done)

            if LAYERS > 3:
                c = piece()
                pt = ptr[:, 0:T]
                wptr = ptf[:, 0:4 * T].rearrange("p (w t) -> p w t", t=T)
                dve.wait_ge(ids_loaded, 48)
                for w in range(3):
                    c.link(dve.tensor_scalar(wptr[:, w], pt, float(w), 0.0, ALU.add, ALU.max))
                    c.link(dve.tensor_scalar(wptr[:, w], wptr[:, w], float(SCTX - 1), None, ALU.min))
                    c.link(dve.tensor_tensor(row_of.rearrange("p (t w) -> p w t", w=4)[:, w, 0:T], wptr[:, w], tile_base, ALU.add))
                finished(rows_ready)
                c.link(dve.tensor_scalar(wptr[:, 3], wptr[:, 0], float(S - 1), None, ALU.min))
                for t in range(T):
                    c.link(dve.scalar_tensor_tensor(out=id_hit[:, 0:S], in0=key_no[:], scalar=wptr[:, 3, t:t + 1], in1=ids_rows[:, t],
                                                    op0=ALU.is_equal, op1=ALU.mult, accum_out=rel_id[:, t:t + 1]))
                cw = cols[:, C_CW:C_CW + 2]
                c.link(dve.tensor_reduce(council[:, 0:1], cw, AX.X, ALU.max))
                c.link(dve.tensor_scalar(council[:, 2:4], cw, council[:, 0:1], None, ALU.subtract))
                finished(logit)
                g = Pass(dve, "fold")

                def folded(first, pair):
                    for m in range(KC):
                        bank = g.wait_hi(first + m)
                        dve.tensor_tensor(pair[1][:, m, :], bank, pair[0][:, m, :], ALU.subtract).then_inc(dve_freed, 1)

                folded(0, fold[0])
                folded(4, fold[1])
                wait_slot(dve, W["win", "WoutT"])
                for x in range(2):
                    copy_turned(g, 8 + 2 * x + 1, w_of(("win", "WoutT"))[x][:, 2:4, :])
                folded(12, fold[2])
                folded(16, fold[3])
                dve.wait_ge(e_ready, 1)
                c.link(dve.reduce_sum(council[:, 0:1], council[:, 4:6], AX.X))
                c.link(dve.reciprocal(council[:, 1:2], council[:, 0:1]))
                c.link(dve.tensor_scalar(council[:, 6:8], council[:, 4:6], council[:, 1:2], None, ALU.mult))
                close(c)
                with dve.Fori(0, 2) as h:
                    c = piece(h, 2, "window")
                    g = Pass(dve, "window", h)
                    norm_half(c, g, h)
                    dve.wait_ge(win_loaded, 16 * 3 * HT * (h + 1))
                    for u in range(HT):
                        for s in range(2):
                            bank = g.take(4 + 2 * u + s)
                            for w in range(3):
                                ins = dve.tensor_tensor_reduce(junk[:, w % 2], bank, win[:, u, w, :], D ** -0.5, 0.0, ALU.mult,
                                                               ALU.add, sc[:, 3 * s + w, u:u + 1])
                                if w < 2:
                                    c.link(ins)
                                else:
                                    ins.then_inc(dve_freed, 1)
                                    g.wait_done(4 + 2 * u + s)
                    col = lambda i: sc[:, i, :]
                    rel, v1, v2 = col(0), col(1), col(2)
                    ids = rel_id[:, bass.ds(h * HT, HT)]

                    def tt(o, x, y, op):
                        c.link(dve.tensor_tensor(col(o), x, y, op))

                    def ts(o, x, s1, s2, op0, op1=None):
                        c.link(dve.tensor_scalar(col(o), x, s1, s2, op0, *([op1] if op1 is not None else [])))

                    tt(8, v1, v2, ALU.add)
                    tt(9, v1, v2, ALU.max)
                    ts(10, v1, -1.0, None, ALU.mult)
                    tt(11, col(10), v2, ALU.max)
                    tt(12, v1, v2, ALU.subtract)
                    ts(13, col(12), -1.0, None, ALU.mult)
                    tt(12, col(12), col(13), ALU.max)
                    for e in range(5):
                        x = col(14 if e == 0 else 15)
                        c.link(dve.scalar_tensor_tensor(out=x, in0=ids, scalar=float(e), in1=col(8 + e), op0=ALU.is_equal,
                                                        op1=ALU.mult))
                        if e:
                            tt(14, col(14), col(15), ALU.add)
                    ts(16, ids, 0.0, None, ALU.is_ge)
                    c.link(dve.scalar_tensor_tensor(out=col(16), in0=ids, scalar=4.0, in1=col(16), op0=ALU.is_le, op1=ALU.mult))
                    tt(14, col(14), col(16), ALU.mult)
                    ts(17, col(16), -1.0, 1.0, ALU.mult, ALU.add)
                    tt(17, col(17), rel, ALU.mult)
                    tt(0, col(14), col(17), ALU.add)
                    for s in range(2):
                        tt(18, col(3 * s), col(3 * s + 1), ALU.max)
                        tt(18, col(18), col(3 * s + 2), ALU.max)
                        for w in range(3):
                            tt(SC_E + 3 * s + w, col(3 * s + w), col(18), ALU.subtract)
                    finished(logit)
                    dve.wait_ge(e_ready, h + 2)
                    for s in range(2):
                        e0 = SC_E + 3 * s
                        tt(18, col(e0), col(e0 + 1), ALU.add)
                        tt(18, col(18), col(e0 + 2), ALU.add)
                        c.link(dve.reciprocal(col(19), col(18)))
                        ts(19, col(19), council[:, 6 + s:7 + s], None, ALU.mult)
                        for w in range(3):
                            tt(e0 + w, col(e0 + w), col(19), ALU.mult)

                    def low(n):
                        sl = slice(n // 2 * P, (n // 2 + 1) * P)
                        pair = (yh, y2)[n % 2]
                        lo_of_tile(g, 12 + n, pair[1][:, :, sl], pair[0][:, :, sl])

                    for n in range(2 * HT):
                        u, s = n // 2, n % 2
                        x = comb[:, s]
                        wt = [sc[:, SC_E + 3 * s + w, u:u + 1] for w in range(3)]
                        c.link(dve.tensor_scalar(x, win[:, u, 0, :], wt[0], None, ALU.mult))
                        c.link(dve.scalar_tensor_tensor(out=x, in0=win[:, u, 1, :], scalar=wt[1], in1=x, op0=ALU.mult, op1=ALU.add))
                        dve.scalar_tensor_tensor(out=x, in0=win[:, u, 2, :], scalar=wt[2], in1=x, op0=ALU.mult, op1=ALU.add)\
                            .then_inc(comb_ready, 1)
                        if n:
                            low(n - 1)
                    low(2 * HT - 1)
                    for u in range(HT):
                        dve.scalar_tensor_tensor(out=xt(h, u), in0=g.take(20 + u), scalar=cols[:, C_GAIN:C_GAIN + 1], in1=xt(h, u),
                                                 op0=ALU.mult, op1=ALU.add).then_inc(dve_freed, 1)
                    g.wait_done(23)
                close(c)
                finished(layer_done)

            if LAYERS > 4:
                g = Pass(dve, "turn_w1")
                for i, n in enumerate("qkvo"):
                    dst = woT
                    if n != "o":
                        wait_slot(dve, W["w1", n])
                        dst = w_of(("w1", n))
                    for x in range(2):
                        copy_turned(g, 4 * i + 2 * x + 1, dst[x][:, 2:4, :])
                attention(1, "attn1")

            if LAYERS > 5:
                g = Pass(dve, "turn_mlp")
                for i in range(4):
                    copy_turned(g, 2 * i + 1, fcT[:, i, 2:4, :])
                for i in range(4):
                    copy_turned(g, 8 + 2 * i + 1, projT[:, 4 * i + 2:4 * i + 4, :])
                with dve.Fori(0, 2) as h:
                    c = piece(h, 2, "mlp")
                    g = Pass(dve, "mlp", h)
                    norm_half(c, g, h)
                    at = 4

                    def norm_hidden(u, last):
                        g.wait_done(last)
                        x = hid[:, u % 2]
                        for n in range(4):
                            ins = dve.bn_stats(stats[:, n, :], x[:, n * 512:(n + 1) * 512])
                        c.link(ins)
                        settle(dve)
                        c.link(dve.bn_aggr(mv[:, 0, :], stats[:].rearrange("p n k -> p (n k)")))
                        rstd(c, 1)
                        normed(x, x, 0).then_inc(hid_norm, 1)

                    norm_hidden(0, 7)
                    at = 8
                    for u in range(HT):
                        if u + 1 < HT:
                            norm_hidden(u + 1, at + 3)
                            at += 4
                        for n in range(4):
                            lo_of_tile(g, at + n, hT[u % 2][1][:, 4 * n:4 * n + 4, :], hT[u % 2][0][:, 4 * n:4 * n + 4, :])
                        dve.tensor_tensor(xt(h, u), g.take(at + 4), xt(h, u), ALU.add).then_inc(dve_freed, 1)
                        at += 5
                close(c)
                finished(layer_done)


def kernel(**inputs):
    import numpy as _np
    import concourse.bacc as _bacc
    from concourse import mybir as _mybir
    from concourse.bass_utils import run_bass_kernel_spmd as _run

    nc = _bacc.Bacc("TRN2", target_bir_lowering=False, num_devices=1)
    arrays, args = {}, {}
    for name in inputs:
        arr = _np.ascontiguousarray(inputs[name])
        if arr.ndim == 0 or name == "L1_xattn_gain":
            arr = arr.reshape(1)
        arrays[f"in_{name}_dram"] = arr
        args[name] = nc.dram_tensor(f"in_{name}_dram", arr.shape, _mybir.dt.from_np(arr.dtype), kind="ExternalInput").ap()
    out = nc.dram_tensor("out_0_dram", (B, S, D), F32, kind="ExternalOutput").ap()
    build(nc, args, out)
    r = _run(nc, [arrays], core_ids=[0])
    return r.results[0]["out_0_dram"]
```

```python
from contextlib import ExitStack

import concourse.bass as bass
from concourse import mybir

F32 = mybir.dt.float32
BF16 = mybir.dt.bfloat16
I32 = mybir.dt.int32
ALU = mybir.AluOpType
ACT = mybir.ActivationFunctionType
AX = mybir.AxisListType

LAYERS = 6
P = 128
B, S, D = 16, 64, 512
T = B * S // P
HT = T // 2
KC = D // P
SCTX = 1601
XH, XD = 16, 64
FF = 2048
AH, AD = 16, 32
RING = 6
STAGED = 2
LN_EPS = 1e-5
ABSMEAN_EPS = 1e-6
MASKED = -3.0e38
NEG = -3.4028234663852886e38
ALL_MASKED = 1.0e38
DVE_CREDIT = 1
ACT_CREDIT = 2
CONSTS = 11
SC_E = 20
LINKS = {"ln0": 30, "norm": 14, "end": 5, "attention": 27, "mix": 18, "window": 92, "mlp": 70}
RSQRT_SEED = float(0x5F3759DF)
KB = 256

FULL_TILES = (SCTX + P - 1) // P
TAIL_TILES = 4
TAIL = TAIL_TILES * P
HEAD_ROWS = SCTX - (FULL_TILES - 1) * P
KEYS = FULL_TILES * P


class Stage:

    def __init__(self, letters, passes=1, banks=8, rolling=False):
        self.letters, self.passes, self.banks, self.rolling = letters, passes, banks, rolling
        assert not rolling or len(letters) == banks
        self.n = len(letters)
        self.n_dve = self.n - letters.count("A")
        self.n_act = letters.count("A")
        self.n_hi = letters.count("h")
        self.base = None

    def freed(self, g):
        head = self.letters[:g + 1]
        return (True, head.count("A")) if self.letters[g] == "A" else (False, len(head) - head.count("A"))


class Chain:

    def __init__(self, eng, semaphore, base=0, i=0, per_pass=0):
        self.eng, self.sem, self.start, self.n, self.per_pass = eng, semaphore, base + i * per_pass, 0, per_pass

    def link(self, ins):
        self.n += 1
        ins.then_inc(self.sem, 1)
        self.eng.wait_ge(self.sem, self.start + self.n)

    def close(self):
        assert not self.per_pass or self.n == self.per_pass, f"links in a pass: {self.n}"


def build(nc, a, out):
    ctx = ExitStack()
    with ctx:
        def sb(name, shape, dt=F32):
            return ctx.enter_context(nc.sbuf_tensor(name, shape, dt))

        def sem(name):
            return ctx.enter_context(nc.semaphore(name))

        X = sb("X", [P, T, D])
        y_mem = sb("y_mem", [P, 16 * KB])
        o_mem = sb("o_mem", [P, 32 * KB])
        big = sb("big", [P, 64 * KB])
        side = sb("side", [P, 8 * KB])
        ring_hi = sb("ring_hi", [P, RING, KC, D], BF16)
        ring_lo = sb("ring_lo", [P, RING, KC, D], BF16)
        stage = sb("stage", [P, STAGED, KC, D])
        ybuf = sb("ybuf", [P, 2, D])
        ident = sb("ident", [P, P])
        identb = sb("identb", [P, P], BF16)
        ones = sb("ones", [P, P])
        causal = sb("causal", [P, S])
        stats = sb("stats", [P, 4, 6])
        mv = sb("mv", [P, 4, 2])
        nw = sb("nw", [P, 3, 4])
        cols = sb("cols", [P, 48])
        small = sb("small", [P, 168])
        key_no = sb("key_no", [P, S], I32)
        flag = sb("flag", [P, 1], I32)
        spare = sb("spare", [P, KB])
        psum = ctx.enter_context(nc.psum_tensor("psum", [P, 8, 512], F32))

        def settle(eng):
            eng.sem_inc(idle, 1)

        def carve(mem, at_kb, kb, dt, pattern=None, **dims):
            v = mem[:, int(at_kb * KB):int((at_kb + kb) * KB)]
            if dt != F32:
                v = v.bitcast(dt)
            return v.rearrange(pattern, **dims) if pattern else v

        def halves(mem, at_kb, kb, pattern, **dims):
            return [carve(mem, at_kb + i * kb, kb, BF16, pattern, **dims) for i in range(2)]

        yT = halves(y_mem, 0, 8, "p (k n) -> p k n", k=KC)
        yh = halves(y_mem, 0, 4, "p (k n) -> p k n", k=KC)
        y2 = halves(y_mem, 8, 4, "p (k n) -> p k n", k=KC)
        oT = halves(o_mem, 0, 16, "p (k n) -> p k n", k=8)
        Q = carve(big, 0, 32, BF16, "p (b h s) -> p b h s", b=B, h=XH)
        x0 = carve(big, 32, 8, F32, "p (t n) -> p t n", t=HT)
        gamma_row = carve(big, 40, 2, F32)
        wkv_f = carve(o_mem, 0, 2, F32, "p (k n) -> p k n", k=KC)
        mask_i = carve(o_mem, 8, 7, I32)
        mask_f = carve(o_mem, 16, 7, F32)
        maskadd = carve(side, 0, 3.25, BF16)
        wk = halves(side, 3.25, 1, "p (k n) -> p k n", k=KC)
        wv = halves(side, 5.25, 0.5, "p (k n) -> p k n", k=KC)
        ffT = halves(big, 0, 32, "p (k n) -> p k n", k=FF // P)
        prod = carve(side, 0, 4, F32, "p (i n) -> p i n", i=2)
        qh = halves(big, 0, 4, "p (k n) -> p k n", k=KC)
        kh = halves(big, 8, 4, "p (k n) -> p k n", k=KC)
        vb = halves(big, 16, 8, "p (b g m e) -> p b g m e", b=8, g=8, m=2)
        vb_words = carve(big, 16, 16, I32)
        prob = carve(big, 32, 8, F32, "p (i r m s) -> p i r m s", i=2, r=4, m=4)
        pT = [carve(big, 40 + 4 * i, 4, BF16, "p (i g q) -> p i g q", i=2, g=8) for i in range(2)]
        vf = carve(big, 48, 4, F32, "p (i n) -> p i n", i=2)
        ah = halves(big, 52, 4, "p (k n) -> p k n", k=KC)
        bv = carve(side, 4, 1, F32, "p (j e) -> p j e", j=2)
        bo = carve(side, 5, 2, F32)
        woT = halves(y_mem, 8, 4, "p (k n) -> p k n", k=KC)
        zp = carve(big, 0, 8.125, F32, "p (k b s) -> p k b s", k=KC, b=8)
        mixT = [halves(big, 9 + 8 * i, 4, "p (k n) -> p k n", k=KC) for i in range(2)]
        mix_t = carve(big, 25, 4, F32, "p (i n) -> p i n", i=2)
        mix_f = carve(big, 29, 4, F32, "p (i n) -> p i n", i=2)
        kact = halves(big, 33, 4, "p (k n) -> p k n", k=KC)
        recept = carve(big, 41, 8, F32, "p (t n) -> p t n", t=HT)
        relu = carve(big, 49, 4, F32, "p (i n) -> p i n", i=2)
        relu2 = carve(big, 53, 4, F32, "p (i n) -> p i n", i=2)
        fold = [halves(big, 8 * i, 4, "p (k n) -> p k n", k=KC) for i in range(4)]
        win = carve(big, 32, 24, F32, "p (t w n) -> p t w n", t=HT, w=3)
        comb = carve(big, 56, 4, F32, "p (i n) -> p i n", i=2)
        junk = carve(big, 60, 4, F32, "p (i n) -> p i n", i=2)
        ids_rows = carve(o_mem, 0, 2, I32, "p (t s) -> p t s", t=T)
        id_hit = carve(o_mem, 3, 0.25, F32)
        ptr = carve(o_mem, 4, 1, I32)
        ptf = carve(o_mem, 5, 1, F32)
        row_of = carve(o_mem, 6, 1, I32)[:, 0:4 * T]
        sc = carve(o_mem, 8, 2, F32, "p (n t) -> p n t", t=HT)
        rel_id = carve(o_mem, 7, 0.25, F32)
        fcT = carve(big, 0, 16, BF16, "p (i k n) -> p i k n", i=4, k=KC)
        projT = carve(big, 16, 16, BF16, "p (k n) -> p k n", k=FF // P)
        lnw = carve(big, 32, 8, F32)
        lnb = carve(big, 40, 8, F32)
        hid = carve(o_mem, 0, 16, F32, "p (i n) -> p i n", i=2)
        hT = [halves(o_mem, 16 + 8 * i, 4, "p (k n) -> p k n", k=FF // P) for i in range(2)]

        C_CGAMMA, C_BQ0, C_BK0, C_BQ1, C_BK1, C_MUR, C_MUK, C_OMR, C_OMK, C_GAIN, C_CW = 0, 4, 8, 12, 16, 20, 24, 28, 32, 36, 38
        gsum = small[:, 0:32].rearrange("p (w b) -> p w b", w=2)
        gtot = small[:, 32:34]
        thr = small[:, 34:36]
        nthr = small[:, 36:38]
        s_max = small[:, 40:72].rearrange("p (i h) -> p i h", i=2)
        s_sum = small[:, 72:104].rearrange("p (i h) -> p i h", i=2)
        xq_max, xq_neg, xq_sum, xq_ok, xq_r = (
            carve(side, 7.25 + i / 16, 1 / 16, F32, "p (i j) -> p i j", i=2) for i in range(5))
        council = small[:, 160:168]
        tile_base = small[:, 144:152].bitcast(I32)

        x_loaded, cols_loaded, gamma_loaded, wkv_loaded, mask_loaded = map(
            sem, ("x_loaded", "cols_loaded", "gamma_loaded", "wkv_loaded", "mask_loaded"))
        stage_loaded = [sem(f"stage_loaded{i}") for i in range(STAGED)]
        bias_loaded, ids_loaded, win_loaded, out_stored = map(sem, ("bias_loaded", "ids_loaded", "win_loaded", "out_stored"))
        idle = sem("idle")
        const_ready = sem("const_ready")
        pool_split = sem("pool_split")
        pool_part = sem("pool_part")
        group_ready = sem("group_ready")
        act_hi = sem("act_hi")
        dve_freed = sem("dve_freed")
        act_freed = sem("act_freed")
        step = sem("step")
        y_ready = sem("y_ready")
        wkv_ready = sem("wkv_ready")
        sg_ready, prod_ready, prod_hi, prod_lo = map(sem, ("sg_ready", "prod_ready", "prod_hi", "prod_lo"))
        v_sum, v_hi, v_done, p_max, p_exp, o_free = map(sem, ("v_sum", "v_hi", "v_done", "p_max", "p_exp", "o_free"))
        layer_done = sem("layer_done")
        zeroed = sem("zeroed")
        om_ready, mix_a, mix_b, mix_hi, mix_lo = map(sem, ("om_ready", "mix_a", "mix_b", "mix_hi", "mix_lo"))
        relu_ready, relu_sq, relu_hi, relu_lo = map(sem, ("relu_ready", "relu_sq", "relu_hi", "relu_lo"))
        rows_ready, win_used, logit, e_ready, comb_ready = map(sem, ("rows_ready", "win_used", "logit", "e_ready", "comb_ready"))
        thr_ready, gelu_done, hid_norm, hid_ready = map(sem, ("thr_ready", "gelu_done", "hid_norm", "hid_ready"))
        flag_part, flag_ready, x_attended, gamma_part, hid_scaled = map(
            sem, ("flag_part", "flag_ready", "x_attended", "gamma_part", "hid_scaled"))

        def rows(w, c0=0):
            return w[:, c0:c0 + D].rearrange("(k p) n -> p k n", p=P)

        entries, W = [], {}

        def entry(key, kind, src=None):
            W[key] = len(entries)
            entries.append((kind, src))

        for i in range(2):
            entry(("q", i), "n", rows(a["L0_xattn_Wq"], i * D))
        for i in range(4):
            entry(("ffa", i), "n", rows(a["L0_xattn_Wff1"], i * D))
            entry(("ffg", i), "n", rows(a["L0_xattn_Wff1"], FF + i * D))
        for i in range(2):
            entry(("xo", i), "n", rows(a["L0_xattn_Wout"][i * D:(i + 1) * D, :]))
        for i in range(4):
            entry(("ff2", i), "n", rows(a["L0_xattn_Wff2"][i * D:(i + 1) * D, :]))
        before_x = 8
        ends = [len(entries)]
        for n in "qkvo":
            entry(("w0", n), "n", rows(a["L0_attn_w" + n]))
        ends.append(len(entries))
        for n in "rkv":
            entry(("mixn", n), "n", rows(a["L0_ffn_W_" + n]))
            entry(("mix", n), "T")
        ends.append(len(entries))
        for n in ("Wqj", "Wkj", "Wqi", "Wki", "Wout"):
            entry(("win", n), "n", rows(a["L1_xattn_" + n]))
        entry(("win", "WoutT"), "T")
        for n in ("Wvj", "Wvi"):
            entry(("win", n), "n", rows(a["L1_xattn_" + n]))
        ends.append(len(entries))
        for i, n in enumerate("qkv"):
            entry(("w1n", n), "n", rows(a["L1_attn_W_qkv"][i * D:(i + 1) * D, :]))
            entry(("w1", n), "T")
        entry(("w1n", "o"), "n", rows(a["L1_attn_W_out"]))
        ends.append(len(entries))
        for i in range(4):
            entry(("fc", i), "t", rows(a["L1_ffn_W_fc"][i * D:(i + 1) * D, :]))
        for i in range(4):
            entry(("proj", i), "t", rows(a["L1_ffn_W_proj"], i * D))
        ends.append(len(entries))
        entries = entries[:ends[LAYERS - 1]]
        staged_order = [e for e, (kind, _) in enumerate(entries) if kind != "T"]
        released = {}

        def w_of(key):
            s = W[key] % RING
            return ring_hi[:, s], ring_lo[:, s]

        def wait_slot(eng, e):
            if e >= RING:
                eng.wait_ge(*released[e - RING])

        def wait_split(eng, key):
            eng.wait_ge(pool_split, staged_order.index(W[key]) + 1)

        plan = {"ln0": Stage("hhhh", 2), "q": Stage("hhhh", 4, 4, True), "ff": Stage("DADA", 16, 4, True),
                "xout": Stage("DDDD", 2)}
        if LAYERS > 5:
            plan["gamma"] = Stage("D")
        attn = ("hhhh" "hhhh" "hhhh" "DDDD"
                "DDDD" + "DDDDhhDh" * 3 + "hhDh"
                + "DDDD")
        if LAYERS > 1:
            plan["attn0"] = Stage(attn, 2)
        if LAYERS > 2:
            plan["turn_mix"] = Stage("AD" * 6)
            plan["mix"] = Stage("AAAA" "AAAA" "DDDD" "DDDD", 2)
        if LAYERS > 3:
            plan["fold"] = Stage("hhhh" "hhhh" "ADAD" "hhhh" "hhhh")
            plan["window"] = Stage("hhhh" "DDDDDDDD" "hhhhhhhh" "DDDD", 2)
        if LAYERS > 4:
            plan["turn_w1"] = Stage("AD" * 8)
            plan["attn1"] = Stage(attn, 2)
        if LAYERS > 5:
            plan["turn_mlp"] = Stage("AD" * 8)
            plan["mlp"] = Stage("hhhh" + "AAAA" + "AAAAhhhhD" * 3 + "hhhhD", 2)
        total = [0, DVE_CREDIT, ACT_CREDIT, 0]
        for st in plan.values():
            st.base = tuple(total)
            for i, n in enumerate((st.n, st.n_dve, st.n_act, st.n_hi)):
                total[i] += n * st.passes

        def after(name, groups=None):
            st = plan[name]
            return group_ready, st.base[0] + (st.n * st.passes if groups is None else groups)

        class Pass:

            def __init__(self, eng, name, i=0):
                self.eng, self.st = eng, plan[name]
                st = self.st
                self.ready, self.dve, self.act, self.hi = (
                    b + n * i for b, n in zip(st.base, (st.n, st.n_dve, st.n_act, st.n_hi)))
                self.first = st.base[0] == 0
                self.at = 0

            def bank(self, g):
                return psum[:, g % self.st.banks, :]

            def open(self):
                g, st = self.at, self.st
                self.at += 1
                if st.rolling:
                    is_act, n = st.freed(g)
                    if is_act:
                        self.eng.wait_ge(act_freed, self.act - st.n_act + n)
                    else:
                        self.eng.wait_ge(dve_freed, self.dve - st.n_dve + n)
                elif g >= st.banks:
                    is_act, n = st.freed(g - st.banks)
                    self.eng.wait_ge(act_freed if is_act else dve_freed, (self.act if is_act else self.dve) + n)
                elif g == 0:
                    self.all_free()
                return self.bank(g)

            def all_free(self):
                self.eng.wait_ge(dve_freed, self.dve)
                self.eng.wait_ge(act_freed, self.act)

            def take(self, g):
                self.eng.wait_ge(group_ready, self.ready + g + 1)
                return self.bank(g)

            def wait_hi(self, g):
                self.eng.wait_ge(act_hi, self.hi + self.st.letters[:g + 1].count("h"))
                return self.bank(g)

            def wait_done(self, g):
                is_act, n = self.st.freed(g)
                self.eng.wait_ge(act_freed if is_act else dve_freed, (self.act if is_act else self.dve) + n)

        for i in range(2):
            released[W["q", i]] = after("q", 8 * (i + 1))
        for i in range(4):
            released[W["ffa", i]] = released[W["ffg", i]] = after("ff", 16 * (i + 1))
            released[W["ff2", i]] = after("xout")
        for i in range(2):
            released[W["xo", i]] = after("xout")
        if LAYERS > 1:
            for n in "qkvo":
                released[W["w0", n]] = after("attn0")
        if LAYERS > 2:
            for i, n in enumerate("rkv"):
                released[W["mixn", n]] = after("turn_mix", 4 * (i + 1))
                released[W["mix", n]] = after("mix")
        if LAYERS > 3:
            for n, g in (("Wqj", 4), ("Wkj", 4), ("Wqi", 8), ("Wki", 8), ("Wout", 12), ("WoutT", 20), ("Wvj", 16), ("Wvi", 20)):
                released[W["win", n]] = after("fold", g)
        if LAYERS > 4:
            for i, n in enumerate("qkvo"):
                released[W["w1n", n]] = after("turn_w1", 4 * (i + 1))
                if n != "o":
                    released[W["w1", n]] = after("attn1")
        if LAYERS > 5:
            for i in range(4):
                released[W["fc", i]] = after("turn_mlp", 2 * (i + 1))
                released[W["proj", i]] = after("turn_mlp", 8 + 2 * (i + 1))
        y_base, n_y = {}, 0
        for name, passes, n in (("ln0", 2, 4), ("attn0", 2, 4), ("mix", 2, 4), ("window", 2, 4), ("attn1", 2, 4), ("mlp", 2, 4)):
            y_base[name] = (n_y, n)
            n_y += passes * n

        def xviews(nkt):
            n = nkt * P
            full = nkt > TAIL_TILES
            v = {"full": full, "nkt": nkt, "n": n, "chunks": (nkt + 3) // 4, "m0": 0 if full else (FULL_TILES - 1 - TAIL_TILES) * P}
            at = 32

            def put(key, kb, dt, pattern=None, **dims):
                nonlocal at
                v[key] = carve(big, at, kb, dt, pattern, **dims)
                at += kb
            kb = n / 512
            put("KA", kb, BF16)
            put("KB", kb, BF16)
            put("V", kb, F32, "p (t e) -> p t e", e=XD)
            put("mb", kb, BF16)
            shared = at
            put("ctx", 8, F32, "p (t n) -> p t n", t=4)
            put("cT_hi", 4, BF16, "p (k n) -> p k n", k=KC)
            put("cT_lo", 4, BF16, "p (k n) -> p k n", k=KC)
            if full:
                v["P"] = carve(big, shared, n / 256, F32, "p (i n) -> p i n", i=1)
                v["PT"] = carve(big, shared + n / 256, 4, F32, "p (i t q) -> p i t q", i=2, t=4)
            else:
                put("P", n / 256 * 2, F32, "p (i n) -> p i n", i=2)
                put("PT", 4, F32, "p (i t q) -> p i t q", i=2, t=4)
            put("O", 2, F32, "p (j d) -> p j d", j=8)
            for key in ("KA", "KB", "V", "mb"):
                v[key] = [v[key]]
            if not full:
                v["KA"].append(carve(big, at, 1, BF16))
                v["KB"].append(carve(big, at + 1, 1, BF16))
                v["V"].append(spare.rearrange("p (t e) -> p t e", e=XD))
                v["mb"].append(carve(side, 6.25, 1, BF16))
                at += 2
            assert at <= 64, at
            return v


        XN = {n: sem("x_" + n) for n in (
            "ctx_loaded",
            "ctx_zero",
            "ctx_norm",
            "ctx_turned",
            "ctx_hi", "ctx_lo",
            "shared_ready",
            "shared_free",
            "k_hi", "v_mm", "v_copied", "s_mm", "s_max", "exp", "p_turned", "p_act", "p_dve", "pv", "o_norm",
            "ot_hi", "g_loaded", "g_summed")}
        norm_step, max_step, end_step = map(sem, ("norm_step", "max_step", "end_step"))

        def x_wait(eng, name, n):
            eng.wait_ge(XN[name], n + 1)

        def xmap(nkt):
            v = xviews(nkt)
            v["tiles_of"] = [range(4 * c, min(4 * c + 4, nkt)) for c in range(v["chunks"])]
            v["S"] = (lambda j: psum[:, 0:4].rearrange("p a n -> p (a n)")[:, 0:v["n"]]) if v["full"] \
                else (lambda j: psum[:, j % 2])
            v["PTbank"] = (lambda w: psum[:, 6 + w % 2]) if v["full"] else (lambda w: psum[:, 2 + w % 2])
            v["groups"] = 8 * v["chunks"]

            def keys_at(b, c):
                if v["full"]:
                    return b * (2 * v["chunks"] + 2) + 2 * c
                return 0 if isinstance(b, int) and b == 0 else 4 * b - 2

            def outs_at(b):
                if v["full"]:
                    return b * (2 * v["chunks"] + 2) + 2 * v["chunks"]
                return 4 * b + 2 if isinstance(b, int) and b == B - 1 else 4 * b + 4
            v["keys_at"], v["outs_at"] = keys_at, outs_at
            return v
        O_BANK, SHARED, V_BANK = psum[:, 4], psum[:, 5], psum[:, 6]

        def batches(eng, nkt, keys, tiles, ends):
            if nkt > TAIL_TILES:
                with eng.Fori(0, B) as b:
                    for _ in keys(b, 0):
                        pass
                    for j in range(-1, 8):
                        tiles(b, 0, j)
                    for _ in ends(b, 0):
                        pass
                return

            def batch(b, i, first=False, last=False):
                k = iter(()) if last else keys(b + 1, 1 - i)
                e = iter(()) if first else ends(b - 1, 1 - i)
                for j in range(8):
                    tiles(b, i, j)
                    next(e, None)
                    next(k, None)
                for _ in e:
                    pass
                assert next(k, "none") == "none"

            for _ in keys(0, 0):
                pass
            tiles(0, 0, -1)
            batch(0, 0, first=True)
            with eng.Fori(0, B // 2 - 1) as pair:
                batch(2 * pair + 1, 1)
                batch(2 * pair + 2, 0)
            batch(B - 1, 1, last=True)
            for _ in ends(B - 1, 1):
                pass

        block = ctx.enter_context(nc.Block())

        @block.sync
        def _(sp):
            def stage_block(e):
                i = staged_order.index(e)
                if i >= STAGED:
                    sp.wait_ge(pool_split, i - STAGED + 1)
                sp.dma_start(stage[:, i % STAGED], entries[e][1]).then_inc(stage_loaded[i % STAGED], 16)

            def across(v, n=P):
                return v.rearrange("(a n) -> a n", a=1).to_broadcast([n, v.shape[0]])

            for t in range(T):
                sp.dma_start(X[:, t], a["x"][2 * t:2 * t + 2].rearrange("b s d -> (b s) d")).then_inc(x_loaded, 16)
            sp.dma_start(gamma_row, across(a["L0_xattn_gamma"])).then_inc(gamma_loaded, 16)
            with nc.allow_non_contiguous_dma(reason="short vectors as columns"):
                for c, src in ((C_CGAMMA, a["L0_xattn_ctx_gamma"]), (C_BQ0, a["L0_attn_bq"]), (C_BK0, a["L0_attn_bk"]),
                               (C_BQ1, a["L1_attn_b_qkv"][0:D]), (C_BK1, a["L1_attn_b_qkv"][D:2 * D]),
                               (C_MUR, a["L0_ffn_mu_r"]), (C_MUK, a["L0_ffn_mu_k"])):
                    sp.dma_start(cols[:, c:c + KC], src.rearrange("(k p) -> p k", p=P)).then_inc(cols_loaded, 16)
                sp.dma_start(cols[:, C_GAIN:C_GAIN + 1], across(a["L1_xattn_gain"])).then_inc(cols_loaded, 16)
                sp.dma_start(cols[:, C_CW:C_CW + 2], across(a["L1_xattn_council_weights"])).then_inc(cols_loaded, 16)
            stage_block(staged_order[0])
            stage_block(staged_order[1])
            sp.dma_start(wkv_f, a["L0_xattn_Wkv"].rearrange("(k p) n -> p k n", p=P)).then_inc(wkv_loaded, 16)
            sp.dma_start(mask_i[0:B, 0:SCTX], a["mask_BxS2_ik0"]).then_inc(mask_loaded, 16)
            for e in staged_order[2:before_x]:
                stage_block(e)

            fc_rows = a["L1_ffn_W_fc"].rearrange("(b p) n -> b p n", p=P)
            proj_rows = a["L1_ffn_W_proj"].rearrange("d (c n) -> (d c) n", n=D).rearrange("(b p) n -> b p n", p=P)

            def context(nkt):
                v = xmap(nkt)
                with sp.Fori(0, B) as b:
                    if LAYERS > 5:
                        x_wait(sp, "g_summed", b)
                        settle(sp)
                        for w, r in enumerate((fc_rows, proj_rows)):
                            sp.dma_start(ybuf[:, w], r[bass.ds(b, 1)].rearrange("b p n -> (b p) n"))\
                                .then_inc(XN["g_loaded"], 16)
                    for c, tiles in enumerate(v["tiles_of"]):
                        x_wait(sp, "ctx_turned", b * nkt + tiles[0])
                        settle(sp)
                        if v["full"] and c == 0:
                            x_wait(sp, "pv", b * v["groups"])
                            settle(sp)
                        for kt in tiles:
                            src = a["ctx_1024"][bass.ds(b, 1)].rearrange("b s d -> (b s) d")
                            if kt == FULL_TILES - 1:
                                x_wait(sp, "ctx_zero", b + 1)
                                settle(sp)
                                sp.dma_start(v["ctx"][0:HEAD_ROWS, kt % 4], src[0:HEAD_ROWS]).then_inc(XN["ctx_loaded"], 16)
                            else:
                                r0 = HEAD_ROWS + kt * P if v["full"] else SCTX - TAIL + kt * P
                                sp.dma_start(v["ctx"][:, kt % 4], src[r0:r0 + P]).then_inc(XN["ctx_loaded"], 16)

            sp.wait_ge(flag_ready, 1)
            sp.wait_ge(*after("q"))
            head_rows_used = sp.value_load(flag[0:1, 0:1], min_val=0, max_val=1)
            with sp.If(head_rows_used > 0):
                context(FULL_TILES)
            with sp.If(head_rows_used < 1):
                context(TAIL_TILES)

            def load_bias(n, v_src, o_src):
                if n:
                    sp.wait_ge(layer_done, 2)
                sp.wait_ge(*after("ff", 4))
                for m in range(2):
                    sp.dma_start(bv[64 * m:64 * m + 64], v_src.rearrange("(a j m e) -> a m j e", a=1, j=2, m=2)[:, m]
                                 .to_broadcast([64, 2, P])).then_inc(bias_loaded, 16)
                sp.dma_start(bo, across(o_src)).then_inc(bias_loaded, 16)

            for e in staged_order[before_x:]:
                if LAYERS > 1 and e == W["w0", "o"]:
                    load_bias(0, a["L0_attn_bv"], a["L0_attn_bo"])
                if LAYERS > 3 and e == W["win", "Wqj"]:
                    sp.wait_ge(layer_done, 1)
                    for b2 in range(2):
                        src = a["itok_BxS_0_7"].rearrange("(a t c) s -> c a t s", a=1, c=2)[b2]
                        sp.dma_start(ids_rows[64 * b2:64 * b2 + 64], src.to_broadcast([64, T, S])).then_inc(ids_loaded, 16)
                    with nc.allow_non_contiguous_dma(reason="a pointer per token"):
                        sp.dma_start(ptr[:, 0:T], a["itok_BxS_0_4092"].rearrange("(t c) s -> (c s) t", c=2))\
                            .then_inc(ids_loaded, 16)
                if LAYERS > 4 and e == W["w1n", "o"]:
                    load_bias(1, a["L1_attn_b_qkv"][2 * D:3 * D], a["L1_attn_b_out"])
                stage_block(e)
            if LAYERS > 5:
                sp.wait_ge(layer_done, 5)
                sp.dma_start(lnw, across(a["L1_ffn_ln_w"])).then_inc(bias_loaded, 16)
                sp.dma_start(lnb, across(a["L1_ffn_ln_b"])).then_inc(bias_loaded, 16)
            sp.wait_ge(layer_done, LAYERS)
            for t in range(T):
                sp.dma_start(out[2 * t:2 * t + 2].rearrange("b s d -> (b s) d"), X[:, t]).then_inc(out_stored, 16)
            sp.wait_ge(out_stored, 16 * T)

        @block.gpsimd
        def _(pool):
            for name, semaphore in XN.items():
                if name not in ("ctx_loaded", "g_loaded"):
                    pool.sem_inc(semaphore, 1)
            pool.sem_inc(prod_lo, 1)
            consts = [0]

            def const(ins, wait=False):
                consts[0] += 1
                ins.then_inc(const_ready, 1)
                if wait:
                    pool.wait_ge(const_ready, consts[0])

            const(pool.memset(ident[:], 0.0), wait=True)
            const(pool.affine_select(out=ident[:], in_=ident[:], compare_op=ALU.not_equal, fill=1.0, base=0,
                                     pattern=[[-1, P]], channel_multiplier=1), wait=True)
            const(pool.tensor_copy(identb[:], ident[:]))
            const(pool.memset(ones[:], 1.0))
            const(pool.memset(small[:, 153:154], 0.0))
            const(pool.memset(causal[:], 0.0), wait=True)
            for b2 in range(2):
                part = causal[64 * b2:64 * b2 + 64]
                const(pool.affine_select(out=part, in_=part, compare_op=ALU.is_ge, fill=NEG, base=0,
                                         pattern=[[-1, S]], channel_multiplier=1), wait=True)
                const(pool.iota(tile_base[64 * b2:64 * b2 + 64], pattern=[[2 * SCTX, T]], base=b2 * SCTX,
                                channel_multiplier=0), wait=True)
            const(pool.iota(key_no[:], pattern=[[1, S]], base=0, channel_multiplier=0))
            assert consts[0] == CONSTS

            def split(e):
                i = staged_order.index(e)
                src = stage[:, i % STAGED]
                pool.wait_ge(stage_loaded[i % STAGED], 16 * (i // STAGED + 1))
                wait_slot(pool, e)
                hi, lo = ring_hi[:, e % RING], ring_lo[:, e % RING]
                if entries[e][0] == "n":
                    pool.tensor_tensor(hi, src, small[:, 153:154].unsqueeze(2).to_broadcast([P, KC, D]), ALU.add)\
                        .then_inc(pool_part, 1)
                    parts[0] += 1
                    pool.wait_ge(pool_part, parts[0])
                    pool.tensor_tensor(lo, src, hi, ALU.subtract).then_inc(pool_split, 1)
                else:
                    w = 0 if e < W["proj", 0] else 1
                    if e == W["fc", 0]:
                        pool.wait_ge(thr_ready, 1)
                    pool.tensor_scalar(hi, src, thr[:, w:w + 1], None, ALU.is_gt).then_inc(pool_part, 1)
                    pool.tensor_scalar(lo, src, nthr[:, w:w + 1], None, ALU.is_lt).then_inc(pool_part, 1)
                    parts[0] += 2
                    pool.wait_ge(pool_part, parts[0])
                    pool.tensor_tensor(hi, hi, lo, ALU.subtract).then_inc(pool_split, 1)

            parts = [0]
            ctx_rows = a["ctx_1024"].rearrange("b s d -> (b s) d")

            def gather(h):
                for u in range(HT):
                    for w in range(3):
                        idx = row_of.rearrange("p (t w) -> p t w", w=4)[:, 4 * h + u, w:w + 1]
                        pool.indirect_dma_start(win[:, u, w, :], None, ctx_rows,
                                                bass.IndirectOffsetOnAxis(ap=idx.bitcast(mybir.dt.uint32), axis=0))\
                            .then_inc(win_loaded, 16)

            def window_gathers():
                pool.wait_ge(rows_ready, 1)
                gather(0)
                pool.wait_ge(comb_ready, 2 * HT)
                gather(1)

            for e in staged_order:
                if LAYERS > 3 and e == W["win", "Wvi"] + 1:
                    window_gathers()
                split(e)
            if LAYERS == 4:
                window_gathers()
            if LAYERS > 5:
                pool.wait_ge(bias_loaded, 16 * 8)
                with pool.Fori(0, 2) as h:
                    for u in range(HT):
                        x = hid[:, u % 2]
                        pool.wait_ge(hid_norm, h * HT + u + 1)
                        pool.tensor_tensor(x, x, lnw, ALU.mult).then_inc(hid_scaled, 1)
                        pool.wait_ge(hid_scaled, h * HT + u + 1)
                        pool.tensor_tensor(x, x, lnb, ALU.add).then_inc(hid_ready, 1)

        @block.tensor
        def _(pe):
            pe.wait_ge(const_ready, CONSTS)

            def product(bank, terms):
                passes = []
                for (lh, ll), (rh, rl) in terms:
                    passes.append((lh, rh))
                    if rl is not None:
                        passes.append((lh, rl))
                    if ll is not None:
                        passes.append((ll, rh))
                for n, (l, r) in enumerate(passes):
                    ins = pe.matmul(bank, l, r, start=n == 0, stop=n == len(passes) - 1)
                return ins

            def cut(pair, f):
                return tuple(None if x is None else f(x) for x in pair)

            def turn_tile(bank, tile):
                for k in range(KC):
                    ins = pe.transpose(bank[:, k * P:(k + 1) * P], tile[:, k * P:(k + 1) * P], ident[:])
                return ins

            def turn_y(g, name, i):
                base, n = y_base[name]
                for u in range(HT):
                    bank = g.open()
                    pe.wait_ge(y_ready, base + i * n + u + 1)
                    turn_tile(bank, ybuf[:, u % 2]).then_inc(group_ready, 1)

            def turn_block(g, pair):
                for x in pair:
                    for z in range(2):
                        bank = g.open().bitcast(BF16).rearrange("p (c n) -> p c n", c=2)
                        for c2 in range(2):
                            for c in range(KC):
                                ins = pe.transpose(bank[:, c2, c * P:(c + 1) * P],
                                                   x[:, c, (2 * z + c2) * P:(2 * z + c2 + 1) * P], identb[:])
                        ins.then_inc(group_ready, 1)

            with pe.Fori(0, 2) as h:
                g = Pass(pe, "ln0", h)
                turn_y(g, "ln0", h)
            Pass(pe, "q").all_free()
            for i in range(2):
                wait_split(pe, ("q", i))
                w = w_of(("q", i))
                with pe.Fori(0, 2) as mp:
                    g = Pass(pe, "q", 2 * i + mp)
                    for mm in range(2):
                        for hf in range(2):
                            bank = g.open()
                            product(bank, [(cut(w, lambda x: x[:, k, bass.ds(mp * 256 + mm * P, P)]),
                                            cut(yT, lambda x: x[:, k, hf * 512:(hf + 1) * 512])) for k in range(KC)])\
                                .then_inc(group_ready, 1)

            pe.wait_ge(flag_part, 1)
            Pass(pe, "ff").all_free()
            pe.matmul(SHARED[:, 0:1], ones[0:B, :], small[0:B, 152:153], start=True, stop=True).then_inc(XN["shared_ready"], 1)

            def attend(nkt):
                v = xmap(nkt)
                W_, ch = v["groups"], v["chunks"]
                cT = (v["cT_hi"], v["cT_lo"])

                def open_shared(n):
                    x_wait(pe, "shared_free", n + 1)
                    return SHARED

                def keys(b, i):
                    if v["full"]:
                        x_wait(pe, "p_act", b * (W_ // 2))
                        x_wait(pe, "p_dve", b * (W_ // 2))
                    for c, tiles in enumerate(v["tiles_of"]):
                        n = len(tiles)
                        if not v["full"]:
                            yield
                            yield
                            yield
                        for kt in tiles:
                            if kt == tiles[0]:
                                x_wait(pe, "v_copied", b * ch + c)
                            x_wait(pe, "ctx_lo", b * nkt + max(kt - 1, 0))
                            x_wait(pe, "ctx_norm", b * nkt + kt + 1)
                            turn_tile(psum[:, 6 + kt % 2], v["ctx"][:, kt % 4]).then_inc(XN["ctx_turned"], 1)
                            if kt % 2:
                                yield
                        bank = open_shared(v["keys_at"](b, c))
                        settle(pe)
                        pe.matmul(bank[:, 0:n * P], identb[0:B, bass.ds(b, 1)].to_broadcast([B, P]),
                                  maskadd[0:B, v["m0"] + tiles[0] * P:v["m0"] + tiles[0] * P + n * P],
                                  start=True, stop=True).then_inc(XN["shared_ready"], 1)
                        yield
                        x_wait(pe, "ctx_lo", b * nkt + tiles[0] + n)
                        bank = open_shared(v["keys_at"](b, c) + 1)
                        product(bank[:, 0:n * P], [(cut(wk, lambda x: x[:, k, :]), cut(cT, lambda x: x[:, k, 0:n * P]))
                                                   for k in range(KC)]).then_inc(XN["shared_ready"], 1)
                        for u in range(n):
                            ins = product(V_BANK[:, u * XD:(u + 1) * XD],
                                          [(cut(cT, lambda x: x[:, k, u * P:(u + 1) * P]), cut(wv, lambda x: x[:, k, :]))
                                           for k in range(KC)])
                        ins.then_inc(XN["v_mm"], 1)

                def scores(b, i, j):
                    if j == 0:
                        x_wait(pe, "shared_free", v["keys_at"](b, ch - 1) + 3)
                    x_wait(pe, "s_max", b * 8 + j if v["full"] else
                           0 if isinstance(b, int) and b == 0 and j == 0 else b * 8 + j - 1)
                    S = v["S"](j)
                    q = Q[:, bass.ds(b, 1), 2 * j:2 * j + 2, :].rearrange("p b h s -> p (b h s)")
                    for tiles in v["tiles_of"]:
                        c0, c1 = tiles[0] * P, (tiles[-1] + 1) * P
                        pe.matmul(S[:, c0:c1], q, v["KA"][i][:, c0:c1], start=True, stop=False)
                        ins = pe.matmul(S[:, c0:c1], q, v["KB"][i][:, c0:c1], start=False, stop=True)
                    ins.then_inc(XN["s_mm"], 1)

                def turn_p(b, j, c):
                    w = j * ch + c
                    if c == 0:
                        x_wait(pe, "exp", b * 8 + j + 1)
                    if w == 0 and v["full"]:
                        x_wait(pe, "v_copied", (b + 1) * ch)
                    x_wait(pe, "p_dve" if w % 2 else "p_act", b * (W_ // 2) + w // 2)
                    bank = v["PTbank"](w)
                    for n, kt in enumerate(v["tiles_of"][c]):
                        ins = pe.transpose(bank[:, n * P:(n + 1) * P],
                                           v["P"][:, j % v["P"].shape[1], kt * P:(kt + 1) * P], ident[:])
                    ins.then_inc(XN["p_turned"], 1)

                def values(b, i, j, c):
                    w = j * ch + c
                    if w == 0:
                        x_wait(pe, "v_copied", (b + 1) * ch)
                        x_wait(pe, "o_norm", b)
                    x_wait(pe, "p_dve" if w % 2 else "p_act", b * (W_ // 2) + w // 2 + 1)
                    for n, kt in enumerate(v["tiles_of"][c]):
                        ins = pe.matmul(O_BANK[:, j * XD:(j + 1) * XD], v["PT"][:, w % 2, n, :], v["V"][i][:, kt, :],
                                        start=kt == 0, stop=kt == nkt - 1)
                    ins.then_inc(XN["pv"], 1)

                before = [None]

                def tiles(b, i, j):
                    if v["full"]:
                        if j < 7:
                            if j >= 0:
                                for c in range(ch):
                                    turn_p(b, j, c)
                                    if before[0]:
                                        values(*before[0])
                                    before[0] = (b, i, j, c)
                            scores(b, i, j + 1)
                        else:
                            for c in range(ch):
                                turn_p(b, j, c)
                                values(*before[0])
                                before[0] = (b, i, j, c)
                            values(*before[0])
                            before[0] = None
                        return
                    if j < 7:
                        scores(b, i, j + 1)
                    elif not (isinstance(b, int) and b == B - 1):
                        scores(b + 1, 1 - i, 0)
                    if j < 0:
                        return
                    turn_p(b, j, 0)
                    if j > 0:
                        values(b, i, j - 1, 0)
                    elif not (isinstance(b, int) and b == 0):
                        values(b - 1, 1 - i, 7, 0)

                def ends(b, i):
                    if not v["full"] and isinstance(b, int) and b == B - 1:
                        values(b, 1, 7, 0)
                    if not v["full"]:
                        yield
                    x_wait(pe, "o_norm", b + 1)
                    for half in range(2):
                        bank = open_shared(v["outs_at"](b) + half)
                        settle(pe)
                        for jj in range(4):
                            ins = pe.transpose(bank[0:XD, jj * P:(jj + 1) * P], v["O"][:, 4 * half + jj, :], ident[:])
                        ins.then_inc(XN["shared_ready"], 1)
                        yield

                batches(pe, nkt, keys, tiles, ends)

            pe.wait_ge(flag_ready, 1)
            head_rows_used = pe.value_load(flag[0:1, 0:1], min_val=0, max_val=1)
            with pe.If(head_rows_used > 0):
                attend(FULL_TILES)
            with pe.If(head_rows_used < 1):
                attend(TAIL_TILES)

            pe.wait_ge(x_attended, 1)
            for i in range(4):
                wait_split(pe, ("ffg", i))
                wa, wg = w_of(("ffa", i)), w_of(("ffg", i))
                with pe.Fori(0, 4) as m:
                    g = Pass(pe, "ff", 4 * i + m)
                    for hf in range(2):
                        for w in (wa, wg):
                            bank = g.open()
                            product(bank, [(cut(w, lambda x: x[:, k, bass.ds(m * P, P)]),
                                            cut(yT, lambda x: x[:, k, hf * 512:(hf + 1) * 512])) for k in range(KC)])\
                                .then_inc(group_ready, 1)
            pe.wait_ge(prod_lo, 33)
            wait_split(pe, ("ff2", 3))
            with pe.Fori(0, 2) as h:
                g = Pass(pe, "xout", h)
                for u in range(HT):
                    bank = g.open()
                    terms = []
                    for c in range(24):
                        src, w = (oT, w_of(("xo", c // 4))) if c < 8 else (ffT, w_of(("ff2", (c - 8) // 4)))
                        cc = c if c < 8 else c - 8
                        terms.append((cut(src, lambda x: x[:, cc, bass.ds(h * 512 + u * P, P)]),
                                      cut(w, lambda x: x[:, c % 4, :])))
                    product(bank, terms).then_inc(group_ready, 1)
            if LAYERS > 5:
                g = Pass(pe, "gamma")
                bank = g.open()
                pe.wait_ge(gamma_part, 1)
                pe.matmul(bank[:, 0:2], ones[:], gtot, start=True, stop=True).then_inc(group_ready, 1)

            def attention(n, name):
                wq, wk_, wv_ = (w_of((f"w{n}", x)) for x in "qkv")
                wo = woT if n else w_of(("w0", "o"))
                if not n:
                    wait_split(pe, ("w0", "o"))
                with pe.Fori(0, 2) as h:
                    g = Pass(pe, name, h)
                    turn_y(g, name, h)
                    g.wait_done(3)
                    for w in (wq, wk_):
                        for m in range(KC):
                            bank = g.open()
                            product(bank, [(cut(w, lambda x: x[:, k, m * P:(m + 1) * P]), cut(yh, lambda x: x[:, k, :]))
                                           for k in range(KC)]).then_inc(group_ready, 1)
                    wv4 = cut(wv_, lambda x: x.rearrange("p k (j m e) -> p k j m e", j=2, m=2))
                    for u in range(HT):
                        bank = g.open()
                        for m in range(2):
                            for b2 in range(2):
                                t0 = u * P + b2 * S
                                ins = product(bank[64 * m:64 * m + 64, b2 * 256:(b2 + 1) * 256],
                                              [(cut(yh, lambda x: x[:, k, t0:t0 + S]), cut(wv4, lambda x: x[:, k, :, m, :]))
                                               for k in range(KC)])
                        ins.then_inc(group_ready, 1)

                    def scores(u):
                        for r in range(4):
                            bank = g.open()
                            if u == 0 and r == 0:
                                g.wait_done(11)
                            for m in range(4):
                                for b2 in range(2):
                                    t0 = u * P + b2 * S
                                    f = lambda x: x[32 * r:32 * r + 32, m, t0:t0 + S]
                                    ins = product(bank[64 * b2:64 * b2 + 64, m * S:(m + 1) * S], [(cut(qh, f), cut(kh, f))])
                            ins.then_inc(group_ready, 1)

                    scores(0)
                    for u in range(HT):
                        if u + 1 < HT:
                            scores(u + 1)
                        pe.wait_ge(p_exp, (n * 2 + h) * HT + u + 1)
                        for j in range(2):
                            bank = g.open()
                            for r in range(4):
                                ins = pe.transpose(bank[:, r * P:(r + 1) * P],
                                                   prob[:, u % 2, r, 2 * j:2 * j + 2, :].rearrange("p m s -> p (m s)"), ident[:])
                            ins.then_inc(group_ready, 1)
                        pt = g.at - 1
                        bank = g.open()
                        if u == 0:
                            pe.wait_ge(v_done, (n * 2 + h) * HT + HT)
                        g.wait_done(pt)
                        for j in range(2):
                            for r in range(4):
                                for b2 in range(2):
                                    o = bank.rearrange("p (j m r d) -> p j m r d", j=2, m=2, r=4)[64 * b2:64 * b2 + 64, j, :, r, :]
                                    ins = product(o, [(cut(pT, lambda x: x[:, u % 2, 4 * j + r, b2 * S:(b2 + 1) * S]),
                                                       cut(vb, lambda x: x[:, 2 * u + b2, 4 * j + r]))])
                        ins.then_inc(group_ready, 1)
                        o_group = g.at - 1
                        bank = g.open()
                        g.wait_done(o_group)
                        turn_tile(bank, ybuf[:, u % 2]).then_inc(group_ready, 1)
                    last = g.at - 1
                    for u in range(HT):
                        bank = g.open()
                        if u == 0:
                            g.wait_done(last)
                        product(bank, [(cut(ah, lambda x: x[:, k, u * P:(u + 1) * P]), cut(wo, lambda x: x[:, k, :]))
                                       for k in range(KC)]).then_inc(group_ready, 1)

            if LAYERS > 1:
                attention(0, "attn0")

            if LAYERS > 2:
                g = Pass(pe, "turn_mix")
                for n in "rkv":
                    wait_split(pe, ("mixn", n))
                    turn_block(g, w_of(("mixn", n)))
                wr, wk2, wv2 = (w_of(("mix", n)) for n in "rkv")
                with pe.Fori(0, 2) as h:
                    g = Pass(pe, "mix", h)
                    turn_y(g, "mix", h)
                    for u in range(HT):
                        bank = g.open()
                        if u == 0:
                            pe.wait_ge(mix_lo, 8 * h + 4)
                        product(bank, [(cut(mixT[0], lambda x: x[:, k, u * P:(u + 1) * P]), cut(wr, lambda x: x[:, k, :]))
                                       for k in range(KC)]).then_inc(group_ready, 1)
                    pe.wait_ge(mix_lo, 8 * h + 8)
                    for m in range(KC):
                        bank = g.open()
                        product(bank, [(cut(wk2, lambda x: x[:, k, m * P:(m + 1) * P]), cut(mixT[1], lambda x: x[:, k, :]))
                                       for k in range(KC)]).then_inc(group_ready, 1)
                    for u in range(HT):
                        bank = g.open()
                        if u == 0:
                            pe.wait_ge(relu_lo, 4 * h + 4)
                        product(bank, [(cut(kact, lambda x: x[:, k, u * P:(u + 1) * P]), cut(wv2, lambda x: x[:, k, :]))
                                       for k in range(KC)]).then_inc(group_ready, 1)

            if LAYERS > 3:
                g = Pass(pe, "fold")

                def weights_product(left, right):
                    for m in range(KC):
                        bank = g.open()
                        product(bank, [(cut(left, lambda x: x[:, k, m * P:(m + 1) * P]), cut(right, lambda x: x[:, k, :]))
                                       for k in range(KC)]).then_inc(group_ready, 1)

                for s in "ji":
                    wait_split(pe, ("win", "Wk" + s))
                    weights_product(w_of(("win", "Wq" + s)), w_of(("win", "Wk" + s)))
                wait_split(pe, ("win", "Wout"))
                turn_block(g, w_of(("win", "Wout")))
                g.wait_done(10)
                g.wait_done(11)
                for s in "ji":
                    wait_split(pe, ("win", "Wv" + s))
                    weights_product(w_of(("win", "Wv" + s)), w_of(("win", "WoutT")))
                with pe.Fori(0, 2) as h:
                    g = Pass(pe, "window", h)
                    turn_y(g, "window", h)
                    for u in range(HT):
                        for s in range(2):
                            bank = g.open()
                            g.wait_done(u)
                            product(bank, [(cut(yh, lambda x: x[:, k, u * P:(u + 1) * P]), cut(fold[s], lambda x: x[:, k, :]))
                                           for k in range(KC)]).then_inc(group_ready, 1)
                    for n in range(2 * HT):
                        bank = g.open()
                        pe.wait_ge(comb_ready, h * 2 * HT + n + 1)
                        turn_tile(bank, comb[:, n % 2]).then_inc(group_ready, 1)
                    last = g.at - 1
                    for u in range(HT):
                        bank = g.open()
                        if u == 0:
                            g.wait_done(last)
                        product(bank, [(cut(src, lambda x: x[:, k, u * P:(u + 1) * P]), cut(fold[2 + s], lambda x: x[:, k, :]))
                                       for s, src in enumerate((yh, y2)) for k in range(KC)]).then_inc(group_ready, 1)

            if LAYERS > 4:
                g = Pass(pe, "turn_w1")
                for n in "qkvo":
                    wait_split(pe, ("w1n", n))
                    turn_block(g, w_of(("w1n", n)))
                attention(1, "attn1")

            if LAYERS > 5:
                g = Pass(pe, "turn_mlp")
                for kind in ("fc", "proj"):
                    for i in range(4):
                        wait_split(pe, (kind, i))
                        turn_block(g, w_of((kind, i))[:1])
                with pe.Fori(0, 2) as h:
                    g = Pass(pe, "mlp", h)
                    turn_y(g, "mlp", h)

                    def hidden(u):
                        for n in range(4):
                            bank = g.open()
                            if u == 0 and n == 0:
                                g.wait_done(3)
                            product(bank, [(cut(yh, lambda x: x[:, k, u * P:(u + 1) * P]), (fcT[:, n, k, :], None))
                                           for k in range(KC)]).then_inc(group_ready, 1)

                    hidden(0)
                    for u in range(HT):
                        if u + 1 < HT:
                            hidden(u + 1)
                        pe.wait_ge(hid_ready, h * HT + u + 1)
                        for n in range(4):
                            turn_tile(g.open(), hid[:, u % 2, n * 512:(n + 1) * 512]).then_inc(group_ready, 1)
                        last = g.at - 1
                        bank = g.open()
                        g.wait_done(last)
                        product(bank, [(cut(hT[u % 2], lambda x: x[:, c, :]), (projT[:, c, :], None)) for c in range(FF // P)])\
                            .then_inc(group_ready, 1)

        @block.scalar
        def _(act):
            for _ in range(ACT_CREDIT):
                act.drain().then_inc(act_freed, 1)
            act.wait_ge(const_ready, CONSTS)

            def copy_hi(dst, bank, g_=None, **kw):
                return act.activation(dst, bank, ACT.Copy, **kw)

            def quad(bank):
                return bank.rearrange("p (k n) -> p k n", k=KC)

            def hi_of_tile(g, i, dst):
                copy_hi(dst, quad(g.take(i))).then_inc(act_hi, 1)

            def turned_half(g):
                for u in range(HT):
                    hi_of_tile(g, u, yh[0][:, :, u * P:(u + 1) * P])

            def copy_turned(g, i, dst):
                act.activation(dst, g.take(i).bitcast(BF16).rearrange("p (c n) -> p c n", c=2), ACT.Copy).then_inc(act_freed, 1)

            with act.Fori(0, 2) as h:
                g = Pass(act, "ln0", h)
                for u in range(HT):
                    hi_of_tile(g, u, yT[0][:, :, bass.ds(h * 512 + u * P, P)])
            for i in range(2):
                with act.Fori(0, 2) as mp:
                    g = Pass(act, "q", 2 * i + mp)
                    for mm in range(2):
                        for hf in range(2):
                            bank = g.take(2 * mm + hf)
                            for h2 in range(2):
                                dst = Q[0:64, hf * 8:hf * 8 + 8, bass.ds(i * 8 + mp * 4 + mm * 2 + h2, 1), :]
                                ins = act.activation(dst.rearrange("p b h s -> p b (h s)"),
                                                     bank[64 * h2:64 * h2 + 64].rearrange("p (b s) -> p b s", b=8),
                                                     ACT.Copy, scale=XD ** -0.5)
                            ins.then_inc(act_hi, 1)

            def attend(nkt):
                v = xmap(nkt)
                W_, ch = v["groups"], v["chunks"]

                def keys(b, i):
                    for c, tiles in enumerate(v["tiles_of"]):
                        n = len(tiles)
                        if not v["full"]:
                            yield
                        if LAYERS > 5 and c == 0:
                            act.wait_ge(XN["g_loaded"], 32 * (b + 1))
                            for w in range(2):
                                ins = act.activation(ybuf[:, w], ybuf[:, w], ACT.Abs, accum_out=gsum[:, w, bass.ds(b, 1)])
                            ins.then_inc(XN["g_summed"], 1)
                        if not v["full"]:
                            yield
                            yield
                        for kt in tiles:
                            x_wait(act, "ctx_turned", b * nkt + kt + 1)
                            u = kt % 4
                            copy_hi(v["cT_hi"][:, :, u * P:(u + 1) * P], quad(psum[:, 6 + kt % 2])).then_inc(XN["ctx_hi"], 1)
                            if kt % 2:
                                yield
                        cols_ = slice(tiles[0] * P, (tiles[-1] + 1) * P)
                        x_wait(act, "shared_ready", v["keys_at"](b, c) + 2)
                        copy_hi(v["mb"][i][:, cols_], SHARED[:, 0:n * P]).then_inc(XN["shared_free"], 1)
                        yield
                        x_wait(act, "shared_ready", v["keys_at"](b, c) + 3)
                        copy_hi(v["KA"][i][:, cols_], SHARED[:, 0:n * P]).then_inc(XN["k_hi"], 1)
                        x_wait(act, "v_mm", b * ch + c + 1)
                        copy_hi(v["V"][i][:, tiles[0]:tiles[-1] + 1, :],
                                V_BANK[:, 0:n * XD].rearrange("p (t e) -> p t e", e=XD)).then_inc(XN["v_copied"], 1)

                def exp(b, i, j):
                    p = v["P"][:, j % v["P"].shape[1], :]
                    x_wait(act, "s_max", b * 8 + j + 1)
                    act.activation(p, p, ACT.Exp, bias=xq_neg[:, i, j:j + 1], accum_out=xq_sum[:, i, j:j + 1])\
                        .then_inc(XN["exp"], 1)

                def copies(b, j):
                    for c in range(ch):
                        w = j * ch + c
                        if w % 2 == 0:
                            n = len(v["tiles_of"][c])
                            x_wait(act, "p_turned", b * W_ + w + 1)
                            if v["full"]:
                                x_wait(act, "pv", b * W_ + max(w - 1, 0))
                            else:
                                x_wait(act, "pv", 0 if w == 0 and isinstance(b, int) and b == 0 else b * W_ + w - 1)
                            copy_hi(v["PT"][:, 0, 0:n, :], v["PTbank"](w)[:, 0:n * P].rearrange("p (t q) -> p t q", q=P))\
                                .then_inc(XN["p_act"], 1)

                def tiles(b, i, j):
                    if v["full"] and j >= 0:
                        copies(b, j)
                    if j < 7:
                        exp(b, i, j + 1)
                    elif not v["full"] and not (isinstance(b, int) and b == B - 1):
                        exp(b + 1, 1 - i, 0)
                    if not v["full"] and j >= 0:
                        copies(b, j)

                def ends(b, i):
                    if not v["full"]:
                        yield
                    for half in range(2):
                        x_wait(act, "shared_ready", v["outs_at"](b) + half + 2)
                        bank = SHARED[0:XD].rearrange("p (j m s) -> p j m s", j=4, m=2)
                        for h2 in range(2):
                            ins = copy_hi(oT[0][64 * h2:64 * h2 + 64, 4 * half:4 * half + 4, bass.ds(b * S, S)], bank[:, :, h2, :])
                        ins.then_inc(XN["ot_hi"], 1)
                        yield

                batches(act, nkt, keys, tiles, ends)

            act.wait_ge(flag_ready, 1)
            head_rows_used = act.value_load(flag[0:1, 0:1], min_val=0, max_val=1)
            with act.If(head_rows_used > 0):
                attend(FULL_TILES)
            with act.If(head_rows_used < 1):
                attend(TAIL_TILES)

            for i in range(4):
                with act.Fori(0, 4) as m:
                    g = Pass(act, "ff", 4 * i + m)
                    for hf in range(2):
                        act.activation(ybuf[:, hf], g.take(2 * hf + 1), ACT.Silu).then_inc(act_freed, 1)
                    for hf in range(2):
                        g.wait_done(2 * hf)
                        act.activation(ffT[0][:, bass.ds(4 * i + m, 1), hf * 512:(hf + 1) * 512].rearrange("p a n -> p (a n)"),
                                       prod[:, hf], ACT.Copy).then_inc(prod_hi, 1)

            def attention(n, name):
                bq, bk = (C_BQ1, C_BK1) if n else (C_BQ0, C_BK0)
                with act.Fori(0, 2) as h:
                    g = Pass(act, name, h)
                    turned_half(g)
                    for x, (dst, bias) in enumerate(((qh, bq), (kh, bk))):
                        for m in range(KC):
                            act.activation(dst[0][:, m, :], g.take(4 + 4 * x + m), ACT.Identity,
                                           bias=cols[:, bias + m:bias + m + 1]).then_inc(act_hi, 1)
                    for u in range(HT):
                        g.wait_done(12 + u)
                        for m in range(2):
                            rows_ = slice(64 * m, 64 * m + 64)
                            ins = act.activation(vb[0][rows_, 2 * u:2 * u + 2, :, m, :],
                                                 vf[rows_, u % 2].rearrange("p (b g e) -> p b g e", b=2, g=8), ACT.Copy)
                        ins.then_inc(v_hi, 1)

                    def exp(u):
                        act.wait_ge(p_max, (n * 2 + h) * HT + u + 1)
                        p = prob[:, u % 2].rearrange("p r m s -> p (r m s)")
                        act.activation(p, p, ACT.Exp).then_inc(p_exp, 1)

                    at = 16 + 4
                    exp(0)
                    for u in range(HT):
                        if u + 1 < HT:
                            exp(u + 1)
                            at += 4
                        for j in range(2):
                            hi_of_tile(g, at + j, pT[0][:, u % 2, 4 * j:4 * j + 4, :])
                        hi_of_tile(g, at + 3, ah[0][:, :, u * P:(u + 1) * P])
                        at += 4

            if LAYERS > 1:
                attention(0, "attn0")

            if LAYERS > 2:
                g = Pass(act, "turn_mix")
                for i, n in enumerate("rkv"):
                    wait_slot(act, W["mix", n])
                    for x in range(2):
                        copy_turned(g, 4 * i + 2 * x, w_of(("mix", n))[x][:, 0:2, :])
                act.wait_ge(om_ready, 1)
                with act.Fori(0, 2) as h:
                    g = Pass(act, "mix", h)
                    for u in range(HT):
                        act.activation(zp[:, :, 2 * u:2 * u + 2, 1:], g.take(u).rearrange("p (k b s) -> p k b s", k=KC, b=2),
                                       ACT.Copy).then_inc(act_freed, 1)
                    g.wait_done(HT - 1)

                    def previous_part(n):
                        act.activation(mix_t[:, n % 2].rearrange("p (b s) -> p b s", b=8), zp[:, n % 4, :, 0:S], ACT.Copy,
                                       scale=cols[:, (C_OMR, C_OMK)[n // 4] + n % 4:(C_OMR, C_OMK)[n // 4] + n % 4 + 1])\
                            .then_inc(mix_a, 1)

                    previous_part(0)
                    for n in range(8):
                        if n < 7:
                            previous_part(n + 1)
                        act.wait_ge(mix_b, 8 * h + n + 1)
                        act.activation(mixT[n // 4][0][:, n % 4, :], mix_f[:, n % 2], ACT.Copy).then_inc(mix_hi, 1)
                    for u in range(HT):
                        act.activation(recept[:, u], g.take(4 + u), ACT.Sigmoid).then_inc(act_freed, 1)
                    for m in range(KC):
                        g.wait_done(8 + m)
                        if m >= 2:
                            act.wait_ge(relu_lo, 4 * h + m - 1)
                        act.activation(relu2[:, m % 2], relu[:, m % 2], ACT.Square).then_inc(relu_sq, 1)
                        act.activation(kact[0][:, m, :], relu[:, m % 2], ACT.Square).then_inc(relu_hi, 1)

            if LAYERS > 3:
                g = Pass(act, "fold")

                def folded(first, pair):
                    for m in range(KC):
                        copy_hi(pair[0][:, m, :], g.take(first + m)).then_inc(act_hi, 1)

                folded(0, fold[0])
                folded(4, fold[1])
                wait_slot(act, W["win", "WoutT"])
                for x in range(2):
                    copy_turned(g, 8 + 2 * x, w_of(("win", "WoutT"))[x][:, 0:2, :])
                folded(12, fold[2])
                folded(16, fold[3])
                act.wait_ge(logit, 1)
                act.activation(council[:, 4:6], council[:, 2:4], ACT.Exp).then_inc(e_ready, 1)
                with act.Fori(0, 2) as h:
                    g = Pass(act, "window", h)
                    turned_half(g)
                    act.wait_ge(logit, h + 2)
                    act.activation(sc[:, SC_E:SC_E + 6, :], sc[:, SC_E:SC_E + 6, :], ACT.Exp).then_inc(e_ready, 1)
                    for n in range(2 * HT):
                        u = n // 2
                        hi_of_tile(g, 12 + n, (yh, y2)[n % 2][0][:, :, u * P:(u + 1) * P])

            if LAYERS > 4:
                g = Pass(act, "turn_w1")
                for i, n in enumerate("qkvo"):
                    dst = woT
                    if n != "o":
                        wait_slot(act, W["w1", n])
                        dst = w_of(("w1", n))
                    for x in range(2):
                        copy_turned(g, 4 * i + 2 * x, dst[x][:, 0:2, :])
                attention(1, "attn1")

            if LAYERS > 5:
                g = Pass(act, "turn_mlp")
                for i in range(4):
                    copy_turned(g, 2 * i, fcT[:, i, 0:2, :])
                for i in range(4):
                    copy_turned(g, 8 + 2 * i, projT[:, 4 * i:4 * i + 2, :])
                with act.Fori(0, 2) as h:
                    g = Pass(act, "mlp", h)
                    turned_half(g)
                    at = 4

                    def gelus(u, at):
                        for n in range(4):
                            act.activation(hid[:, u % 2, n * 512:(n + 1) * 512], g.take(at + n), ACT.Gelu).then_inc(act_freed, 1)

                    gelus(0, at)
                    at += 4
                    for u in range(HT):
                        if u + 1 < HT:
                            gelus(u + 1, at)
                            at += 4
                        for n in range(4):
                            hi_of_tile(g, at + n, hT[u % 2][0][:, 4 * n:4 * n + 4, :])
                        at += 5

        @block.vector
        def _(dve):
            main = Chain(dve, step)
            done = {"step": 0}

            def piece(i=0, passes=1, key=None):
                n = LINKS.get(key, 0)
                c = Chain(dve, step, done["step"], i, n if passes > 1 else 0)
                c.passes, c.key = passes, key
                return c

            def close(c):
                if c.passes > 1:
                    assert c.n == LINKS.get(c.key), f"LINKS[{c.key!r}] = {c.n}"
                done["step"] += c.n * c.passes

            def finished(semaphore):
                settle(dve)
                dve.drain().then_inc(semaphore, 1)

            def xt(i, u):
                return X[:, bass.ds(i * HT + u, 1), :].rearrange("p a n -> p (a n)")

            def quad(x):
                return x.rearrange("p (k n) -> p k n", k=KC)

            def rstd(c, n):
                v, y, t = (nw[:, i, 0:n] for i in range(3))
                c.link(dve.tensor_scalar(v, mv[:, 0:n, 1], LN_EPS, None, ALU.add))
                c.link(dve.tensor_scalar(y.bitcast(I32), v.bitcast(I32), 1, None, ALU.arith_shift_right))
                dve.tensor_scalar(v, v, -0.5, None, ALU.mult)
                c.link(dve.tensor_scalar(y.bitcast(I32), y.bitcast(I32), -1.0, RSQRT_SEED, ALU.mult, ALU.add))
                for _ in range(3):
                    c.link(dve.tensor_tensor(t, y, y, ALU.mult))
                    c.link(dve.tensor_tensor(t, t, v, ALU.mult))
                    c.link(dve.scalar_tensor_tensor(out=y, in0=t, scalar=1.5, in1=y, op0=ALU.add, op1=ALU.mult))

            def moments(c, tiles):
                for _ in moments_in_steps(c, tiles):
                    pass

            def moments_in_steps(c, tiles):
                for u, x in enumerate(tiles):
                    ins = dve.bn_stats(stats[:, u, :], x)
                    if u == 1:
                        yield
                c.link(ins)
                settle(dve)
                for u in range(len(tiles)):
                    ins = dve.bn_aggr(mv[:, u, :], stats[:, u, :])
                c.link(ins)
                yield
                rstd(c, len(tiles))

            def normed(dst, src, u):
                return dve.tensor_scalar(dst, src, mv[:, u, 0:1], nw[:, 1, u:u + 1], ALU.subtract, ALU.mult)

            def lo_of_tile(g, i, dst, hi):
                bank = g.wait_hi(i)
                dve.tensor_tensor(dst, quad(bank), hi, ALU.subtract).then_inc(dve_freed, 1)

            def norm_half(c, g, i, last=None):
                def low(u):
                    sl = slice(u * P, (u + 1) * P)
                    lo_of_tile(g, u, yh[1][:, :, sl], yh[0][:, :, sl])
                moments(c, [xt(i, u) for u in range(HT)])
                for u in range(HT):
                    if u >= 2:
                        g.take(u - 2)
                    normed(ybuf[:, u % 2], xt(i, u), u).then_inc(y_ready, 1)
                    if u >= 1:
                        low(u - 1)
                low(HT - 1)

            def copy_turned(g, i, dst):
                dve.tensor_copy(dst, g.take(i).bitcast(BF16).rearrange("p (c n) -> p c n", c=2)).then_inc(dve_freed, 1)

            for _ in range(DVE_CREDIT):
                dve.drain().then_inc(dve_freed, 1)
            dve.wait_ge(const_ready, CONSTS)
            dve.wait_ge(x_loaded, 16 * T)
            dve.wait_ge(gamma_loaded, 16)
            with dve.Fori(0, 2) as h:
                c = piece(h, 2, "ln0")
                g = Pass(dve, "ln0", h)
                moments(c, [xt(h, u) for u in range(HT)])
                for u in range(HT):
                    ins = normed(x0[:, u], xt(h, u), u)
                c.link(ins)
                moments(c, [x0[:, u] for u in range(HT)])
                for u in range(HT):
                    ins = normed(x0[:, u], x0[:, u], u)
                c.link(ins)

                def low(u):
                    sl = bass.ds(h * 512 + u * P, P)
                    lo_of_tile(g, u, yT[1][:, :, sl], yT[0][:, :, sl])

                for u in range(HT):
                    if u >= 2:
                        g.take(u - 2)
                    dve.tensor_tensor(ybuf[:, u % 2], x0[:, u], gamma_row, ALU.mult).then_inc(y_ready, 1)
                    if u >= 1:
                        low(u - 1)
                low(HT - 1)
            close(c)

            c = piece()
            dve.wait_ge(mask_loaded, 16)
            head = SCTX - HEAD_ROWS
            c.link(dve.memset(maskadd[0:B, SCTX:KEYS], MASKED))
            c.link(dve.tensor_scalar(maskadd[0:B, 0:head], mask_i[0:B, HEAD_ROWS:SCTX], 0.0, MASKED, ALU.is_equal, ALU.mult))
            c.link(dve.tensor_scalar(maskadd[0:B, head:SCTX], mask_i[0:B, 0:HEAD_ROWS], 0.0, MASKED, ALU.is_equal, ALU.mult))
            c.link(dve.tensor_scalar(mask_f[0:B, 0:SCTX - TAIL], mask_i[0:B, 0:SCTX - TAIL], 0.0, None, ALU.not_equal))
            dve.tensor_reduce(small[0:B, 152:153], mask_f[0:B, 0:SCTX - TAIL], AX.X, ALU.max).then_inc(flag_part, 1)
            dve.wait_ge(wkv_loaded, 16)
            dve.wait_ge(cols_loaded, 16 * 9)
            for k in range(KC):
                ins = dve.tensor_scalar(wkv_f[:, k], wkv_f[:, k], cols[:, C_CGAMMA + k:C_CGAMMA + k + 1], None, ALU.mult)
            c.link(ins)
            for i in range(2):
                ins = dve.tensor_copy(wk[0][:, :, i * XD:(i + 1) * XD], wkv_f[:, :, 0:XD])
            dve.tensor_copy(wv[0], wkv_f[:, :, XD:2 * XD])
            c.link(dve.tensor_scalar(cols[:, C_OMR:C_OMR + 8], cols[:, C_MUR:C_MUR + 8], -1.0, 1.0, ALU.mult, ALU.add))
            for i in range(2):
                sl = slice(i * XD, (i + 1) * XD)
                dve.tensor_tensor(wk[1][:, :, sl], wkv_f[:, :, 0:XD], wk[0][:, :, sl], ALU.subtract)
            c.link(dve.tensor_tensor(wv[1], wkv_f[:, :, XD:2 * XD], wv[0], ALU.subtract))
            close(c)

            for i in range(2):
                with dve.Fori(0, 2) as mp:
                    g = Pass(dve, "q", 2 * i + mp)
                    for mm in range(2):
                        for hf in range(2):
                            bank = g.wait_hi(2 * mm + hf)
                            for h2 in range(2):
                                def q_of(rows_):
                                    return Q[rows_, hf * 8:hf * 8 + 8, bass.ds(i * 8 + mp * 4 + mm * 2 + h2, 1), :]\
                                        .rearrange("p b h s -> p b (h s)")
                                ins = dve.scalar_tensor_tensor(
                                    out=q_of(slice(64, 128)), in0=bank[64 * h2:64 * h2 + 64].rearrange("p (b s) -> p b s", b=8),
                                    scalar=XD ** -0.5, in1=q_of(slice(0, 64)), op0=ALU.mult, op1=ALU.subtract)
                            ins.then_inc(dve_freed, 1)

            x_wait(dve, "shared_ready", 1)
            dve.tensor_scalar(flag[:], SHARED[:, 0:1], 0.5, None, ALU.is_gt).then_inc(XN["shared_free"], 1)
            x_wait(dve, "shared_free", 1)
            finished(flag_ready)

            def attend(nkt):
                v = xmap(nkt)
                W_, ch = v["groups"], v["chunks"]

                def keys(b, i):
                    for c, tiles in enumerate(v["tiles_of"]):
                        n = len(tiles)
                        cm = Chain(dve, norm_step, 0, b * ch + c, LINKS.get("norm", 0))
                        if tiles[-1] == FULL_TILES - 1:
                            x_wait(dve, "ctx_turned", b * nkt + tiles[0])
                            dve.memset(v["ctx"][:, tiles[0] % 4], 0.0).then_inc(XN["ctx_zero"], 1)
                        dve.wait_ge(XN["ctx_loaded"], 16 * (b * nkt + tiles[0] + n))
                        steps = moments_in_steps(cm, [v["ctx"][:, kt % 4] for kt in tiles])
                        for _ in steps:
                            if not v["full"]:
                                yield
                        for u, kt in enumerate(tiles):
                            normed(v["ctx"][:, kt % 4], v["ctx"][:, kt % 4], u).then_inc(XN["ctx_norm"], 1)
                            if kt % 2:
                                yield
                        for kt in tiles:
                            sl = slice(kt % 4 * P, (kt % 4 + 1) * P)
                            x_wait(dve, "ctx_hi", b * nkt + kt + 1)
                            dve.tensor_tensor(v["cT_lo"][:, :, sl], quad(psum[:, 6 + kt % 2]), v["cT_hi"][:, :, sl],
                                              ALU.subtract).then_inc(XN["ctx_lo"], 1)
                            if kt % 4 == 1:
                                yield
                        yield
                        sl = slice(tiles[0] * P, (tiles[-1] + 1) * P)
                        x_wait(dve, "k_hi", b * ch + c + 1)
                        dve.tensor_tensor(v["KB"][i][:, sl], SHARED[:, 0:n * P], v["KA"][i][:, sl], ALU.subtract)\
                            .then_inc(XN["shared_free"], 1)
                        assert cm.n == LINKS.get("norm"), f"LINKS['norm'] = {cm.n}"

                def maximum(b, i, j):
                    x_wait(dve, "s_mm", b * 8 + j + 1)
                    x_wait(dve, "p_turned", b * W_ + j * ch if v["full"] else
                           0 if isinstance(b, int) and b == 0 and j < 2 else b * 8 + j - 1)
                    settle(dve)
                    dve.tensor_tensor_reduce(v["P"][:, j % v["P"].shape[1], :], v["S"](j), v["mb"][i], 1.0, NEG, ALU.add, ALU.max,
                                             xq_max[:, i, j:j + 1]).then_inc(max_step, 1)
                    dve.wait_ge(max_step, b * 8 + j + 1)
                    dve.tensor_scalar(xq_neg[:, i, j:j + 1], xq_max[:, i, j:j + 1], -1.0, None, ALU.mult).then_inc(XN["s_max"], 1)

                def copies(b, j):
                    for c in range(ch):
                        w = j * ch + c
                        if w % 2:
                            n = len(v["tiles_of"][c])
                            x_wait(dve, "p_turned", b * W_ + w + 1)
                            x_wait(dve, "pv", b * W_ + w - 1)
                            dve.tensor_copy(v["PT"][:, 1, 0:n, :], v["PTbank"](w)[:, 0:n * P].rearrange("p (t q) -> p t q", q=P))\
                                .then_inc(XN["p_dve"], 1)

                def tiles(b, i, j):
                    if v["full"] and j >= 0:
                        copies(b, j)
                    if j < 7:
                        maximum(b, i, j + 1)
                    elif not v["full"] and not (isinstance(b, int) and b == B - 1):
                        maximum(b + 1, 1 - i, 0)
                    if not v["full"] and j >= 0:
                        copies(b, j)

                def ends(b, i):
                    c_ = Chain(dve, end_step, 0, b, LINKS.get("end", 0))
                    x_wait(dve, "exp", (b + 1) * 8)
                    neg, r, ok = xq_neg[:, i], xq_r[:, i], xq_ok[:, i]
                    c_.link(dve.tensor_scalar(ok, neg, ALL_MASKED, None, ALU.is_lt))
                    c_.link(dve.reciprocal(r, ok))
                    c_.link(dve.tensor_tensor(r, r, ok, ALU.mult))
                    c_.link(dve.reciprocal(ok, xq_sum[:, i]))
                    c_.link(dve.tensor_tensor(r, r, ok, ALU.mult))
                    x_wait(dve, "pv", (b + 1) * W_)
                    dve.tensor_tensor(v["O"], O_BANK.rearrange("p (j d) -> p j d", j=8), r.unsqueeze(2).to_broadcast([P, 8, XD]),
                                      ALU.mult).then_inc(XN["o_norm"], 1)
                    if not v["full"]:
                        yield
                    for half in range(2):
                        x_wait(dve, "ot_hi", 2 * b + half + 1)
                        bank = SHARED[0:XD].rearrange("p (j m s) -> p j m s", j=4, m=2)
                        for h2 in range(2):
                            o = [x[64 * h2:64 * h2 + 64, 4 * half:4 * half + 4, bass.ds(b * S, S)] for x in oT]
                            ins = dve.tensor_tensor(o[1], bank[:, :, h2, :], o[0], ALU.subtract)
                        ins.then_inc(XN["shared_free"], 1)
                        yield
                    assert c_.n == LINKS.get("end"), f"LINKS['end'] = {c_.n}"

                batches(dve, nkt, keys, tiles, ends)

            head_rows_used = dve.value_load(flag[0:1, 0:1], min_val=0, max_val=1)
            with dve.If(head_rows_used > 0):
                attend(FULL_TILES)
            with dve.If(head_rows_used < 1):
                attend(TAIL_TILES)
            finished(x_attended)
            dve.wait_ge(x_attended, 1)

            for i in range(4):
                with dve.Fori(0, 4) as m:
                    g = Pass(dve, "ff", 4 * i + m)
                    dve.wait_ge(prod_lo, 8 * i + 2 * m + 1)
                    for hf in range(2):
                        g.wait_done(2 * hf + 1)
                        dve.tensor_tensor(prod[:, hf], g.take(2 * hf), ybuf[:, hf], ALU.mult).then_inc(dve_freed, 1)
                    for hf in range(2):
                        dve.wait_ge(prod_hi, 8 * i + 2 * m + hf + 1)
                        x = [t[:, bass.ds(4 * i + m, 1), hf * 512:(hf + 1) * 512].rearrange("p a n -> p (a n)") for t in ffT]
                        dve.tensor_tensor(x[1], prod[:, hf], x[0], ALU.subtract).then_inc(prod_lo, 1)
            with dve.Fori(0, 2) as h:
                g = Pass(dve, "xout", h)
                for u in range(HT):
                    dve.tensor_tensor(xt(h, u), g.take(u), xt(h, u), ALU.add).then_inc(dve_freed, 1)
            if LAYERS > 5:
                c = piece()
                c.link(dve.reduce_sum(gtot, gsum, AX.X))
                finished(gamma_part)
                g = Pass(dve, "gamma")
                dve.tensor_scalar(thr, g.take(0)[:, 0:2], 0.5 / (FF * D), 0.5 * ABSMEAN_EPS, ALU.mult, ALU.add).then_inc(dve_freed, 1)
                g.wait_done(0)
                dve.tensor_scalar(nthr, thr, -1.0, None, ALU.mult).then_inc(thr_ready, 1)
                close(c)
            finished(layer_done)
            dve.wait_ge(layer_done, 1)

            def attention(n, name):
                bq, bk = (C_BQ1, C_BK1) if n else (C_BQ0, C_BK0)
                c = piece()
                dve.wait_ge(bias_loaded, 48 * (n + 1))
                c.link(dve.memset(vb_words, 0))
                close(c)
                with dve.Fori(0, 2) as h:
                    c = piece(h, 2, "attention")
                    g = Pass(dve, name, h)
                    norm_half(c, g, h)
                    for x, (dst, bias) in enumerate(((qh, bq), (kh, bk))):
                        for m in range(KC):
                            bank = g.wait_hi(4 + 4 * x + m)
                            dve.scalar_tensor_tensor(out=dst[1][:, m, :], in0=bank, scalar=cols[:, bias + m:bias + m + 1],
                                                     in1=dst[0][:, m, :], op0=ALU.add, op1=ALU.subtract).then_inc(dve_freed, 1)

                    def v_low(u):
                        dve.wait_ge(v_hi, (n * 2 + h) * HT + u + 1)
                        for m in range(2):
                            r_ = slice(64 * m, 64 * m + 64)
                            ins = dve.tensor_tensor(vb[1][r_, 2 * u:2 * u + 2, :, m, :],
                                                    vf[r_, u % 2].rearrange("p (b g e) -> p b g e", b=2, g=8),
                                                    vb[0][r_, 2 * u:2 * u + 2, :, m, :], ALU.subtract)
                        ins.then_inc(v_done, 1)

                    for u in range(HT):
                        if u >= 2:
                            dve.wait_ge(v_done, (n * 2 + h) * HT + u - 1)
                        dve.tensor_tensor(vf[:, u % 2].rearrange("p (b e) -> p b e", b=2),
                                          g.take(12 + u).rearrange("p (b e) -> p b e", b=2),
                                          bv.rearrange("p j e -> p (j e)").unsqueeze(1).to_broadcast([P, 2, 256]),
                                          ALU.add).then_inc(dve_freed, 1)
                        if u >= 1:
                            v_low(u - 1)
                    v_low(HT - 1)

                    def weigh(u, at):
                        pu = prob[:, u % 2]
                        for r in range(4):
                            s = g.take(at + r)[:, 0:4 * S].rearrange("p (m s) -> p m s", m=4)
                            if n:
                                ins = dve.tensor_scalar(pu[:, r], s, AD ** -0.5, None, ALU.mult)
                            else:
                                ins = dve.scalar_tensor_tensor(out=pu[:, r], in0=s, scalar=AD ** -0.5,
                                                               in1=causal[:].unsqueeze(1).to_broadcast([P, 4, S]),
                                                               op0=ALU.mult, op1=ALU.add)
                            ins.then_inc(dve_freed, 1)
                        g.wait_done(at + 3)
                        flat = pu.rearrange("p r m s -> p (r m) s")
                        c.link(dve.tensor_reduce(s_max[:, u % 2], flat, AX.X, ALU.max))
                        dve.tensor_tensor(flat, flat, s_max[:, u % 2].unsqueeze(2).to_broadcast([P, AH, S]), ALU.subtract)\
                            .then_inc(p_max, 1)

                    at = 16
                    weigh(0, at)
                    at += 4
                    for u in range(HT):
                        if u + 1 < HT:
                            weigh(u + 1, at)
                            at += 4
                        dve.wait_ge(p_exp, (n * 2 + h) * HT + u + 1)
                        c.link(dve.reduce_sum(s_sum[:, u % 2], prob[:, u % 2].rearrange("p r m s -> p (r m) s"), AX.X))
                        c.link(dve.reciprocal(s_sum[:, u % 2], s_sum[:, u % 2]))
                        for j in range(2):
                            lo_of_tile(g, at + j, pT[1][:, u % 2, 4 * j:4 * j + 4, :], pT[0][:, u % 2, 4 * j:4 * j + 4, :])
                        dve.tensor_tensor(ybuf[:, u % 2].rearrange("p (m r d) -> p m r d", m=4, r=4),
                                          g.take(at + 2).rearrange("p (m r d) -> p m r d", m=4, r=4),
                                          s_sum[:, u % 2].rearrange("p (r m) -> p m r", r=4).unsqueeze(3).to_broadcast([P, 4, 4, AD]),
                                          ALU.mult).then_inc(dve_freed, 1)
                        sl = slice(u * P, (u + 1) * P)
                        lo_of_tile(g, at + 3, ah[1][:, :, sl], ah[0][:, :, sl])
                        at += 4
                    for u in range(HT):
                        dve.tensor_tensor(xt(h, u), g.take(at + u), xt(h, u), ALU.add).then_inc(dve_freed, 1)
                    g.wait_done(at + 3)
                    for u in range(HT):
                        ins = dve.tensor_tensor(xt(h, u), xt(h, u), bo, ALU.add)
                    c.link(ins)
                close(c)
                finished(layer_done)

            if LAYERS > 1:
                attention(0, "attn0")

            if LAYERS > 2:
                c = piece()
                g = Pass(dve, "turn_mix")
                for i, n in enumerate("rkv"):
                    wait_slot(dve, W["mix", n])
                    for x in range(2):
                        copy_turned(g, 4 * i + 2 * x + 1, w_of(("mix", n))[x][:, 2:4, :])
                c.link(dve.memset(zp[:, :, :, 0:1], 0.0))
                finished(om_ready)
                close(c)
                with dve.Fori(0, 2) as h:
                    c = piece(h, 2, "mix")
                    g = Pass(dve, "mix", h)
                    moments(c, [xt(h, u) for u in range(HT)])
                    for u in range(HT):
                        if u >= 2:
                            g.take(u - 2)
                        normed(ybuf[:, u % 2], xt(h, u), u).then_inc(y_ready, 1)

                    def mixed(n):
                        mu = (C_MUR, C_MUK)[n // 4] + n % 4
                        if n >= 2:
                            dve.wait_ge(mix_lo, 8 * h + n - 1)
                        dve.wait_ge(mix_a, 8 * h + n + 1)
                        dve.scalar_tensor_tensor(out=mix_f[:, n % 2].rearrange("p (b s) -> p b s", b=8),
                                                 in0=zp[:, n % 4, :, 1:], scalar=cols[:, mu:mu + 1],
                                                 in1=mix_t[:, n % 2].rearrange("p (b s) -> p b s", b=8),
                                                 op0=ALU.mult, op1=ALU.add).then_inc(mix_b, 1)

                    def mixed_low(n):
                        dve.wait_ge(mix_hi, 8 * h + n + 1)
                        dst = mixT[n // 4]
                        dve.tensor_tensor(dst[1][:, n % 4, :], mix_f[:, n % 2], dst[0][:, n % 4, :], ALU.subtract)\
                            .then_inc(mix_lo, 1)

                    mixed(0)
                    for n in range(8):
                        if n < 7:
                            mixed(n + 1)
                        mixed_low(n)

                    def relu_low(m):
                        dve.wait_ge(relu_hi, 4 * h + m + 1)
                        dve.tensor_tensor(kact[1][:, m, :], relu2[:, m % 2], kact[0][:, m, :], ALU.subtract).then_inc(relu_lo, 1)

                    for m in range(KC):
                        dve.tensor_scalar(relu[:, m % 2], g.take(8 + m), 0.0, None, ALU.max).then_inc(dve_freed, 1)
                        if m:
                            relu_low(m - 1)
                    relu_low(KC - 1)
                    g.wait_done(7)
                    for u in range(HT):
                        dve.tensor_tensor(relu[:, u % 2], g.take(12 + u), recept[:, u], ALU.mult).then_inc(dve_freed, 1)
                        g.wait_done(12 + u)
                        c.link(dve.tensor_tensor(xt(h, u), xt(h, u), relu[:, u % 2], ALU.add))
                close(c)
                finished(layer_done)

            if LAYERS > 3:
                c = piece()
                pt = ptr[:, 0:T]
                wptr = ptf[:, 0:4 * T].rearrange("p (w t) -> p w t", t=T)
                dve.wait_ge(ids_loaded, 48)
                for w in range(3):
                    c.link(dve.tensor_scalar(wptr[:, w], pt, float(w), 0.0, ALU.add, ALU.max))
                    c.link(dve.tensor_scalar(wptr[:, w], wptr[:, w], float(SCTX - 1), None, ALU.min))
                    c.link(dve.tensor_tensor(row_of.rearrange("p (t w) -> p w t", w=4)[:, w, 0:T], wptr[:, w], tile_base, ALU.add))
                finished(rows_ready)
                c.link(dve.tensor_scalar(wptr[:, 3], wptr[:, 0], float(S - 1), None, ALU.min))
                for t in range(T):
                    c.link(dve.scalar_tensor_tensor(out=id_hit[:, 0:S], in0=key_no[:], scalar=wptr[:, 3, t:t + 1], in1=ids_rows[:, t],
                                                    op0=ALU.is_equal, op1=ALU.mult, accum_out=rel_id[:, t:t + 1]))
                cw = cols[:, C_CW:C_CW + 2]
                c.link(dve.tensor_reduce(council[:, 0:1], cw, AX.X, ALU.max))
                c.link(dve.tensor_scalar(council[:, 2:4], cw, council[:, 0:1], None, ALU.subtract))
                finished(logit)
                g = Pass(dve, "fold")

                def folded(first, pair):
                    for m in range(KC):
                        bank = g.wait_hi(first + m)
                        dve.tensor_tensor(pair[1][:, m, :], bank, pair[0][:, m, :], ALU.subtract).then_inc(dve_freed, 1)

                folded(0, fold[0])
                folded(4, fold[1])
                wait_slot(dve, W["win", "WoutT"])
                for x in range(2):
                    copy_turned(g, 8 + 2 * x + 1, w_of(("win", "WoutT"))[x][:, 2:4, :])
                folded(12, fold[2])
                folded(16, fold[3])
                dve.wait_ge(e_ready, 1)
                c.link(dve.reduce_sum(council[:, 0:1], council[:, 4:6], AX.X))
                c.link(dve.reciprocal(council[:, 1:2], council[:, 0:1]))
                c.link(dve.tensor_scalar(council[:, 6:8], council[:, 4:6], council[:, 1:2], None, ALU.mult))
                close(c)
                with dve.Fori(0, 2) as h:
                    c = piece(h, 2, "window")
                    g = Pass(dve, "window", h)
                    norm_half(c, g, h)
                    dve.wait_ge(win_loaded, 16 * 3 * HT * (h + 1))
                    for u in range(HT):
                        for s in range(2):
                            bank = g.take(4 + 2 * u + s)
                            for w in range(3):
                                ins = dve.tensor_tensor_reduce(junk[:, w % 2], bank, win[:, u, w, :], D ** -0.5, 0.0, ALU.mult,
                                                               ALU.add, sc[:, 3 * s + w, u:u + 1])
                                if w < 2:
                                    c.link(ins)
                                else:
                                    ins.then_inc(dve_freed, 1)
                                    g.wait_done(4 + 2 * u + s)
                    col = lambda i: sc[:, i, :]
                    rel, v1, v2 = col(0), col(1), col(2)
                    ids = rel_id[:, bass.ds(h * HT, HT)]

                    def tt(o, x, y, op):
                        c.link(dve.tensor_tensor(col(o), x, y, op))

                    def ts(o, x, s1, s2, op0, op1=None):
                        c.link(dve.tensor_scalar(col(o), x, s1, s2, op0, *([op1] if op1 is not None else [])))

                    tt(8, v1, v2, ALU.add)
                    tt(9, v1, v2, ALU.max)
                    ts(10, v1, -1.0, None, ALU.mult)
                    tt(11, col(10), v2, ALU.max)
                    tt(12, v1, v2, ALU.subtract)
                    ts(13, col(12), -1.0, None, ALU.mult)
                    tt(12, col(12), col(13), ALU.max)
                    for e in range(5):
                        x = col(14 if e == 0 else 15)
                        c.link(dve.scalar_tensor_tensor(out=x, in0=ids, scalar=float(e), in1=col(8 + e), op0=ALU.is_equal,
                                                        op1=ALU.mult))
                        if e:
                            tt(14, col(14), col(15), ALU.add)
                    ts(16, ids, 0.0, None, ALU.is_ge)
                    c.link(dve.scalar_tensor_tensor(out=col(16), in0=ids, scalar=4.0, in1=col(16), op0=ALU.is_le, op1=ALU.mult))
                    tt(14, col(14), col(16), ALU.mult)
                    ts(17, col(16), -1.0, 1.0, ALU.mult, ALU.add)
                    tt(17, col(17), rel, ALU.mult)
                    tt(0, col(14), col(17), ALU.add)
                    for s in range(2):
                        tt(18, col(3 * s), col(3 * s + 1), ALU.max)
                        tt(18, col(18), col(3 * s + 2), ALU.max)
                        for w in range(3):
                            tt(SC_E + 3 * s + w, col(3 * s + w), col(18), ALU.subtract)
                    finished(logit)
                    dve.wait_ge(e_ready, h + 2)
                    for s in range(2):
                        e0 = SC_E + 3 * s
                        tt(18, col(e0), col(e0 + 1), ALU.add)
                        tt(18, col(18), col(e0 + 2), ALU.add)
                        c.link(dve.reciprocal(col(19), col(18)))
                        ts(19, col(19), council[:, 6 + s:7 + s], None, ALU.mult)
                        for w in range(3):
                            tt(e0 + w, col(e0 + w), col(19), ALU.mult)

                    def low(n):
                        sl = slice(n // 2 * P, (n // 2 + 1) * P)
                        pair = (yh, y2)[n % 2]
                        lo_of_tile(g, 12 + n, pair[1][:, :, sl], pair[0][:, :, sl])

                    for n in range(2 * HT):
                        u, s = n // 2, n % 2
                        x = comb[:, s]
                        wt = [sc[:, SC_E + 3 * s + w, u:u + 1] for w in range(3)]
                        c.link(dve.tensor_scalar(x, win[:, u, 0, :], wt[0], None, ALU.mult))
                        c.link(dve.scalar_tensor_tensor(out=x, in0=win[:, u, 1, :], scalar=wt[1], in1=x, op0=ALU.mult, op1=ALU.add))
                        dve.scalar_tensor_tensor(out=x, in0=win[:, u, 2, :], scalar=wt[2], in1=x, op0=ALU.mult, op1=ALU.add)\
                            .then_inc(comb_ready, 1)
                        if n:
                            low(n - 1)
                    low(2 * HT - 1)
                    for u in range(HT):
                        dve.scalar_tensor_tensor(out=xt(h, u), in0=g.take(20 + u), scalar=cols[:, C_GAIN:C_GAIN + 1], in1=xt(h, u),
                                                 op0=ALU.mult, op1=ALU.add).then_inc(dve_freed, 1)
                    g.wait_done(23)
                close(c)
                finished(layer_done)

            if LAYERS > 4:
                g = Pass(dve, "turn_w1")
                for i, n in enumerate("qkvo"):
                    dst = woT
                    if n != "o":
                        wait_slot(dve, W["w1", n])
                        dst = w_of(("w1", n))
                    for x in range(2):
                        copy_turned(g, 4 * i + 2 * x + 1, dst[x][:, 2:4, :])
                attention(1, "attn1")

            if LAYERS > 5:
                g = Pass(dve, "turn_mlp")
                for i in range(4):
                    copy_turned(g, 2 * i + 1, fcT[:, i, 2:4, :])
                for i in range(4):
                    copy_turned(g, 8 + 2 * i + 1, projT[:, 4 * i + 2:4 * i + 4, :])
                with dve.Fori(0, 2) as h:
                    c = piece(h, 2, "mlp")
                    g = Pass(dve, "mlp", h)
                    norm_half(c, g, h)
                    at = 4

                    def norm_hidden(u, last):
                        g.wait_done(last)
                        x = hid[:, u % 2]
                        for n in range(4):
                            ins = dve.bn_stats(stats[:, n, :], x[:, n * 512:(n + 1) * 512])
                        c.link(ins)
                        settle(dve)
                        c.link(dve.bn_aggr(mv[:, 0, :], stats[:].rearrange("p n k -> p (n k)")))
                        rstd(c, 1)
                        normed(x, x, 0).then_inc(hid_norm, 1)

                    norm_hidden(0, 7)
                    at = 8
                    for u in range(HT):
                        if u + 1 < HT:
                            norm_hidden(u + 1, at + 3)
                            at += 4
                        for n in range(4):
                            lo_of_tile(g, at + n, hT[u % 2][1][:, 4 * n:4 * n + 4, :], hT[u % 2][0][:, 4 * n:4 * n + 4, :])
                        dve.tensor_tensor(xt(h, u), g.take(at + 4), xt(h, u), ALU.add).then_inc(dve_freed, 1)
                        at += 5
                close(c)
                finished(layer_done)


def kernel(**inputs):
    import numpy as _np
    import concourse.bacc as _bacc
    from concourse import mybir as _mybir
    from concourse.bass_utils import run_bass_kernel_spmd as _run

    nc = _bacc.Bacc("TRN2", target_bir_lowering=False, num_devices=1)
    arrays, args = {}, {}
    for name in inputs:
        arr = _np.ascontiguousarray(inputs[name])
        if arr.ndim == 0 or name == "L1_xattn_gain":
            arr = arr.reshape(1)
        arrays[f"in_{name}_dram"] = arr
        args[name] = nc.dram_tensor(f"in_{name}_dram", arr.shape, _mybir.dt.from_np(arr.dtype), kind="ExternalInput").ap()
    out = nc.dram_tensor("out_0_dram", (B, S, D), F32, kind="ExternalOutput").ap()
    build(nc, args, out)
    r = _run(nc, [arrays], core_ids=[0])
    return r.results[0]["out_0_dram"]
```

```python
from contextlib import ExitStack

import concourse.bass as bass
from concourse import mybir

F32 = mybir.dt.float32
BF16 = mybir.dt.bfloat16
I32 = mybir.dt.int32
ALU = mybir.AluOpType
ACT = mybir.ActivationFunctionType
AX = mybir.AxisListType

P = 128
B, S, D = 16, 64, 512
T = B * S // P
HT = T // 2
KC = D // P
SCTX = 1601
XH, XD = 16, 64
FF = 2048
AH, AD = 16, 32
RING = 6
STAGED = 2
LN_EPS = 1e-5
ABSMEAN_EPS = 1e-6
MASKED = -3.0e38
NEG = -3.4028234663852886e38
ALL_MASKED = 1.0e38
DVE_CREDIT = 1
ACT_CREDIT = 2
CONSTS = 11
SC_E = 20
LINKS = {"ln0": 30, "rstd": 12, "end": 3, "attention": 27, "mix": 18, "window": 37, "mlp": 70}
RSQRT_SEED = float(0x5F3759DF)
KB = 256

FULL_TILES = (SCTX + P - 1) // P
TAIL_TILES = 4
TAIL = TAIL_TILES * P
HEAD_ROWS = SCTX - (FULL_TILES - 1) * P
KEYS = FULL_TILES * P


class Stage:

    def __init__(self, letters, passes=1, banks=8, rolling=False):
        self.letters, self.passes, self.banks, self.rolling = letters, passes, banks, rolling
        assert not rolling or len(letters) == banks
        self.n = len(letters)
        self.n_dve = self.n - letters.count("A")
        self.n_act = letters.count("A")
        self.n_hi = letters.count("h")
        self.base = None

    def freed(self, g):
        head = self.letters[:g + 1]
        return (True, head.count("A")) if self.letters[g] == "A" else (False, len(head) - head.count("A"))


class Chain:

    def __init__(self, eng, semaphore, base=0, i=0, per_pass=0):
        self.eng, self.sem, self.start, self.n, self.per_pass = eng, semaphore, base + i * per_pass, 0, per_pass

    def link(self, ins):
        self.n += 1
        ins.then_inc(self.sem, 1)
        self.eng.wait_ge(self.sem, self.start + self.n)

    def close(self):
        assert not self.per_pass or self.n == self.per_pass, f"links in a pass: {self.n}"


def build(nc, a, out):
    ctx = ExitStack()
    with ctx:
        def sb(name, shape, dt=F32):
            return ctx.enter_context(nc.sbuf_tensor(name, shape, dt))

        def sem(name):
            return ctx.enter_context(nc.semaphore(name))

        X = sb("X", [P, T, D])
        y_mem = sb("y_mem", [P, 16 * KB])
        o_mem = sb("o_mem", [P, 32 * KB])
        big = sb("big", [P, 64 * KB])
        side = sb("side", [P, 8 * KB])
        ring_hi = sb("ring_hi", [P, RING, KC, D], BF16)
        ring_lo = sb("ring_lo", [P, RING, KC, D], BF16)
        stage = sb("stage", [P, STAGED, KC, D])
        ybuf = sb("ybuf", [P, 2, D])
        ident = sb("ident", [P, P])
        identb = sb("identb", [P, P], BF16)
        ones = sb("ones", [P, P])
        causal = sb("causal", [P, S])
        stats = sb("stats", [P, 4, 6])
        mv = sb("mv", [P, 4, 2])
        nw = sb("nw", [P, 3, 4])
        cols = sb("cols", [P, 48])
        small = sb("small", [P, 168])
        key_no = sb("key_no", [P, S], I32)
        flag = sb("flag", [P, 1], I32)
        spare = sb("spare", [P, KB])
        psum = ctx.enter_context(nc.psum_tensor("psum", [P, 8, 512], F32))

        def settle(eng):
            eng.sem_inc(idle, 1)

        def carve(mem, at_kb, kb, dt, pattern=None, **dims):
            v = mem[:, int(at_kb * KB):int((at_kb + kb) * KB)]
            if dt != F32:
                v = v.bitcast(dt)
            return v.rearrange(pattern, **dims) if pattern else v

        def halves(mem, at_kb, kb, pattern, **dims):
            return [carve(mem, at_kb + i * kb, kb, BF16, pattern, **dims) for i in range(2)]

        yT = halves(y_mem, 0, 8, "p (k n) -> p k n", k=KC)
        yh = halves(y_mem, 0, 4, "p (k n) -> p k n", k=KC)
        y2 = halves(y_mem, 8, 4, "p (k n) -> p k n", k=KC)
        oT = halves(o_mem, 0, 16, "p (k n) -> p k n", k=8)
        Q = carve(big, 0, 32, BF16, "p (b h s) -> p b h s", b=B, h=XH)
        x0 = carve(big, 32, 8, F32, "p (t n) -> p t n", t=HT)
        gamma_row = carve(big, 40, 2, F32)
        wkv_f = carve(o_mem, 0, 2, F32, "p (k n) -> p k n", k=KC)
        mask_i = carve(o_mem, 8, 7, I32)
        mask_f = carve(o_mem, 16, 7, F32)
        maskadd = carve(side, 0, 3.25, BF16)
        wk = halves(side, 3.25, 1, "p (k n) -> p k n", k=KC)
        wv = halves(side, 5.25, 0.5, "p (k n) -> p k n", k=KC)
        ffT = halves(big, 0, 32, "p (k n) -> p k n", k=FF // P)
        prod = carve(side, 0, 4, F32, "p (i n) -> p i n", i=2)
        qh = halves(big, 0, 4, "p (k n) -> p k n", k=KC)
        kh = halves(big, 8, 4, "p (k n) -> p k n", k=KC)
        vb = halves(big, 16, 8, "p (b g m e) -> p b g m e", b=8, g=8, m=2)
        vb_words = carve(big, 16, 16, I32)
        prob = carve(big, 32, 8, F32, "p (i r m s) -> p i r m s", i=2, r=4, m=4)
        pT = [carve(big, 40 + 4 * i, 4, BF16, "p (i g q) -> p i g q", i=2, g=8) for i in range(2)]
        vf = carve(big, 48, 4, F32, "p (i n) -> p i n", i=2)
        ah = halves(big, 52, 4, "p (k n) -> p k n", k=KC)
        bv = carve(side, 4, 1, F32, "p (j e) -> p j e", j=2)
        bo = carve(side, 5, 2, F32)
        woT = halves(y_mem, 8, 4, "p (k n) -> p k n", k=KC)
        zp = carve(big, 0, 8.125, F32, "p (k b s) -> p k b s", k=KC, b=8)
        mixT = [halves(big, 9 + 8 * i, 4, "p (k n) -> p k n", k=KC) for i in range(2)]
        turned = [halves(o_mem, 8 + 8 * i, 4, "p (k n) -> p k n", k=KC) for i in range(3)]
        mix_t = carve(big, 25, 4, F32, "p (i n) -> p i n", i=2)
        mix_f = carve(big, 29, 4, F32, "p (i n) -> p i n", i=2)
        kact = halves(big, 33, 4, "p (k n) -> p k n", k=KC)
        recept = carve(big, 41, 8, F32, "p (t n) -> p t n", t=HT)
        relu = carve(big, 49, 4, F32, "p (i n) -> p i n", i=2)
        relu2 = carve(big, 53, 4, F32, "p (i n) -> p i n", i=2)
        fold = [halves(big, 8 * i, 4, "p (k n) -> p k n", k=KC) for i in range(4)]
        win = carve(big, 32, 24, F32, "p (t w n) -> p t w n", t=HT, w=3)
        comb = carve(big, 56, 4, F32, "p (i n) -> p i n", i=2)
        junk = carve(big, 60, 4, F32, "p (i n) -> p i n", i=2)
        ids_rows = carve(o_mem, 0, 2, I32, "p (t s) -> p t s", t=T)
        id_hit = carve(o_mem, 3, 0.25, F32)
        ptr = carve(o_mem, 4, 1, I32)
        ptf = carve(o_mem, 5, 1, F32)
        row_of = carve(o_mem, 6, 1, I32)[:, 0:4 * T]
        sc = carve(o_mem, 8, 2, F32, "p (n t) -> p n t", t=HT)
        rel_id = carve(o_mem, 7, 0.25, F32)
        fcT = carve(big, 0, 16, BF16, "p (i k n) -> p i k n", i=4, k=KC)
        projT = carve(big, 16, 16, BF16, "p (k n) -> p k n", k=FF // P)
        lnw = carve(big, 32, 8, F32)
        lnb = carve(big, 40, 8, F32)
        below = carve(o_mem, 0, 4, BF16, "p (k n) -> p k n", k=KC)
        hid = carve(o_mem, 0, 16, F32, "p (i n) -> p i n", i=2)
        hT = [halves(o_mem, 16 + 8 * i, 4, "p (k n) -> p k n", k=FF // P) for i in range(2)]

        C_CGAMMA, C_BQ0, C_BK0, C_BQ1, C_BK1, C_MUR, C_MUK, C_OMR, C_OMK, C_GAIN, C_CW = 0, 4, 8, 12, 16, 20, 24, 28, 32, 36, 38
        gsum = small[:, 0:32].rearrange("p (w b) -> p w b", w=2)
        gtot = small[:, 32:34]
        thr = small[:, 34:36]
        nthr = small[:, 36:38]
        s_max = small[:, 40:72].rearrange("p (i h) -> p i h", i=2)
        s_sum = small[:, 72:104].rearrange("p (i h) -> p i h", i=2)
        mv_hid = small[:, 104:106].unsqueeze(1)
        nw_hid = small[:, 106:109].unsqueeze(2)
        xq_max, xq_neg, xq_sum, xq_ok, xq_r = (
            carve(side, 7.25 + i / 16, 1 / 16, F32, "p (i j) -> p i j", i=2) for i in range(5))
        council = small[:, 160:168]
        tile_base = small[:, 144:152].bitcast(I32)

        x_loaded, cols_loaded, gamma_loaded, wkv_loaded, mask_loaded = map(
            sem, ("x_loaded", "cols_loaded", "gamma_loaded", "wkv_loaded", "mask_loaded"))
        stage_loaded = [sem(f"stage_loaded{i}") for i in range(STAGED)]
        bias_loaded, ids_loaded, win_loaded, out_stored = map(sem, ("bias_loaded", "ids_loaded", "win_loaded", "out_stored"))
        idle = sem("idle")
        const_ready = sem("const_ready")
        pool_split = sem("pool_split")
        pool_part = sem("pool_part")
        group_ready = sem("group_ready")
        act_hi = sem("act_hi")
        dve_freed = sem("dve_freed")
        act_freed = sem("act_freed")
        step = sem("step")
        y_ready = sem("y_ready")
        prod_hi, prod_lo = map(sem, ("prod_hi", "prod_lo"))
        block_used = sem("block_used")
        v_hi, v_done, p_max, p_exp = map(sem, ("v_hi", "v_done", "p_max", "p_exp"))
        layer_done = sem("layer_done")
        om_ready, mix_a, mix_b, mix_hi, mix_lo = map(sem, ("om_ready", "mix_a", "mix_b", "mix_hi", "mix_lo"))
        relu_sq, relu_hi, relu_lo = map(sem, ("relu_sq", "relu_hi", "relu_lo"))
        rows_ready, logit, e_ready, weights_ready, first_row, comb_ready = map(
            sem, ("rows_ready", "logit", "e_ready", "weights_ready", "first_row", "comb_ready"))
        thr_ready, hid_norm, hid_ready = map(sem, ("thr_ready", "hid_norm", "hid_ready"))
        flag_part, flag_ready, x_attended, gamma_part, hid_scaled = map(
            sem, ("flag_part", "flag_ready", "x_attended", "gamma_part", "hid_scaled"))

        def rows(w, c0=0):
            return w[:, c0:c0 + D].rearrange("(k p) n -> p k n", p=P)

        entries, W = [], {}

        def entry(key, kind, src=None):
            W[key] = len(entries)
            entries.append((kind, src))

        for i in range(2):
            entry(("q", i), "n", rows(a["L0_xattn_Wq"], i * D))
        for i in range(4):
            entry(("ffa", i), "n", rows(a["L0_xattn_Wff1"], i * D))
            entry(("ffg", i), "n", rows(a["L0_xattn_Wff1"], FF + i * D))
        for i in range(2):
            entry(("xo", i), "n", rows(a["L0_xattn_Wout"][i * D:(i + 1) * D, :]))
        for i in range(4):
            entry(("ff2", i), "n", rows(a["L0_xattn_Wff2"][i * D:(i + 1) * D, :]))
        before_x = 8
        for n in "qkvo":
            entry(("w0", n), "n", rows(a["L0_attn_w" + n]))
        for n in "rkv":
            entry(("mixn", n), "n", rows(a["L0_ffn_W_" + n]))
        for n in ("Wqj", "Wkj", "Wqi", "Wki", "Wout"):
            entry(("win", n), "n", rows(a["L1_xattn_" + n]))
        for n in ("Wvj", "Wvi"):
            entry(("win", n), "n", rows(a["L1_xattn_" + n]))
        for i, n in enumerate("qkv"):
            entry(("w1n", n), "n", rows(a["L1_attn_W_qkv"][i * D:(i + 1) * D, :]))
        entry(("w1n", "o"), "n", rows(a["L1_attn_W_out"]))
        for i in range(4):
            entry(("fc", i), "t", rows(a["L1_ffn_W_fc"][i * D:(i + 1) * D, :]))
        for i in range(4):
            entry(("proj", i), "t", rows(a["L1_ffn_W_proj"], i * D))
        released = {}

        def w_of(key):
            s = W[key] % RING
            return ring_hi[:, s], ring_lo[:, s]

        def ternary_of(t):
            s = (W["fc", 0] + t // 2) % RING
            return (ring_hi, ring_lo)[t % 2][:, s]

        def wait_slot(eng, e):
            if e >= RING:
                eng.wait_ge(*released[e - RING])

        def wait_split(eng, key):
            eng.wait_ge(pool_split, W[key] + 1)

        plan = {"ln0": Stage("hhhh", 2), "q": Stage("hhhh", 4, 4, True), "ff": Stage("DADA", 16, 4, True),
                "xout": Stage("DDDDDDDD")}
        plan["gamma"] = Stage("D")
        attn = ("hhhh" "hhhh" "hhhh" "DDDD"
                "DDDD" + "hhDDDDDh" * 3 + "hhDh"
                + "DDDD")
        plan["attn0"] = Stage(attn, 2)
        plan["turn_mix"] = Stage("AD" * 6)
        plan["mix"] = Stage("AAAA" "AAAA" "DDDD" "DDDD", 2)
        plan["fold"] = Stage("hhhh" "hhhh" "ADAD" "hhhh" "hhhh")
        plan["window"] = Stage("hhhh" "DDDDDDDD" "hhhhhhhh" "DDDD", 2)
        plan["turn_w1"] = Stage("AD" * 8)
        plan["attn1"] = Stage(attn, 2)
        plan["turn_mlp"] = Stage("AD" * 8)
        plan["mlp"] = Stage("hhhh" + "AAAA" + "AAAAhhhhD" * 3 + "hhhhD", 2)
        total = [0, DVE_CREDIT, ACT_CREDIT, 0]
        for st in plan.values():
            st.base = tuple(total)
            for i, n in enumerate((st.n, st.n_dve, st.n_act, st.n_hi)):
                total[i] += n * st.passes

        def after(name, groups=None):
            st = plan[name]
            return group_ready, st.base[0] + (st.n * st.passes if groups is None else groups)

        class Pass:

            def __init__(self, eng, name, i=0):
                self.eng, self.st = eng, plan[name]
                st = self.st
                self.ready, self.dve, self.act, self.hi = (
                    b + n * i for b, n in zip(st.base, (st.n, st.n_dve, st.n_act, st.n_hi)))
                self.first = st.base[0] == 0
                self.at = 0

            def bank(self, g):
                return psum[:, g % self.st.banks, :]

            def open(self):
                g, st = self.at, self.st
                self.at += 1
                if st.rolling:
                    is_act, n = st.freed(g)
                    if is_act:
                        self.eng.wait_ge(act_freed, self.act - st.n_act + n)
                    else:
                        self.eng.wait_ge(dve_freed, self.dve - st.n_dve + n)
                elif g >= st.banks:
                    is_act, n = st.freed(g - st.banks)
                    self.eng.wait_ge(act_freed if is_act else dve_freed, (self.act if is_act else self.dve) + n)
                elif g == 0:
                    self.all_free()
                return self.bank(g)

            def all_free(self):
                self.eng.wait_ge(dve_freed, self.dve)
                self.eng.wait_ge(act_freed, self.act)

            def take(self, g):
                self.eng.wait_ge(group_ready, self.ready + g + 1)
                return self.bank(g)

            def wait_hi(self, g):
                self.eng.wait_ge(act_hi, self.hi + self.st.letters[:g + 1].count("h"))
                return self.bank(g)

            def wait_done(self, g):
                is_act, n = self.st.freed(g)
                self.eng.wait_ge(act_freed if is_act else dve_freed, (self.act if is_act else self.dve) + n)

        for i in range(2):
            released[W["q", i]] = after("q", 8 * (i + 1))
        for i in range(4):
            released[W["ffa", i]] = released[W["ffg", i]] = after("ff", 16 * (i + 1))
            released[W["ff2", i]] = block_used, 2 + i + 1
        for i in range(2):
            released[W["xo", i]] = block_used, i + 1
        for n in "qkvo":
            released[W["w0", n]] = after("attn0")
        for i, n in enumerate("rkv"):
            released[W["mixn", n]] = after("turn_mix", 4 * (i + 1))
        for n, g in (("Wqj", 4), ("Wkj", 4), ("Wqi", 8), ("Wki", 8), ("Wout", 12), ("Wvj", 16), ("Wvi", 20)):
            released[W["win", n]] = after("fold", g)
        for i, n in enumerate("qkvo"):
            released[W["w1n", n]] = after("turn_w1", 4 * (i + 1))
        y_base, n_y = {}, 0
        for name, passes, n in (("ln0", 2, 4), ("attn0", 2, 4), ("mix", 2, 4), ("window", 2, 4), ("attn1", 2, 4), ("mlp", 2, 4)):
            y_base[name] = (n_y, n)
            n_y += passes * n

        def xviews(nkt):
            n = nkt * P
            full = nkt > TAIL_TILES
            v = {"full": full, "nkt": nkt, "n": n, "chunks": (nkt + 3) // 4, "m0": 0 if full else (FULL_TILES - 1 - TAIL_TILES) * P}
            at = 32

            def put(key, kb, dt, pattern=None, **dims):
                nonlocal at
                v[key] = carve(big, at, kb, dt, pattern, **dims)
                at += kb
            kb = n / 512
            put("KA", kb, BF16)
            put("KB", kb, BF16)
            put("V", kb, F32, "p (t e) -> p t e", e=XD)
            put("mb", kb, BF16)
            shared = at
            put("ctx", 8, F32, "p (t n) -> p t n", t=4)
            put("cT_hi", 4, BF16, "p (k n) -> p k n", k=KC)
            put("cT_lo", 4, BF16, "p (k n) -> p k n", k=KC)
            if full:
                v["P"] = carve(big, shared, n / 256, F32, "p (i n) -> p i n", i=1)
                v["PT"] = carve(big, shared + n / 256, 4, F32, "p (i t q) -> p i t q", i=2, t=4)
            else:
                put("P", n / 256 * 2, F32, "p (i n) -> p i n", i=2)
                put("PT", 4, F32, "p (i t q) -> p i t q", i=2, t=4)
            put("O", 2, F32, "p (j d) -> p j d", j=8)
            for key in ("KA", "KB", "V", "mb"):
                v[key] = [v[key]]
            if not full:
                v["KA"].append(carve(big, at, 1, BF16))
                v["KB"].append(carve(big, at + 1, 1, BF16))
                v["V"].append(spare.rearrange("p (t e) -> p t e", e=XD))
                v["mb"].append(carve(side, 6.25, 1, BF16))
                at += 2
            assert at <= 64, at
            return v


        XN = {n: sem("x_" + n) for n in (
            "ctx_loaded",
            "ctx_zero",
            "ctx_norm",
            "ctx_turned",
            "ctx_hi", "ctx_lo",
            "shared_ready",
            "shared_free",
            "k_hi", "v_mm", "v_copied", "s_mm", "s_max", "exp", "p_turned", "p_act", "p_dve", "pv", "o_norm",
            "ot_hi", "g_loaded", "g_summed")}
        norm_step, rstd_step, max_step, end_step = map(sem, ("norm_step", "rstd_step", "max_step", "end_step"))

        def x_wait(eng, name, n):
            eng.wait_ge(XN[name], n + 1)

        def xmap(nkt):
            v = xviews(nkt)
            v["tiles_of"] = [range(4 * c, min(4 * c + 4, nkt)) for c in range(v["chunks"])]
            v["S"] = (lambda j: psum[:, 0:4].rearrange("p a n -> p (a n)")[:, 0:v["n"]]) if v["full"] \
                else (lambda j: psum[:, j % 2])
            v["PTbank"] = (lambda w: psum[:, 6 + w % 2]) if v["full"] else (lambda w: psum[:, 2 + w % 2])
            v["groups"] = 8 * v["chunks"]

            def keys_at(b, c):
                if v["full"]:
                    return b * (2 * v["chunks"] + 2) + 2 * c
                return 0 if isinstance(b, int) and b == 0 else 4 * b - 2

            def outs_at(b):
                if v["full"]:
                    return b * (2 * v["chunks"] + 2) + 2 * v["chunks"]
                return 4 * b + 2 if isinstance(b, int) and b == B - 1 else 4 * b + 4
            v["keys_at"], v["outs_at"] = keys_at, outs_at
            return v
        O_BANK, SHARED, V_BANK = psum[:, 4], psum[:, 5], psum[:, 6]

        def batches(eng, nkt, norms, keys, tiles, ends):
            if nkt > TAIL_TILES:
                with eng.Fori(0, B) as b:
                    for _ in norms(b):
                        pass
                    for _ in keys(b, 0):
                        pass
                    for j in range(-1, 8):
                        tiles(b, 0, j)
                    for _ in ends(b, 0):
                        pass
                return

            def batch(b, i):
                known = isinstance(b, int)
                k = iter(()) if known and b == B - 1 else keys(b + 1, 1 - i)
                e = iter(()) if known and b == 0 else ends(b - 1, 1 - i)
                n = iter(()) if known and b >= B - 2 else norms(b + 2)
                for j in range(8):
                    def between():
                        next(e, None)
                        next(k, None)
                        if j >= 4:
                            next(n, None)
                    tiles(b, i, j, between)
                assert all(next(x, "none") == "none" for x in (k, e, n))

            for _ in norms(0):
                pass
            for _ in keys(0, 0):
                pass
            for _ in norms(1):
                pass
            tiles(0, 0, -1)
            batch(0, 0)
            with eng.Fori(0, B // 2 - 2) as pair:
                batch(2 * pair + 1, 1)
                batch(2 * pair + 2, 0)
            for b in range(B - 3, B):
                batch(b, b % 2)
            for _ in ends(B - 1, 1):
                pass

        block = ctx.enter_context(nc.Block())

        @block.sync
        def _(sp):
            def stage_block(e):
                i = e
                if i >= STAGED:
                    sp.wait_ge(pool_split, i - STAGED + 1)
                sp.dma_start(stage[:, i % STAGED], entries[e][1]).then_inc(stage_loaded[i % STAGED], 16)

            def across(v, n=P):
                return v.rearrange("(a n) -> a n", a=1).to_broadcast([n, v.shape[0]])

            for t in range(T):
                sp.dma_start(X[:, t], a["x"][2 * t:2 * t + 2].rearrange("b s d -> (b s) d")).then_inc(x_loaded, 16)
            sp.dma_start(gamma_row, across(a["L0_xattn_gamma"])).then_inc(gamma_loaded, 16)
            with nc.allow_non_contiguous_dma(reason="short vectors as columns"):
                for c, src in ((C_CGAMMA, a["L0_xattn_ctx_gamma"]), (C_BQ0, a["L0_attn_bq"]), (C_BK0, a["L0_attn_bk"]),
                               (C_BQ1, a["L1_attn_b_qkv"][0:D]), (C_BK1, a["L1_attn_b_qkv"][D:2 * D]),
                               (C_MUR, a["L0_ffn_mu_r"]), (C_MUK, a["L0_ffn_mu_k"])):
                    sp.dma_start(cols[:, c:c + KC], src.rearrange("(k p) -> p k", p=P)).then_inc(cols_loaded, 16)
                sp.dma_start(cols[:, C_GAIN:C_GAIN + 1], across(a["L1_xattn_gain"])).then_inc(cols_loaded, 16)
                sp.dma_start(cols[:, C_CW:C_CW + 2], across(a["L1_xattn_council_weights"])).then_inc(cols_loaded, 16)
            stage_block(0)
            stage_block(1)
            sp.dma_start(wkv_f, a["L0_xattn_Wkv"].rearrange("(k p) n -> p k n", p=P)).then_inc(wkv_loaded, 16)
            sp.dma_start(mask_i[0:B, 0:SCTX], a["mask_BxS2_ik0"]).then_inc(mask_loaded, 16)
            for e in range(2, before_x):
                stage_block(e)

            fc_rows = a["L1_ffn_W_fc"].rearrange("(b p) n -> b p n", p=P)
            proj_rows = a["L1_ffn_W_proj"].rearrange("d (c n) -> (d c) n", n=D).rearrange("(b p) n -> b p n", p=P)

            def context(nkt):
                v = xmap(nkt)
                def weight_rows(b):
                    x_wait(sp, "g_summed", b)
                    settle(sp)
                    for w, r in enumerate((fc_rows, proj_rows)):
                        sp.dma_start(ybuf[:, w], r[bass.ds(b, 1)].rearrange("b p n -> (b p) n"))\
                            .then_inc(XN["g_loaded"], 16)

                with sp.Fori(0, B) as b:
                    if v["full"]:
                        weight_rows(b)
                    for c, tiles in enumerate(v["tiles_of"]):
                        x_wait(sp, "ctx_turned", b * nkt + tiles[0])
                        settle(sp)
                        if v["full"] and c == 0:
                            x_wait(sp, "pv", b * v["groups"])
                            settle(sp)
                        for kt in tiles:
                            src = a["ctx_1024"][bass.ds(b, 1)].rearrange("b s d -> (b s) d")
                            if kt == FULL_TILES - 1:
                                x_wait(sp, "ctx_zero", b + 1)
                                settle(sp)
                                sp.dma_start(v["ctx"][0:HEAD_ROWS, kt % 4], src[0:HEAD_ROWS]).then_inc(XN["ctx_loaded"], 16)
                            else:
                                r0 = HEAD_ROWS + kt * P if v["full"] else SCTX - TAIL + kt * P
                                sp.dma_start(v["ctx"][:, kt % 4], src[r0:r0 + P]).then_inc(XN["ctx_loaded"], 16)
                    if not v["full"]:
                        weight_rows(b)

            sp.wait_ge(flag_ready, 1)
            sp.wait_ge(*after("ln0"))
            head_rows_used = sp.value_load(flag[0:1, 0:1], min_val=0, max_val=1)
            with sp.If(head_rows_used > 0):
                context(FULL_TILES)
            with sp.If(head_rows_used < 1):
                context(TAIL_TILES)

            def load_bias(n, v_src, o_src):
                if n:
                    sp.wait_ge(layer_done, 2)
                sp.wait_ge(*after("ff", 4))
                for m in range(2):
                    sp.dma_start(bv[64 * m:64 * m + 64], v_src.rearrange("(a j m e) -> a m j e", a=1, j=2, m=2)[:, m]
                                 .to_broadcast([64, 2, P])).then_inc(bias_loaded, 16)
                sp.dma_start(bo, across(o_src)).then_inc(bias_loaded, 16)

            for e in range(before_x, len(entries)):
                if e == W["w0", "o"]:
                    load_bias(0, a["L0_attn_bv"], a["L0_attn_bo"])
                if e == W["win", "Wqj"]:
                    sp.wait_ge(layer_done, 1)
                    for b2 in range(2):
                        src = a["itok_BxS_0_7"].rearrange("(a t c) s -> c a t s", a=1, c=2)[b2]
                        sp.dma_start(ids_rows[64 * b2:64 * b2 + 64], src.to_broadcast([64, T, S])).then_inc(ids_loaded, 16)
                    with nc.allow_non_contiguous_dma(reason="a pointer per token"):
                        sp.dma_start(ptr[:, 0:T], a["itok_BxS_0_4092"].rearrange("(t c) s -> (c s) t", c=2))\
                            .then_inc(ids_loaded, 16)
                if e == W["w1n", "o"]:
                    load_bias(1, a["L1_attn_b_qkv"][2 * D:3 * D], a["L1_attn_b_out"])
                stage_block(e)
            sp.wait_ge(layer_done, 5)
            sp.dma_start(lnw, across(a["L1_ffn_ln_w"])).then_inc(bias_loaded, 16)
            sp.dma_start(lnb, across(a["L1_ffn_ln_b"])).then_inc(bias_loaded, 16)
            last_of = [i for i, x in enumerate(plan["mlp"].letters) if x == "D"]
            for t in range(T):
                Pass(sp, "mlp", t // HT).wait_done(last_of[t % HT])
                sp.dma_start(out[2 * t:2 * t + 2].rearrange("b s d -> (b s) d"), X[:, t]).then_inc(out_stored, 16)
            sp.wait_ge(out_stored, 16 * T)

        @block.gpsimd
        def _(pool):
            for name, semaphore in XN.items():
                if name not in ("ctx_loaded", "g_loaded"):
                    pool.sem_inc(semaphore, 1)
            pool.sem_inc(prod_lo, 1)
            consts = [0]

            def const(ins, wait=False):
                consts[0] += 1
                ins.then_inc(const_ready, 1)
                if wait:
                    pool.wait_ge(const_ready, consts[0])

            const(pool.memset(ident[:], 0.0), wait=True)
            const(pool.affine_select(out=ident[:], in_=ident[:], compare_op=ALU.not_equal, fill=1.0, base=0,
                                     pattern=[[-1, P]], channel_multiplier=1), wait=True)
            const(pool.tensor_copy(identb[:], ident[:]))
            const(pool.memset(ones[:], 1.0))
            const(pool.memset(small[:, 153:154], 0.0))
            const(pool.memset(causal[:], 0.0), wait=True)
            for b2 in range(2):
                part = causal[64 * b2:64 * b2 + 64]
                const(pool.affine_select(out=part, in_=part, compare_op=ALU.is_ge, fill=NEG, base=0,
                                         pattern=[[-1, S]], channel_multiplier=1), wait=True)
                const(pool.iota(tile_base[64 * b2:64 * b2 + 64], pattern=[[2 * SCTX, T]], base=b2 * SCTX,
                                channel_multiplier=0), wait=True)
            const(pool.iota(key_no[:], pattern=[[1, S]], base=0, channel_multiplier=0))
            assert consts[0] == CONSTS

            def split(e):
                src = stage[:, e % STAGED]
                pool.wait_ge(stage_loaded[e % STAGED], 16 * (e // STAGED + 1))
                if entries[e][0] == "n":
                    wait_slot(pool, e)
                    hi, lo = ring_hi[:, e % RING], ring_lo[:, e % RING]
                    pool.tensor_tensor(hi, src, small[:, 153:154].unsqueeze(2).to_broadcast([P, KC, D]), ALU.add)\
                        .then_inc(pool_part, 1)
                    parts[0] += 1
                    pool.wait_ge(pool_part, parts[0])
                    pool.tensor_tensor(lo, src, hi, ALU.subtract).then_inc(pool_split, 1)
                else:
                    t, w = e - W["fc", 0], 0 if e < W["proj", 0] else 1
                    if t == 0:
                        pool.wait_ge(thr_ready, 1)
                    if t % 2 == 0:
                        wait_slot(pool, W["fc", 0] + t // 2)
                    sign = ternary_of(t)
                    pool.wait_ge(pool_split, e)
                    pool.tensor_scalar(sign, src, thr[:, w:w + 1], None, ALU.is_gt).then_inc(pool_part, 1)
                    pool.tensor_scalar(below, src, nthr[:, w:w + 1], None, ALU.is_lt).then_inc(pool_part, 1)
                    parts[0] += 2
                    pool.wait_ge(pool_part, parts[0])
                    pool.tensor_tensor(sign, sign, below, ALU.subtract).then_inc(pool_split, 1)

            parts = [0]
            ctx_rows = a["ctx_1024"].rearrange("b s d -> (b s) d")

            def gather(h):
                for u in range(HT):
                    for w in range(3):
                        idx = row_of.rearrange("p (t w) -> p t w", w=4)[:, 4 * h + u, w:w + 1]
                        pool.indirect_dma_start(win[:, u, w, :], None, ctx_rows,
                                                bass.IndirectOffsetOnAxis(ap=idx.bitcast(mybir.dt.uint32), axis=0))\
                            .then_inc(win_loaded, 16)

            for e in range(len(entries) + 1):
                if e == W["win", "Wvi"] + 1:
                    pool.wait_ge(rows_ready, 1)
                    gather(0)
                if e == W["fc", 0]:
                    pool.wait_ge(comb_ready, 2 * HT)
                    gather(1)
                if e < len(entries):
                    split(e)
            pool.wait_ge(bias_loaded, 16 * 8)
            with pool.Fori(0, 2) as h:
                for u in range(HT):
                    pool.wait_ge(hid_norm, h * HT + u + 1)
                    for n in range(4):
                        cols_ = slice(n * 512, (n + 1) * 512)
                        x = hid[:, u % 2, cols_]
                        pool.tensor_tensor(x, x, lnw[:, cols_], ALU.mult).then_inc(hid_scaled, 1)
                        pool.wait_ge(hid_scaled, (h * HT + u) * 4 + n + 1)
                        pool.tensor_tensor(x, x, lnb[:, cols_], ALU.add).then_inc(hid_ready, 1)

        @block.tensor
        def _(pe):
            pe.wait_ge(const_ready, CONSTS)

            def product(bank, terms):
                passes = []
                for (lh, ll), (rh, rl) in terms:
                    passes.append((lh, rh))
                    if rl is not None:
                        passes.append((lh, rl))
                    if ll is not None:
                        passes.append((ll, rh))
                for n, (l, r) in enumerate(passes):
                    ins = pe.matmul(bank, l, r, start=n == 0, stop=n == len(passes) - 1)
                return ins

            def cut(pair, f):
                return tuple(None if x is None else f(x) for x in pair)

            def turn_tile(bank, tile):
                for k in range(KC):
                    ins = pe.transpose(bank[:, k * P:(k + 1) * P], tile[:, k * P:(k + 1) * P], ident[:])
                return ins

            def turn_y(g, name, i):
                base, n = y_base[name]
                for u in range(HT):
                    bank = g.open()
                    pe.wait_ge(y_ready, base + i * n + u + 1)
                    turn_tile(bank, ybuf[:, u % 2]).then_inc(group_ready, 1)

            def turn_block(g, pair):
                for x in pair:
                    for z in range(2):
                        bank = g.open().bitcast(BF16).rearrange("p (c n) -> p c n", c=2)
                        for c2 in range(2):
                            for c in range(KC):
                                ins = pe.transpose(bank[:, c2, c * P:(c + 1) * P],
                                                   x[:, c, (2 * z + c2) * P:(2 * z + c2 + 1) * P], identb[:])
                        ins.then_inc(group_ready, 1)

            with pe.Fori(0, 2) as h:
                g = Pass(pe, "ln0", h)
                turn_y(g, "ln0", h)
            Pass(pe, "q").all_free()
            for i in range(2):
                if i == 1:
                    pe.wait_ge(flag_part, 1)
                    pe.matmul(SHARED[:, 0:1], ones[0:B, :], small[0:B, 152:153], start=True, stop=True).then_inc(XN["shared_ready"], 1)
                wait_split(pe, ("q", i))
                w = w_of(("q", i))
                with pe.Fori(0, 2) as mp:
                    g = Pass(pe, "q", 2 * i + mp)
                    for mm in range(2):
                        for hf in range(2):
                            bank = g.open()
                            product(bank, [(cut(w, lambda x: x[:, k, bass.ds(mp * 256 + mm * P, P)]),
                                            cut(yT, lambda x: x[:, k, hf * 512:(hf + 1) * 512])) for k in range(KC)])\
                                .then_inc(group_ready, 1)

            Pass(pe, "ff").all_free()

            def attend(nkt):
                v = xmap(nkt)
                W_, ch = v["groups"], v["chunks"]
                cT = (v["cT_hi"], v["cT_lo"])

                def open_shared(n):
                    x_wait(pe, "shared_free", n + 1)
                    return SHARED

                def norms(b):
                    return iter(())

                def keys(b, i):
                    if v["full"]:
                        x_wait(pe, "p_act", b * (W_ // 2))
                        x_wait(pe, "p_dve", b * (W_ // 2))
                    for c, tiles in enumerate(v["tiles_of"]):
                        n = len(tiles)
                        yield
                        for kt in tiles:
                            if kt == tiles[0]:
                                x_wait(pe, "v_copied", b * ch + c)
                            x_wait(pe, "ctx_lo", b * nkt + max(kt - 1, 0))
                            x_wait(pe, "ctx_norm", b * nkt + kt + 1)
                            turn_tile(psum[:, 6 + kt % 2], v["ctx"][:, kt % 4]).then_inc(XN["ctx_turned"], 1)
                            if kt % 2:
                                yield
                        bank = open_shared(v["keys_at"](b, c))
                        settle(pe)
                        pe.matmul(bank[:, 0:n * P], identb[0:B, bass.ds(b, 1)].to_broadcast([B, P]),
                                  maskadd[0:B, v["m0"] + tiles[0] * P:v["m0"] + tiles[0] * P + n * P],
                                  start=True, stop=True).then_inc(XN["shared_ready"], 1)
                        yield
                        x_wait(pe, "ctx_lo", b * nkt + tiles[0] + n)
                        bank = open_shared(v["keys_at"](b, c) + 1)
                        product(bank[:, 0:n * P], [(cut(wk, lambda x: x[:, k, :]), cut(cT, lambda x: x[:, k, 0:n * P]))
                                                   for k in range(KC)]).then_inc(XN["shared_ready"], 1)
                        yield
                        for u in range(n):
                            ins = product(V_BANK[:, u * XD:(u + 1) * XD],
                                          [(cut(cT, lambda x: x[:, k, u * P:(u + 1) * P]), cut(wv, lambda x: x[:, k, :]))
                                           for k in range(KC)])
                        ins.then_inc(XN["v_mm"], 1)

                def scores(b, i, j):
                    if j == 0:
                        x_wait(pe, "shared_free", v["keys_at"](b, ch - 1) + 3)
                    x_wait(pe, "s_max", b * 8 + j if v["full"] else
                           0 if isinstance(b, int) and b == 0 and j == 0 else b * 8 + j - 1)
                    S = v["S"](j)
                    q = Q[:, bass.ds(b, 1), 2 * j:2 * j + 2, :].rearrange("p b h s -> p (b h s)")
                    for tiles in v["tiles_of"]:
                        c0, c1 = tiles[0] * P, (tiles[-1] + 1) * P
                        pe.matmul(S[:, c0:c1], q, v["KA"][i][:, c0:c1], start=True, stop=False)
                        ins = pe.matmul(S[:, c0:c1], q, v["KB"][i][:, c0:c1], start=False, stop=True)
                    ins.then_inc(XN["s_mm"], 1)

                def turn_p(b, j, c):
                    w = j * ch + c
                    if c == 0:
                        x_wait(pe, "exp", b * 8 + j + 1)
                    if w == 0 and v["full"]:
                        x_wait(pe, "v_copied", (b + 1) * ch)
                    x_wait(pe, "p_dve" if w % 2 else "p_act", b * (W_ // 2) + w // 2)
                    bank = v["PTbank"](w)
                    for n, kt in enumerate(v["tiles_of"][c]):
                        ins = pe.transpose(bank[:, n * P:(n + 1) * P],
                                           v["P"][:, j % v["P"].shape[1], kt * P:(kt + 1) * P], ident[:])
                    ins.then_inc(XN["p_turned"], 1)

                def values(b, i, j, c):
                    w = j * ch + c
                    if w == 0:
                        x_wait(pe, "v_copied", (b + 1) * ch)
                        x_wait(pe, "o_norm", b)
                    x_wait(pe, "p_dve" if w % 2 else "p_act", b * (W_ // 2) + w // 2 + 1)
                    for n, kt in enumerate(v["tiles_of"][c]):
                        ins = pe.matmul(O_BANK[:, j * XD:(j + 1) * XD], v["PT"][:, w % 2, n, :], v["V"][i][:, kt, :],
                                        start=kt == 0, stop=kt == nkt - 1)
                    ins.then_inc(XN["pv"], 1)

                before = [None]

                def tiles(b, i, j, between=None):
                    if v["full"]:
                        if j < 7:
                            if j >= 0:
                                for c in range(ch):
                                    turn_p(b, j, c)
                                    if before[0]:
                                        values(*before[0])
                                    before[0] = (b, i, j, c)
                            scores(b, i, j + 1)
                        else:
                            for c in range(ch):
                                turn_p(b, j, c)
                                values(*before[0])
                                before[0] = (b, i, j, c)
                            values(*before[0])
                            before[0] = None
                        return
                    if j < 7:
                        scores(b, i, j + 1)
                    elif not (isinstance(b, int) and b == B - 1):
                        scores(b + 1, 1 - i, 0)
                    if j < 0:
                        return
                    turn_p(b, j, 0)
                    if j > 0:
                        values(b, i, j - 1, 0)
                    elif not (isinstance(b, int) and b == 0):
                        values(b - 1, 1 - i, 7, 0)
                    between()

                def ends(b, i):
                    if not v["full"] and isinstance(b, int) and b == B - 1:
                        values(b, 1, 7, 0)
                    if not v["full"]:
                        yield
                    x_wait(pe, "o_norm", b + 1)
                    for half in range(2):
                        bank = open_shared(v["outs_at"](b) + half)
                        settle(pe)
                        for jj in range(4):
                            ins = pe.transpose(bank[0:XD, jj * P:(jj + 1) * P], v["O"][:, 4 * half + jj, :], ident[:])
                        ins.then_inc(XN["shared_ready"], 1)
                        yield

                batches(pe, nkt, norms, keys, tiles, ends)

            pe.wait_ge(flag_ready, 1)
            head_rows_used = pe.value_load(flag[0:1, 0:1], min_val=0, max_val=1)
            with pe.If(head_rows_used > 0):
                attend(FULL_TILES)
            with pe.If(head_rows_used < 1):
                attend(TAIL_TILES)

            pe.wait_ge(x_attended, 1)
            for i in range(4):
                wait_split(pe, ("ffg", i))
                wa, wg = w_of(("ffa", i)), w_of(("ffg", i))
                with pe.Fori(0, 4) as m:
                    g = Pass(pe, "ff", 4 * i + m)
                    for hf in range(2):
                        for w in (wa, wg):
                            bank = g.open()
                            product(bank, [(cut(w, lambda x: x[:, k, bass.ds(m * P, P)]),
                                            cut(yT, lambda x: x[:, k, hf * 512:(hf + 1) * 512])) for k in range(KC)])\
                                .then_inc(group_ready, 1)
            Pass(pe, "xout").all_free()
            for e in range(6):
                key = ("xo", e) if e < 2 else ("ff2", e - 2)
                wait_split(pe, key)
                if e == 2:
                    pe.wait_ge(prod_lo, 33)
                src, c0 = (oT, 4 * e) if e < 2 else (ffT, 4 * (e - 2))
                with pe.Fori(0, T) as t:
                    bank = psum[:, bass.ds(t, 1), :].rearrange("p a n -> p (a n)")
                    n = 0
                    for k in range(KC):
                        (xh, xl), (wh, wl) = cut(src, lambda x: x[:, c0 + k, bass.ds(t * P, P)]), cut(w_of(key), lambda x: x[:, k, :])
                        for l, r in ((xh, wh), (xh, wl), (xl, wh)):
                            ins = pe.matmul(bank, l, r, start=e == 0 and n == 0, stop=e == 5 and n == 3 * KC - 1)
                            n += 1
                    if e == 5:
                        ins.then_inc(group_ready, 1)
                pe.drain().then_inc(block_used, 1)

            g = Pass(pe, "gamma")
            bank = g.open()
            pe.wait_ge(gamma_part, 1)
            pe.matmul(bank[:, 0:2], ones[:], gtot, start=True, stop=True).then_inc(group_ready, 1)

            def attention(n, name):
                wq, wk_, wv_ = turned if n else (w_of(("w0", x)) for x in "qkv")
                wo = woT if n else w_of(("w0", "o"))
                if not n:
                    wait_split(pe, ("w0", "o"))
                with pe.Fori(0, 2) as h:
                    g = Pass(pe, name, h)
                    turn_y(g, name, h)
                    g.wait_done(3)
                    for w in (wq, wk_):
                        for m in range(KC):
                            bank = g.open()
                            product(bank, [(cut(w, lambda x: x[:, k, m * P:(m + 1) * P]), cut(yh, lambda x: x[:, k, :]))
                                           for k in range(KC)]).then_inc(group_ready, 1)
                    for u in range(HT):
                        bank = g.open()
                        product(bank, [(cut(yh, lambda x: x[:, k, u * P:(u + 1) * P]), cut(wv_, lambda x: x[:, k, :]))
                                       for k in range(KC)]).then_inc(group_ready, 1)

                    def scores(u):
                        for r in range(4):
                            bank = g.open()
                            if u == 0 and r == 0:
                                g.wait_done(11)
                            for m in range(4):
                                for b2 in range(2):
                                    t0 = u * P + b2 * S
                                    f = lambda x: x[32 * r:32 * r + 32, m, t0:t0 + S]
                                    ins = product(bank[64 * b2:64 * b2 + 64, m * S:(m + 1) * S], [(cut(qh, f), cut(kh, f))])
                            ins.then_inc(group_ready, 1)

                    scores(0)
                    for u in range(HT):
                        pe.wait_ge(p_exp, (n * 2 + h) * HT + u + 1)
                        for j in range(2):
                            bank = g.open()
                            for r in range(4):
                                ins = pe.transpose(bank[:, r * P:(r + 1) * P],
                                                   prob[:, u % 2, r, 2 * j:2 * j + 2, :].rearrange("p m s -> p (m s)"), ident[:])
                            ins.then_inc(group_ready, 1)
                        pt = g.at - 1
                        if u + 1 < HT:
                            scores(u + 1)
                        bank = g.open()
                        if u == 0:
                            pe.wait_ge(v_done, (n * 2 + h) * HT + HT)
                        g.wait_done(pt)
                        for j in range(2):
                            for r in range(4):
                                for b2 in range(2):
                                    o = bank.rearrange("p (j m r d) -> p j m r d", j=2, m=2, r=4)[64 * b2:64 * b2 + 64, j, :, r, :]
                                    ins = product(o, [(cut(pT, lambda x: x[:, u % 2, 4 * j + r, b2 * S:(b2 + 1) * S]),
                                                       cut(vb, lambda x: x[:, 2 * u + b2, 4 * j + r]))])
                        ins.then_inc(group_ready, 1)
                        o_group = g.at - 1
                        bank = g.open()
                        g.wait_done(o_group)
                        turn_tile(bank, ybuf[:, u % 2]).then_inc(group_ready, 1)
                    last = g.at - 1
                    for u in range(HT):
                        bank = g.open()
                        if u == 0:
                            g.wait_done(last)
                        product(bank, [(cut(ah, lambda x: x[:, k, u * P:(u + 1) * P]), cut(wo, lambda x: x[:, k, :]))
                                       for k in range(KC)]).then_inc(group_ready, 1)

            attention(0, "attn0")

            g = Pass(pe, "turn_mix")
            for n in "rkv":
                wait_split(pe, ("mixn", n))
                turn_block(g, w_of(("mixn", n)))
            wr, wk2, wv2 = (turned[i] for i in range(3))
            with pe.Fori(0, 2) as h:
                g = Pass(pe, "mix", h)
                turn_y(g, "mix", h)
                for u in range(HT):
                    bank = g.open()
                    if u == 0:
                        pe.wait_ge(mix_lo, 8 * h + 4)
                    product(bank, [(cut(mixT[0], lambda x: x[:, k, u * P:(u + 1) * P]), cut(wr, lambda x: x[:, k, :]))
                                   for k in range(KC)]).then_inc(group_ready, 1)
                pe.wait_ge(mix_lo, 8 * h + 8)
                for m in range(KC):
                    bank = g.open()
                    product(bank, [(cut(wk2, lambda x: x[:, k, m * P:(m + 1) * P]), cut(mixT[1], lambda x: x[:, k, :]))
                                   for k in range(KC)]).then_inc(group_ready, 1)
                for u in range(HT):
                    bank = g.open()
                    if u == 0:
                        pe.wait_ge(relu_lo, 4 * h + 4)
                    product(bank, [(cut(kact, lambda x: x[:, k, u * P:(u + 1) * P]), cut(wv2, lambda x: x[:, k, :]))
                                   for k in range(KC)]).then_inc(group_ready, 1)

            g = Pass(pe, "fold")

            def weights_product(left, right):
                for m in range(KC):
                    bank = g.open()
                    product(bank, [(cut(left, lambda x: x[:, k, m * P:(m + 1) * P]), cut(right, lambda x: x[:, k, :]))
                                   for k in range(KC)]).then_inc(group_ready, 1)

            for s in "ji":
                wait_split(pe, ("win", "Wk" + s))
                weights_product(w_of(("win", "Wq" + s)), w_of(("win", "Wk" + s)))
            wait_split(pe, ("win", "Wout"))
            turn_block(g, w_of(("win", "Wout")))
            g.wait_done(10)
            g.wait_done(11)
            for s in "ji":
                wait_split(pe, ("win", "Wv" + s))
                weights_product(w_of(("win", "Wv" + s)), turned[2])
            with pe.Fori(0, 2) as h:
                g = Pass(pe, "window", h)
                turn_y(g, "window", h)
                for u in range(HT):
                    for s in range(2):
                        bank = g.open()
                        g.wait_done(u)
                        product(bank, [(cut(yh, lambda x: x[:, k, u * P:(u + 1) * P]), cut(fold[s], lambda x: x[:, k, :]))
                                       for k in range(KC)]).then_inc(group_ready, 1)
                for n in range(2 * HT):
                    bank = g.open()
                    pe.wait_ge(comb_ready, h * 2 * HT + n + 1)
                    turn_tile(bank, comb[:, n % 2]).then_inc(group_ready, 1)
                last = g.at - 1
                for u in range(HT):
                    bank = g.open()
                    if u == 0:
                        g.wait_done(last)
                    product(bank, [(cut(src, lambda x: x[:, k, u * P:(u + 1) * P]), cut(fold[2 + s], lambda x: x[:, k, :]))
                                   for s, src in enumerate((yh, y2)) for k in range(KC)]).then_inc(group_ready, 1)

            g = Pass(pe, "turn_w1")
            for n in "qkvo":
                wait_split(pe, ("w1n", n))
                turn_block(g, w_of(("w1n", n)))
            attention(1, "attn1")

            g = Pass(pe, "turn_mlp")
            for t in range(8):
                wait_split(pe, ("fc", t) if t < 4 else ("proj", t - 4))
                turn_block(g, (ternary_of(t),))
            with pe.Fori(0, 2) as h:
                g = Pass(pe, "mlp", h)
                turn_y(g, "mlp", h)

                def hidden(u):
                    for n in range(4):
                        bank = g.open()
                        if u == 0 and n == 0:
                            g.wait_done(3)
                        product(bank, [(cut(yh, lambda x: x[:, k, u * P:(u + 1) * P]), (fcT[:, n, k, :], None))
                                       for k in range(KC)]).then_inc(group_ready, 1)

                hidden(0)
                for u in range(HT):
                    if u + 1 < HT:
                        hidden(u + 1)
                    for n in range(4):
                        bank = g.open()
                        pe.wait_ge(hid_ready, (h * HT + u) * 4 + n + 1)
                        turn_tile(bank, hid[:, u % 2, n * 512:(n + 1) * 512]).then_inc(group_ready, 1)
                    last = g.at - 1
                    bank = g.open()
                    g.wait_done(last)
                    product(bank, [(cut(hT[u % 2], lambda x: x[:, c, :]), (projT[:, c, :], None)) for c in range(FF // P)])\
                        .then_inc(group_ready, 1)

        @block.scalar
        def _(act):
            for _ in range(ACT_CREDIT):
                act.drain().then_inc(act_freed, 1)
            act.wait_ge(const_ready, CONSTS)

            def copy_hi(dst, bank):
                return act.activation(dst, bank, ACT.Copy)

            def quad(bank):
                return bank.rearrange("p (k n) -> p k n", k=KC)

            def hi_of_tile(g, i, dst):
                copy_hi(dst, quad(g.take(i))).then_inc(act_hi, 1)

            def turned_half(g):
                for u in range(HT):
                    hi_of_tile(g, u, yh[0][:, :, u * P:(u + 1) * P])

            def copy_turned(g, i, dst):
                act.activation(dst, g.take(i).bitcast(BF16).rearrange("p (c n) -> p c n", c=2), ACT.Copy).then_inc(act_freed, 1)

            with act.Fori(0, 2) as h:
                g = Pass(act, "ln0", h)
                for u in range(HT):
                    hi_of_tile(g, u, yT[0][:, :, bass.ds(h * 512 + u * P, P)])
            for i in range(2):
                with act.Fori(0, 2) as mp:
                    g = Pass(act, "q", 2 * i + mp)
                    for mm in range(2):
                        for hf in range(2):
                            bank = g.take(2 * mm + hf)
                            for h2 in range(2):
                                dst = Q[0:64, hf * 8:hf * 8 + 8, bass.ds(i * 8 + mp * 4 + mm * 2 + h2, 1), :]
                                ins = act.activation(dst.rearrange("p b h s -> p b (h s)"),
                                                     bank[64 * h2:64 * h2 + 64].rearrange("p (b s) -> p b s", b=8),
                                                     ACT.Copy, scale=XD ** -0.5)
                            ins.then_inc(act_hi, 1)

            def attend(nkt):
                v = xmap(nkt)
                W_, ch = v["groups"], v["chunks"]

                def norms(b):
                    return iter(())

                def keys(b, i):
                    for c, tiles in enumerate(v["tiles_of"]):
                        n = len(tiles)
                        yield
                        if not v["full"]:
                            yield
                        for kt in tiles:
                            x_wait(act, "ctx_turned", b * nkt + kt + 1)
                            u = kt % 4
                            copy_hi(v["cT_hi"][:, :, u * P:(u + 1) * P], quad(psum[:, 6 + kt % 2])).then_inc(XN["ctx_hi"], 1)
                            if kt % 2:
                                yield
                        cols_ = slice(tiles[0] * P, (tiles[-1] + 1) * P)
                        x_wait(act, "shared_ready", v["keys_at"](b, c) + 2)
                        copy_hi(v["mb"][i][:, cols_], SHARED[:, 0:n * P]).then_inc(XN["shared_free"], 1)
                        yield
                        x_wait(act, "shared_ready", v["keys_at"](b, c) + 3)
                        copy_hi(v["KA"][i][:, cols_], SHARED[:, 0:n * P]).then_inc(XN["k_hi"], 1)
                        yield
                        x_wait(act, "v_mm", b * ch + c + 1)
                        copy_hi(v["V"][i][:, tiles[0]:tiles[-1] + 1, :],
                                V_BANK[:, 0:n * XD].rearrange("p (t e) -> p t e", e=XD)).then_inc(XN["v_copied"], 1)
                        if c == 0:
                            yield
                            act.wait_ge(XN["g_loaded"], 32 * (b + 1))
                            for w in range(2):
                                ins = act.activation(ybuf[:, w], ybuf[:, w], ACT.Abs, accum_out=gsum[:, w, bass.ds(b, 1)])
                            ins.then_inc(XN["g_summed"], 1)

                def exp(b, i, j):
                    p = v["P"][:, j % v["P"].shape[1], :]
                    x_wait(act, "s_max", b * 8 + j + 1)
                    act.activation(p, p, ACT.Exp, bias=xq_neg[:, i, j:j + 1], accum_out=xq_sum[:, i, j:j + 1])\
                        .then_inc(XN["exp"], 1)

                def copies(b, j):
                    for c in range(ch):
                        w = j * ch + c
                        if w % 2 == 0:
                            n = len(v["tiles_of"][c])
                            x_wait(act, "p_turned", b * W_ + w + 1)
                            if v["full"]:
                                x_wait(act, "pv", b * W_ + max(w - 1, 0))
                            else:
                                x_wait(act, "pv", 0 if w == 0 and isinstance(b, int) and b == 0 else b * W_ + w - 1)
                            copy_hi(v["PT"][:, 0, 0:n, :], v["PTbank"](w)[:, 0:n * P].rearrange("p (t q) -> p t q", q=P))\
                                .then_inc(XN["p_act"], 1)

                def tiles(b, i, j, between=None):
                    if v["full"] and j >= 0:
                        copies(b, j)
                    if between:
                        between()
                    if j < 7:
                        exp(b, i, j + 1)
                    elif not v["full"] and not (isinstance(b, int) and b == B - 1):
                        exp(b + 1, 1 - i, 0)
                    if not v["full"] and j >= 0:
                        copies(b, j)

                def ends(b, i):
                    if not v["full"]:
                        yield
                        yield
                    for half in range(2):
                        x_wait(act, "shared_ready", v["outs_at"](b) + half + 2)
                        bank = SHARED[0:XD].rearrange("p (j m s) -> p j m s", j=4, m=2)
                        for h2 in range(2):
                            ins = copy_hi(oT[0][64 * h2:64 * h2 + 64, 4 * half:4 * half + 4, bass.ds(b * S, S)], bank[:, :, h2, :])
                        ins.then_inc(XN["ot_hi"], 1)
                        yield

                batches(act, nkt, norms, keys, tiles, ends)

            act.wait_ge(flag_ready, 1)
            head_rows_used = act.value_load(flag[0:1, 0:1], min_val=0, max_val=1)
            with act.If(head_rows_used > 0):
                attend(FULL_TILES)
            with act.If(head_rows_used < 1):
                attend(TAIL_TILES)

            for i in range(4):
                with act.Fori(0, 4) as m:
                    g = Pass(act, "ff", 4 * i + m)
                    for hf in range(2):
                        act.activation(ybuf[:, hf], g.take(2 * hf + 1), ACT.Silu).then_inc(act_freed, 1)
                    for hf in range(2):
                        g.wait_done(2 * hf)
                        act.activation(ffT[0][:, bass.ds(4 * i + m, 1), hf * 512:(hf + 1) * 512].rearrange("p a n -> p (a n)"),
                                       prod[:, hf], ACT.Copy).then_inc(prod_hi, 1)

            def attention(n, name):
                bq, bk = (C_BQ1, C_BK1) if n else (C_BQ0, C_BK0)
                with act.Fori(0, 2) as h:
                    g = Pass(act, name, h)
                    turned_half(g)
                    for x, (dst, bias) in enumerate(((qh, bq), (kh, bk))):
                        for m in range(KC):
                            act.activation(dst[0][:, m, :], g.take(4 + 4 * x + m), ACT.Identity,
                                           bias=cols[:, bias + m:bias + m + 1]).then_inc(act_hi, 1)
                    for u in range(HT):
                        g.wait_done(12 + u)
                        for m in range(2):
                            rows_ = slice(64 * m, 64 * m + 64)
                            ins = act.activation(vb[0][rows_, 2 * u:2 * u + 2, :, m, :],
                                                 vf[rows_, u % 2].rearrange("p (b g e) -> p b g e", b=2, g=8), ACT.Copy)
                        ins.then_inc(v_hi, 1)

                    def exp(u):
                        act.wait_ge(p_max, (n * 2 + h) * HT + u + 1)
                        p = prob[:, u % 2].rearrange("p r m s -> p (r m s)")
                        act.activation(p, p, ACT.Exp).then_inc(p_exp, 1)

                    at = 16 + 4
                    exp(0)
                    for u in range(HT):
                        for j in range(2):
                            hi_of_tile(g, at + j, pT[0][:, u % 2, 4 * j:4 * j + 4, :])
                        if u + 1 < HT:
                            exp(u + 1)
                            at += 4
                        hi_of_tile(g, at + 3, ah[0][:, :, u * P:(u + 1) * P])
                        at += 4

            attention(0, "attn0")

            g = Pass(act, "turn_mix")
            for i, n in enumerate("rkv"):
                for x in range(2):
                    copy_turned(g, 4 * i + 2 * x, turned[i][x][:, 0:2, :])
            act.wait_ge(om_ready, 1)
            with act.Fori(0, 2) as h:
                g = Pass(act, "mix", h)
                for u in range(HT):
                    act.activation(zp[:, :, 2 * u:2 * u + 2, 1:], g.take(u).rearrange("p (k b s) -> p k b s", k=KC, b=2),
                                   ACT.Copy).then_inc(act_freed, 1)
                g.wait_done(HT - 1)

                def previous_part(n):
                    act.activation(mix_t[:, n % 2].rearrange("p (b s) -> p b s", b=8), zp[:, n % 4, :, 0:S], ACT.Copy,
                                   scale=cols[:, (C_OMR, C_OMK)[n // 4] + n % 4:(C_OMR, C_OMK)[n // 4] + n % 4 + 1])\
                        .then_inc(mix_a, 1)

                previous_part(0)
                for n in range(8):
                    if n < 7:
                        previous_part(n + 1)
                    act.wait_ge(mix_b, 8 * h + n + 1)
                    act.activation(mixT[n // 4][0][:, n % 4, :], mix_f[:, n % 2], ACT.Copy).then_inc(mix_hi, 1)
                for u in range(HT):
                    act.activation(recept[:, u], g.take(4 + u), ACT.Sigmoid).then_inc(act_freed, 1)
                for m in range(KC):
                    g.wait_done(8 + m)
                    if m >= 2:
                        act.wait_ge(relu_lo, 4 * h + m - 1)
                    act.activation(relu2[:, m % 2], relu[:, m % 2], ACT.Square).then_inc(relu_sq, 1)
                    act.activation(kact[0][:, m, :], relu[:, m % 2], ACT.Square).then_inc(relu_hi, 1)

            g = Pass(act, "fold")

            def folded(first, pair):
                for m in range(KC):
                    copy_hi(pair[0][:, m, :], g.take(first + m)).then_inc(act_hi, 1)

            folded(0, fold[0])
            folded(4, fold[1])
            for x in range(2):
                copy_turned(g, 8 + 2 * x, turned[2][x][:, 0:2, :])
            folded(12, fold[2])
            folded(16, fold[3])
            act.wait_ge(logit, 1)
            act.activation(council[:, 4:6], council[:, 2:4], ACT.Exp).then_inc(e_ready, 1)
            with act.Fori(0, 2) as h:
                g = Pass(act, "window", h)
                turned_half(g)
                act.wait_ge(logit, h + 2)
                act.activation(sc[:, SC_E:SC_E + 6, :], sc[:, SC_E:SC_E + 6, :], ACT.Exp).then_inc(e_ready, 1)
                act.wait_ge(weights_ready, h + 1)

                def first(n):
                    act.activation(comb[:, n % 2], win[:, n // 2, 0, :], ACT.Copy,
                                   scale=sc[:, SC_E + 3 * (n % 2), n // 2:n // 2 + 1]).then_inc(first_row, 1)

                first(0)
                first(1)
                for n in range(2 * HT):
                    u = n // 2
                    hi_of_tile(g, 12 + n, (yh, y2)[n % 2][0][:, :, u * P:(u + 1) * P])
                    if n + 2 < 2 * HT:
                        first(n + 2)

            g = Pass(act, "turn_w1")
            for i, n in enumerate("qkvo"):
                dst = woT if n == "o" else turned[i]
                for x in range(2):
                    copy_turned(g, 4 * i + 2 * x, dst[x][:, 0:2, :])
            attention(1, "attn1")

            g = Pass(act, "turn_mlp")
            for i in range(4):
                copy_turned(g, 2 * i, fcT[:, i, 0:2, :])
            for i in range(4):
                copy_turned(g, 8 + 2 * i, projT[:, 4 * i:4 * i + 2, :])
            with act.Fori(0, 2) as h:
                g = Pass(act, "mlp", h)
                turned_half(g)
                at = 4

                def gelus(u, at):
                    for n in range(4):
                        act.activation(hid[:, u % 2, n * 512:(n + 1) * 512], g.take(at + n), ACT.Gelu).then_inc(act_freed, 1)

                gelus(0, at)
                at += 4
                for u in range(HT):
                    if u + 1 < HT:
                        gelus(u + 1, at)
                        at += 4
                    for n in range(4):
                        hi_of_tile(g, at + n, hT[u % 2][0][:, 4 * n:4 * n + 4, :])
                    at += 5

        @block.vector
        def _(dve):
            done = {"step": 0}

            def piece(i=0, passes=1, key=None):
                n = LINKS.get(key, 0)
                c = Chain(dve, step, done["step"], i, n if passes > 1 else 0)
                c.passes, c.key = passes, key
                return c

            def close(c):
                if c.passes > 1:
                    assert c.n == LINKS.get(c.key), f"LINKS[{c.key!r}] = {c.n}"
                done["step"] += c.n * c.passes

            def finished(semaphore):
                settle(dve)
                dve.drain().then_inc(semaphore, 1)

            def xt(i, u):
                return X[:, bass.ds(i * HT + u, 1), :].rearrange("p a n -> p (a n)")

            def quad(x):
                return x.rearrange("p (k n) -> p k n", k=KC)

            def rstd(c, n, mv=mv, nw=nw):
                for _ in rstd_in_steps(c, n, mv, nw):
                    pass

            def rstd_in_steps(c, n, mv, nw):
                v, y, t = (nw[:, i, 0:n] for i in range(3))
                c.link(dve.tensor_scalar(v, mv[:, 0:n, 1], LN_EPS, None, ALU.add))
                c.link(dve.tensor_scalar(y.bitcast(I32), v.bitcast(I32), 1, None, ALU.arith_shift_right))
                dve.tensor_scalar(v, v, -0.5, None, ALU.mult)
                c.link(dve.tensor_scalar(y.bitcast(I32), y.bitcast(I32), -1.0, RSQRT_SEED, ALU.mult, ALU.add))
                for i in range(3):
                    c.link(dve.tensor_tensor(t, y, y, ALU.mult))
                    c.link(dve.tensor_tensor(t, t, v, ALU.mult))
                    c.link(dve.scalar_tensor_tensor(out=y, in0=t, scalar=1.5, in1=y, op0=ALU.add, op1=ALU.mult))
                    if i == 0:
                        yield

            def moments(c, tiles):
                for _ in bn_in_steps(c, tiles):
                    pass
                rstd(c, len(tiles))

            def bn_in_steps(c, tiles):
                for u, x in enumerate(tiles):
                    ins = dve.bn_stats(stats[:, u, :], x)
                    if u == 1:
                        yield
                c.link(ins)
                settle(dve)
                for u in range(len(tiles)):
                    ins = dve.bn_aggr(mv[:, u, :], stats[:, u, :])
                c.link(ins)

            def normed(dst, src, u, mv=mv, nw=nw):
                return dve.tensor_scalar(dst, src, mv[:, u, 0:1], nw[:, 1, u:u + 1], ALU.subtract, ALU.mult)

            def lo_of_tile(g, i, dst, hi):
                bank = g.wait_hi(i)
                dve.tensor_tensor(dst, quad(bank), hi, ALU.subtract).then_inc(dve_freed, 1)

            def next_moments(c, i):
                moments(c, [xt(i, u) for u in range(HT)])

            def norm_half(g, i):
                def low(u):
                    sl = slice(u * P, (u + 1) * P)
                    lo_of_tile(g, u, yh[1][:, :, sl], yh[0][:, :, sl])
                for u in range(HT):
                    if u >= 2:
                        g.take(u - 2)
                    normed(ybuf[:, u % 2], xt(i, u), u).then_inc(y_ready, 1)
                    if u >= 1:
                        low(u - 1)
                low(HT - 1)

            def copy_turned(g, i, dst):
                dve.tensor_copy(dst, g.take(i).bitcast(BF16).rearrange("p (c n) -> p c n", c=2)).then_inc(dve_freed, 1)

            for _ in range(DVE_CREDIT):
                dve.drain().then_inc(dve_freed, 1)
            dve.wait_ge(const_ready, CONSTS)
            dve.wait_ge(gamma_loaded, 16)
            with dve.Fori(0, 2) as h:
                c = piece(h, 2, "ln0")
                g = Pass(dve, "ln0", h)
                dve.wait_ge(x_loaded, 16 * HT * (h + 1))
                moments(c, [xt(h, u) for u in range(HT)])
                for u in range(HT):
                    ins = normed(x0[:, u], xt(h, u), u)
                c.link(ins)
                moments(c, [x0[:, u] for u in range(HT)])
                for u in range(HT):
                    ins = normed(x0[:, u], x0[:, u], u)
                c.link(ins)

                def low(u):
                    sl = bass.ds(h * 512 + u * P, P)
                    lo_of_tile(g, u, yT[1][:, :, sl], yT[0][:, :, sl])

                for u in range(HT):
                    if u >= 2:
                        g.take(u - 2)
                    dve.tensor_tensor(ybuf[:, u % 2], x0[:, u], gamma_row, ALU.mult).then_inc(y_ready, 1)
                    if u >= 1:
                        low(u - 1)
                low(HT - 1)
            close(c)

            c = piece()
            dve.wait_ge(mask_loaded, 16)
            head = SCTX - HEAD_ROWS
            c.link(dve.memset(maskadd[0:B, SCTX:KEYS], MASKED))
            c.link(dve.tensor_scalar(maskadd[0:B, 0:head], mask_i[0:B, HEAD_ROWS:SCTX], 0.0, MASKED, ALU.is_equal, ALU.mult))
            c.link(dve.tensor_scalar(maskadd[0:B, head:SCTX], mask_i[0:B, 0:HEAD_ROWS], 0.0, MASKED, ALU.is_equal, ALU.mult))
            c.link(dve.tensor_scalar(mask_f[0:B, 0:SCTX - TAIL], mask_i[0:B, 0:SCTX - TAIL], 0.0, None, ALU.not_equal))
            dve.tensor_reduce(small[0:B, 152:153], mask_f[0:B, 0:SCTX - TAIL], AX.X, ALU.max).then_inc(flag_part, 1)
            dve.wait_ge(wkv_loaded, 16)
            dve.wait_ge(cols_loaded, 16 * 9)
            for k in range(KC):
                ins = dve.tensor_scalar(wkv_f[:, k], wkv_f[:, k], cols[:, C_CGAMMA + k:C_CGAMMA + k + 1], None, ALU.mult)
            c.link(ins)
            for i in range(2):
                ins = dve.tensor_copy(wk[0][:, :, i * XD:(i + 1) * XD], wkv_f[:, :, 0:XD])
            dve.tensor_copy(wv[0], wkv_f[:, :, XD:2 * XD])
            c.link(dve.tensor_scalar(cols[:, C_OMR:C_OMR + 8], cols[:, C_MUR:C_MUR + 8], -1.0, 1.0, ALU.mult, ALU.add))
            for i in range(2):
                sl = slice(i * XD, (i + 1) * XD)
                dve.tensor_tensor(wk[1][:, :, sl], wkv_f[:, :, 0:XD], wk[0][:, :, sl], ALU.subtract)
            c.link(dve.tensor_tensor(wv[1], wkv_f[:, :, XD:2 * XD], wv[0], ALU.subtract))
            close(c)

            for i in range(2):
                if i == 1:
                    x_wait(dve, "shared_ready", 1)
                    dve.tensor_scalar(flag[:], SHARED[:, 0:1], 0.5, None, ALU.is_gt).then_inc(XN["shared_free"], 1)
                    x_wait(dve, "shared_free", 1)
                    finished(flag_ready)
                with dve.Fori(0, 2) as mp:
                    g = Pass(dve, "q", 2 * i + mp)
                    for mm in range(2):
                        for hf in range(2):
                            bank = g.wait_hi(2 * mm + hf)
                            for h2 in range(2):
                                def q_of(rows_):
                                    return Q[rows_, hf * 8:hf * 8 + 8, bass.ds(i * 8 + mp * 4 + mm * 2 + h2, 1), :]\
                                        .rearrange("p b h s -> p b (h s)")
                                ins = dve.scalar_tensor_tensor(
                                    out=q_of(slice(64, 128)), in0=bank[64 * h2:64 * h2 + 64].rearrange("p (b s) -> p b s", b=8),
                                    scalar=XD ** -0.5, in1=q_of(slice(0, 64)), op0=ALU.mult, op1=ALU.subtract)
                            ins.then_inc(dve_freed, 1)


            def attend(nkt):
                v = xmap(nkt)
                W_, ch = v["groups"], v["chunks"]

                def chunk_norms(b, c):
                    tiles = v["tiles_of"][c]
                    n = len(tiles)
                    cm = Chain(dve, norm_step, 0, b * ch + c, 2)
                    if tiles[-1] == FULL_TILES - 1:
                        x_wait(dve, "ctx_turned", b * nkt + tiles[0])
                        dve.memset(v["ctx"][:, tiles[0] % 4], 0.0).then_inc(XN["ctx_zero"], 1)
                    dve.wait_ge(XN["ctx_loaded"], 16 * (b * nkt + tiles[0] + n))
                    yield from bn_in_steps(cm, [v["ctx"][:, kt % 4] for kt in tiles])
                    cm.close()

                def chunk_rstd(b, c):
                    cr = Chain(dve, rstd_step, 0, b * ch + c, LINKS.get("rstd", 0))
                    yield from rstd_in_steps(cr, len(v["tiles_of"][c]), mv, nw)
                    assert cr.n == LINKS.get("rstd"), f"LINKS['rstd'] = {cr.n}"

                def norms(b):
                    if not v["full"]:
                        yield from chunk_norms(b, 0)
                        yield
                        yield from chunk_rstd(b, 0)

                def keys(b, i):
                    for c, tiles in enumerate(v["tiles_of"]):
                        n = len(tiles)
                        if v["full"]:
                            for _ in chunk_norms(b, c):
                                pass
                            for _ in chunk_rstd(b, c):
                                pass
                        for u, kt in enumerate(tiles):
                            normed(v["ctx"][:, kt % 4], v["ctx"][:, kt % 4], u).then_inc(XN["ctx_norm"], 1)
                            if kt % 2:
                                yield
                        for kt in tiles:
                            sl = slice(kt % 4 * P, (kt % 4 + 1) * P)
                            x_wait(dve, "ctx_hi", b * nkt + kt + 1)
                            dve.tensor_tensor(v["cT_lo"][:, :, sl], quad(psum[:, 6 + kt % 2]), v["cT_hi"][:, :, sl],
                                              ALU.subtract).then_inc(XN["ctx_lo"], 1)
                            if kt % 2:
                                yield
                        if not v["full"]:
                            yield
                        sl = slice(tiles[0] * P, (tiles[-1] + 1) * P)
                        x_wait(dve, "k_hi", b * ch + c + 1)
                        dve.tensor_tensor(v["KB"][i][:, sl], SHARED[:, 0:n * P], v["KA"][i][:, sl], ALU.subtract)\
                            .then_inc(XN["shared_free"], 1)

                def maximum(b, i, j):
                    x_wait(dve, "s_mm", b * 8 + j + 1)
                    x_wait(dve, "p_turned", b * W_ + j * ch if v["full"] else
                           0 if isinstance(b, int) and b == 0 and j < 2 else b * 8 + j - 1)
                    settle(dve)
                    dve.tensor_tensor_reduce(v["P"][:, j % v["P"].shape[1], :], v["S"](j), v["mb"][i], 1.0, NEG, ALU.add, ALU.max,
                                             xq_max[:, i, j:j + 1]).then_inc(max_step, 1)
                    dve.wait_ge(max_step, b * 8 + j + 1)
                    dve.tensor_scalar(xq_neg[:, i, j:j + 1], xq_max[:, i, j:j + 1], -1.0, None, ALU.mult).then_inc(XN["s_max"], 1)

                def copies(b, j):
                    for c in range(ch):
                        w = j * ch + c
                        if w % 2:
                            n = len(v["tiles_of"][c])
                            x_wait(dve, "p_turned", b * W_ + w + 1)
                            x_wait(dve, "pv", b * W_ + w - 1)
                            dve.tensor_copy(v["PT"][:, 1, 0:n, :], v["PTbank"](w)[:, 0:n * P].rearrange("p (t q) -> p t q", q=P))\
                                .then_inc(XN["p_dve"], 1)

                def tiles(b, i, j, between=None):
                    if v["full"] and j >= 0:
                        copies(b, j)
                    if j < 7:
                        maximum(b, i, j + 1)
                    elif not v["full"] and not (isinstance(b, int) and b == B - 1):
                        maximum(b + 1, 1 - i, 0)
                    if between:
                        between()
                    if not v["full"] and j >= 0:
                        copies(b, j)

                def ends(b, i):
                    c_ = Chain(dve, end_step, 0, b, LINKS.get("end", 0))
                    x_wait(dve, "exp", (b + 1) * 8)
                    neg, r, ok = xq_neg[:, i], xq_r[:, i], xq_ok[:, i]
                    c_.link(dve.scalar_tensor_tensor(out=ok, in0=neg, scalar=ALL_MASKED, in1=xq_sum[:, i], op0=ALU.is_lt,
                                                     op1=ALU.mult))
                    c_.link(dve.reciprocal(ok, ok))
                    c_.link(dve.scalar_tensor_tensor(out=r, in0=neg, scalar=ALL_MASKED, in1=ok, op0=ALU.is_lt, op1=ALU.mult))
                    x_wait(dve, "pv", (b + 1) * W_)
                    dve.tensor_tensor(v["O"], O_BANK.rearrange("p (j d) -> p j d", j=8), r.unsqueeze(2).to_broadcast([P, 8, XD]),
                                      ALU.mult).then_inc(XN["o_norm"], 1)
                    if not v["full"]:
                        yield
                        yield
                    for half in range(2):
                        x_wait(dve, "ot_hi", 2 * b + half + 1)
                        bank = SHARED[0:XD].rearrange("p (j m s) -> p j m s", j=4, m=2)
                        for h2 in range(2):
                            o = [x[64 * h2:64 * h2 + 64, 4 * half:4 * half + 4, bass.ds(b * S, S)] for x in oT]
                            ins = dve.tensor_tensor(o[1], bank[:, :, h2, :], o[0], ALU.subtract)
                        ins.then_inc(XN["shared_free"], 1)
                        yield
                    assert c_.n == LINKS.get("end"), f"LINKS['end'] = {c_.n}"

                batches(dve, nkt, norms, keys, tiles, ends)

            head_rows_used = dve.value_load(flag[0:1, 0:1], min_val=0, max_val=1)
            with dve.If(head_rows_used > 0):
                attend(FULL_TILES)
            with dve.If(head_rows_used < 1):
                attend(TAIL_TILES)
            finished(x_attended)
            dve.wait_ge(x_attended, 1)

            for i in range(4):
                with dve.Fori(0, 4) as m:
                    g = Pass(dve, "ff", 4 * i + m)
                    dve.wait_ge(prod_lo, 8 * i + 2 * m + 1)
                    for hf in range(2):
                        g.wait_done(2 * hf + 1)
                        dve.tensor_tensor(prod[:, hf], g.take(2 * hf), ybuf[:, hf], ALU.mult).then_inc(dve_freed, 1)
                    for hf in range(2):
                        dve.wait_ge(prod_hi, 8 * i + 2 * m + hf + 1)
                        x = [t[:, bass.ds(4 * i + m, 1), hf * 512:(hf + 1) * 512].rearrange("p a n -> p (a n)") for t in ffT]
                        dve.tensor_tensor(x[1], prod[:, hf], x[0], ALU.subtract).then_inc(prod_lo, 1)
            g = Pass(dve, "xout")
            for t in range(T):
                dve.tensor_tensor(X[:, t], g.take(t), X[:, t], ALU.add).then_inc(dve_freed, 1)
                if t == HT - 1:
                    c = piece()
                    g.wait_done(t)
                    next_moments(c, 0)
                    close(c)
            c = piece()
            c.link(dve.reduce_sum(gtot, gsum, AX.X))
            finished(gamma_part)
            g = Pass(dve, "gamma")
            dve.tensor_scalar(thr, g.take(0)[:, 0:2], 0.5 / (FF * D), 0.5 * ABSMEAN_EPS, ALU.mult, ALU.add).then_inc(dve_freed, 1)
            g.wait_done(0)
            dve.tensor_scalar(nthr, thr, -1.0, None, ALU.mult).then_inc(thr_ready, 1)
            close(c)
            finished(layer_done)
            dve.wait_ge(layer_done, 1)

            def attention(n, name):
                bq, bk = (C_BQ1, C_BK1) if n else (C_BQ0, C_BK0)
                c = piece()
                dve.wait_ge(bias_loaded, 48 * (n + 1))
                c.link(dve.memset(vb_words, 0))
                close(c)
                with dve.Fori(0, 2) as h:
                    c = piece(h, 2, "attention")
                    g = Pass(dve, name, h)
                    norm_half(g, h)
                    for x, (dst, bias) in enumerate(((qh, bq), (kh, bk))):
                        for m in range(KC):
                            bank = g.wait_hi(4 + 4 * x + m)
                            dve.scalar_tensor_tensor(out=dst[1][:, m, :], in0=bank, scalar=cols[:, bias + m:bias + m + 1],
                                                     in1=dst[0][:, m, :], op0=ALU.add, op1=ALU.subtract).then_inc(dve_freed, 1)

                    def v_low(u):
                        dve.wait_ge(v_hi, (n * 2 + h) * HT + u + 1)
                        for m in range(2):
                            r_ = slice(64 * m, 64 * m + 64)
                            ins = dve.tensor_tensor(vb[1][r_, 2 * u:2 * u + 2, :, m, :],
                                                    vf[r_, u % 2].rearrange("p (b g e) -> p b g e", b=2, g=8),
                                                    vb[0][r_, 2 * u:2 * u + 2, :, m, :], ALU.subtract)
                        ins.then_inc(v_done, 1)

                    for u in range(HT):
                        if u >= 2:
                            dve.wait_ge(v_done, (n * 2 + h) * HT + u - 1)
                        bank = g.take(12 + u).rearrange("p (j m e) -> p j m e", j=2, m=2)
                        for b2 in range(2):
                            for m in range(2):
                                ins = dve.tensor_tensor(
                                    vf[64 * m:64 * m + 64, u % 2].rearrange("p (b j e) -> p b j e", b=2, j=2)[:, b2],
                                    bank[64 * b2:64 * b2 + 64, :, m, :], bv[64 * m:64 * m + 64], ALU.add)
                        ins.then_inc(dve_freed, 1)
                        if u >= 1:
                            v_low(u - 1)
                    v_low(HT - 1)

                    def weigh(u, at):
                        pu = prob[:, u % 2]
                        for r in range(4):
                            s = g.take(at + r)[:, 0:4 * S].rearrange("p (m s) -> p m s", m=4)
                            if n:
                                ins = dve.tensor_scalar(pu[:, r], s, AD ** -0.5, None, ALU.mult)
                            else:
                                ins = dve.scalar_tensor_tensor(out=pu[:, r], in0=s, scalar=AD ** -0.5,
                                                               in1=causal[:].unsqueeze(1).to_broadcast([P, 4, S]),
                                                               op0=ALU.mult, op1=ALU.add)
                            ins.then_inc(dve_freed, 1)
                        g.wait_done(at + 3)
                        flat = pu.rearrange("p r m s -> p (r m) s")
                        c.link(dve.tensor_reduce(s_max[:, u % 2], flat, AX.X, ALU.max))
                        dve.tensor_tensor(flat, flat, s_max[:, u % 2].unsqueeze(2).to_broadcast([P, AH, S]), ALU.subtract)\
                            .then_inc(p_max, 1)

                    at = 16
                    weigh(0, at)
                    at += 4
                    for u in range(HT):
                        dve.wait_ge(p_exp, (n * 2 + h) * HT + u + 1)
                        c.link(dve.reduce_sum(s_sum[:, u % 2], prob[:, u % 2].rearrange("p r m s -> p (r m) s"), AX.X))
                        c.link(dve.reciprocal(s_sum[:, u % 2], s_sum[:, u % 2]))
                        for j in range(2):
                            lo_of_tile(g, at + j, pT[1][:, u % 2, 4 * j:4 * j + 4, :], pT[0][:, u % 2, 4 * j:4 * j + 4, :])
                        if u + 1 < HT:
                            weigh(u + 1, at + 2)
                            at += 4
                        dve.tensor_tensor(ybuf[:, u % 2].rearrange("p (m r d) -> p m r d", m=4, r=4),
                                          g.take(at + 2).rearrange("p (m r d) -> p m r d", m=4, r=4),
                                          s_sum[:, u % 2].rearrange("p (r m) -> p m r", r=4).unsqueeze(3).to_broadcast([P, 4, 4, AD]),
                                          ALU.mult).then_inc(dve_freed, 1)
                        sl = slice(u * P, (u + 1) * P)
                        lo_of_tile(g, at + 3, ah[1][:, :, sl], ah[0][:, :, sl])
                        at += 4
                    next_moments(c, 1 - h)
                    for u in range(HT):
                        ins = dve.tensor_tensor(xt(h, u), xt(h, u), bo, ALU.add)
                    c.link(ins)
                    for u in range(HT):
                        dve.tensor_tensor(xt(h, u), g.take(at + u), xt(h, u), ALU.add).then_inc(dve_freed, 1)
                close(c)
                finished(layer_done)

            attention(0, "attn0")

            c = piece()
            g = Pass(dve, "turn_mix")
            for i, n in enumerate("rkv"):
                for x in range(2):
                    copy_turned(g, 4 * i + 2 * x + 1, turned[i][x][:, 2:4, :])
            c.link(dve.memset(zp[:, :, :, 0:1], 0.0))
            finished(om_ready)
            close(c)
            with dve.Fori(0, 2) as h:
                c = piece(h, 2, "mix")
                g = Pass(dve, "mix", h)
                for u in range(HT):
                    if u >= 2:
                        g.take(u - 2)
                    normed(ybuf[:, u % 2], xt(h, u), u).then_inc(y_ready, 1)

                def mixed(n):
                    mu = (C_MUR, C_MUK)[n // 4] + n % 4
                    if n >= 2:
                        dve.wait_ge(mix_lo, 8 * h + n - 1)
                    dve.wait_ge(mix_a, 8 * h + n + 1)
                    dve.scalar_tensor_tensor(out=mix_f[:, n % 2].rearrange("p (b s) -> p b s", b=8),
                                             in0=zp[:, n % 4, :, 1:], scalar=cols[:, mu:mu + 1],
                                             in1=mix_t[:, n % 2].rearrange("p (b s) -> p b s", b=8),
                                             op0=ALU.mult, op1=ALU.add).then_inc(mix_b, 1)

                def mixed_low(n):
                    dve.wait_ge(mix_hi, 8 * h + n + 1)
                    dst = mixT[n // 4]
                    dve.tensor_tensor(dst[1][:, n % 4, :], mix_f[:, n % 2], dst[0][:, n % 4, :], ALU.subtract)\
                        .then_inc(mix_lo, 1)

                mixed(0)
                for n in range(8):
                    if n < 7:
                        mixed(n + 1)
                    mixed_low(n)
                next_moments(c, 1 - h)

                def relu_low(m):
                    dve.wait_ge(relu_hi, 4 * h + m + 1)
                    dve.tensor_tensor(kact[1][:, m, :], relu2[:, m % 2], kact[0][:, m, :], ALU.subtract).then_inc(relu_lo, 1)

                for m in range(KC):
                    dve.tensor_scalar(relu[:, m % 2], g.take(8 + m), 0.0, None, ALU.max).then_inc(dve_freed, 1)
                    if m:
                        relu_low(m - 1)
                relu_low(KC - 1)
                g.wait_done(7)
                for u in range(HT):
                    dve.tensor_tensor(relu[:, u % 2], g.take(12 + u), recept[:, u], ALU.mult).then_inc(dve_freed, 1)
                    g.wait_done(12 + u)
                    c.link(dve.tensor_tensor(xt(h, u), xt(h, u), relu[:, u % 2], ALU.add))
            close(c)
            finished(layer_done)

            c = piece()
            pt = ptr[:, 0:T]
            wptr = ptf[:, 0:4 * T].rearrange("p (w t) -> p w t", t=T)
            dve.wait_ge(ids_loaded, 48)
            for w in range(3):
                c.link(dve.tensor_scalar(wptr[:, w], pt, float(w), 0.0, ALU.add, ALU.max))
                c.link(dve.tensor_scalar(wptr[:, w], wptr[:, w], float(SCTX - 1), None, ALU.min))
                c.link(dve.tensor_tensor(row_of.rearrange("p (t w) -> p w t", w=4)[:, w, 0:T], wptr[:, w], tile_base, ALU.add))
            finished(rows_ready)
            c.link(dve.tensor_scalar(wptr[:, 3], wptr[:, 0], float(S - 1), None, ALU.min))
            for t in range(T):
                c.link(dve.scalar_tensor_tensor(out=id_hit[:, 0:S], in0=key_no[:], scalar=wptr[:, 3, t:t + 1], in1=ids_rows[:, t],
                                                op0=ALU.is_equal, op1=ALU.mult, accum_out=rel_id[:, t:t + 1]))
            cw = cols[:, C_CW:C_CW + 2]
            c.link(dve.tensor_reduce(council[:, 0:1], cw, AX.X, ALU.max))
            c.link(dve.tensor_scalar(council[:, 2:4], cw, council[:, 0:1], None, ALU.subtract))
            finished(logit)
            g = Pass(dve, "fold")

            def folded(first, pair):
                for m in range(KC):
                    bank = g.wait_hi(first + m)
                    dve.tensor_tensor(pair[1][:, m, :], bank, pair[0][:, m, :], ALU.subtract).then_inc(dve_freed, 1)

            folded(0, fold[0])
            folded(4, fold[1])
            for x in range(2):
                copy_turned(g, 8 + 2 * x + 1, turned[2][x][:, 2:4, :])
            folded(12, fold[2])
            folded(16, fold[3])
            dve.wait_ge(e_ready, 1)
            c.link(dve.reduce_sum(council[:, 0:1], council[:, 4:6], AX.X))
            c.link(dve.reciprocal(council[:, 1:2], council[:, 0:1]))
            c.link(dve.tensor_scalar(council[:, 6:8], council[:, 4:6], council[:, 1:2], None, ALU.mult))
            close(c)
            with dve.Fori(0, 2) as h:
                c = piece(h, 2, "window")
                g = Pass(dve, "window", h)
                norm_half(g, h)
                next_moments(c, 1 - h)
                dve.wait_ge(win_loaded, 16 * 3 * HT * (h + 1))
                for u in range(HT):
                    for s in range(2):
                        bank = g.take(4 + 2 * u + s)
                        for w in range(3):
                            ins = dve.tensor_tensor_reduce(junk[:, w] if w < 2 else comb[:, 0], bank, win[:, u, w, :], D ** -0.5,
                                                           0.0, ALU.mult, ALU.add, sc[:, 3 * s + w, u:u + 1])
                        ins.then_inc(dve_freed, 1)
                        g.wait_done(4 + 2 * u + s)
                col = lambda i: sc[:, i, :]
                rel, v1, v2 = col(0), col(1), col(2)
                ids = rel_id[:, bass.ds(h * HT, HT)]

                def tt(o, x, y, op):
                    return dve.tensor_tensor(col(o), x, y, op)

                def ts(o, x, s1, s2, op0, op1=None):
                    return dve.tensor_scalar(col(o), x, s1, s2, op0, *([op1] if op1 is not None else []))

                def picked(o, e, op):
                    return dve.scalar_tensor_tensor(out=col(o), in0=ids, scalar=float(e), in1=col(o), op0=op, op1=ALU.mult)

                tt(8, v1, v2, ALU.add)
                tt(9, v1, v2, ALU.max)
                ts(10, v1, -1.0, None, ALU.mult)
                tt(12, v1, v2, ALU.subtract)
                c.link(ts(16, ids, 0.0, None, ALU.is_ge))
                tt(11, col(10), v2, ALU.max)
                ts(13, col(12), -1.0, None, ALU.mult)
                c.link(picked(16, 4, ALU.is_le))
                tt(12, col(12), col(13), ALU.max)
                c.link(ts(17, col(16), -1.0, 1.0, ALU.mult, ALU.add))
                for e in range(5):
                    picked(8 + e, e, ALU.is_equal)
                c.link(tt(17, col(17), rel, ALU.mult))
                tt(8, col(8), col(9), ALU.add)
                c.link(tt(10, col(10), col(11), ALU.add))
                c.link(tt(8, col(8), col(10), ALU.add))
                c.link(tt(8, col(8), col(12), ALU.add))
                c.link(tt(8, col(8), col(16), ALU.mult))
                c.link(tt(0, col(8), col(17), ALU.add))
                for s in range(2):
                    ins = tt(18 + s, col(3 * s), col(3 * s + 1), ALU.max)
                c.link(ins)
                for s in range(2):
                    ins = tt(18 + s, col(18 + s), col(3 * s + 2), ALU.max)
                c.link(ins)
                for s in range(2):
                    for w in range(3):
                        ins = tt(SC_E + 3 * s + w, col(3 * s + w), col(18 + s), ALU.subtract)
                ins.then_inc(logit, 1)
                dve.wait_ge(e_ready, h + 2)
                for s in range(2):
                    ins = tt(18 + s, col(SC_E + 3 * s), col(SC_E + 3 * s + 1), ALU.add)
                c.link(ins)
                for s in range(2):
                    ins = tt(18 + s, col(18 + s), col(SC_E + 3 * s + 2), ALU.add)
                c.link(ins)
                for s in range(2):
                    ins = dve.reciprocal(col(26 + s), col(18 + s))
                c.link(ins)
                for s in range(2):
                    ins = ts(26 + s, col(26 + s), council[:, 6 + s:7 + s], None, ALU.mult)
                c.link(ins)
                for s in range(2):
                    for w in range(3):
                        ins = tt(SC_E + 3 * s + w, col(SC_E + 3 * s + w), col(26 + s), ALU.mult)
                ins.then_inc(weights_ready, 1)

                def low(n):
                    sl = slice(n // 2 * P, (n // 2 + 1) * P)
                    pair = (yh, y2)[n % 2]
                    lo_of_tile(g, 12 + n, pair[1][:, :, sl], pair[0][:, :, sl])

                for n in range(2 * HT):
                    u, s = n // 2, n % 2
                    x = comb[:, s]
                    wt = [sc[:, SC_E + 3 * s + w, u:u + 1] for w in range(3)]
                    dve.wait_ge(first_row, 2 * HT * h + n + 1)
                    c.link(dve.scalar_tensor_tensor(out=x, in0=win[:, u, 1, :], scalar=wt[1], in1=x, op0=ALU.mult, op1=ALU.add))
                    dve.scalar_tensor_tensor(out=x, in0=win[:, u, 2, :], scalar=wt[2], in1=x, op0=ALU.mult, op1=ALU.add)\
                        .then_inc(comb_ready, 1)
                    if n:
                        low(n - 1)
                low(2 * HT - 1)
                for u in range(HT):
                    dve.scalar_tensor_tensor(out=xt(h, u), in0=g.take(20 + u), scalar=cols[:, C_GAIN:C_GAIN + 1], in1=xt(h, u),
                                             op0=ALU.mult, op1=ALU.add).then_inc(dve_freed, 1)
                g.wait_done(23)
            close(c)
            finished(layer_done)

            g = Pass(dve, "turn_w1")
            for i, n in enumerate("qkvo"):
                dst = woT if n == "o" else turned[i]
                for x in range(2):
                    copy_turned(g, 4 * i + 2 * x + 1, dst[x][:, 2:4, :])
            attention(1, "attn1")

            g = Pass(dve, "turn_mlp")
            for i in range(4):
                copy_turned(g, 2 * i + 1, fcT[:, i, 2:4, :])
            for i in range(4):
                copy_turned(g, 8 + 2 * i + 1, projT[:, 4 * i + 2:4 * i + 4, :])
            with dve.Fori(0, 2) as h:
                c = piece(h, 2, "mlp")
                g = Pass(dve, "mlp", h)
                norm_half(g, h)
                next_moments(c, 1 - h)
                at = 4

                def norm_hidden(u, last):
                    g.wait_done(last)
                    x = hid[:, u % 2]
                    for n in range(4):
                        ins = dve.bn_stats(stats[:, n, :], x[:, n * 512:(n + 1) * 512])
                    c.link(ins)
                    settle(dve)
                    c.link(dve.bn_aggr(mv_hid[:, 0, :], stats[:].rearrange("p n k -> p (n k)")))
                    rstd(c, 1, mv_hid, nw_hid)
                    normed(x, x, 0, mv_hid, nw_hid).then_inc(hid_norm, 1)

                norm_hidden(0, 7)
                at = 8
                for u in range(HT):
                    if u + 1 < HT:
                        at += 4
                    for n in range(4):
                        lo_of_tile(g, at + n, hT[u % 2][1][:, 4 * n:4 * n + 4, :], hT[u % 2][0][:, 4 * n:4 * n + 4, :])
                    if u + 1 < HT:
                        norm_hidden(u + 1, at - 1)
                    dve.tensor_tensor(xt(h, u), g.take(at + 4), xt(h, u), ALU.add).then_inc(dve_freed, 1)
                    at += 5
            close(c)
            finished(layer_done)


def kernel(**inputs):
    import numpy as _np
    import concourse.bacc as _bacc
    from concourse import mybir as _mybir
    from concourse.bass_utils import run_bass_kernel_spmd as _run

    nc = _bacc.Bacc("TRN2", target_bir_lowering=False, num_devices=1)
    arrays, args = {}, {}
    for name in inputs:
        arr = _np.ascontiguousarray(inputs[name])
        if arr.ndim == 0 or name == "L1_xattn_gain":
            arr = arr.reshape(1)
        arrays[f"in_{name}_dram"] = arr
        args[name] = nc.dram_tensor(f"in_{name}_dram", arr.shape, _mybir.dt.from_np(arr.dtype), kind="ExternalInput").ap()
    out = nc.dram_tensor("out_0_dram", (B, S, D), F32, kind="ExternalOutput").ap()
    build(nc, args, out)
    r = _run(nc, [arrays], core_ids=[0])
    return r.results[0]["out_0_dram"]
```
